# Optimizing a Trainium2 kernel written in Bass

```python
import numpy as np
import jax
import jax.numpy as jnp

def _softmax(x, axis=-1):
    return jax.nn.softmax(x, axis=axis)

def _gelu(x):
    return jax.nn.gelu(x, approximate=True)

def _silu(x):
    return jax.nn.silu(x)

def _sigmoid(x):
    return jax.nn.sigmoid(x)

def _layernorm(x, axis=-1, eps=1e-05):
    m = jnp.mean(x, axis=axis, keepdims=True)
    v = jnp.var(x, axis=axis, keepdims=True)
    return (x - m) / jnp.sqrt(v + eps)

def _scatter_add(tgt, idx, src, axis=0):
    return tgt.at[idx].add(src)

def _segment_sum(src, seg, n):
    return jax.ops.segment_sum(src, seg, n)
kernel_name = 'mk_prb_d1_jaxref_r4_87b623'

def setup_inputs(seed: int=0):
    np.random.seed(seed)
    _w = jnp.asarray

    def _L0_attn_setup():
        import jax, jax.numpy as jnp
        import numpy as np
        D_MODEL = 256
        N_HEADS = 16
        D_K = D_MODEL // N_HEADS
        SEQ = 1024
        BATCH = 2
        LOCAL_WINDOW = 128
        SCALE = 1.0 / float(np.sqrt(D_K))
        INIT = 1.0 / float(np.sqrt(D_MODEL))

        def _local_mask(seq_len: int) -> jnp.ndarray:
            i = jnp.arange(seq_len)[:, None]
            j = jnp.arange(seq_len)[None, :]
            return (j <= i) & (j >= i - LOCAL_WINDOW)
        key = jax.random.key(seed)
        ks = jax.random.split(key, 9)
        mk = lambda k: jax.random.normal(k, (D_MODEL, D_MODEL), dtype=jnp.float32) * INIT
        return {'x': jax.random.normal(ks[0], (BATCH, SEQ, D_MODEL), dtype=jnp.float32), 'Wq': mk(ks[1]), 'bq': jnp.zeros((D_MODEL,), jnp.float32), 'Wk': mk(ks[2]), 'bk': jnp.zeros((D_MODEL,), jnp.float32), 'Wv': mk(ks[3]), 'bv': jnp.zeros((D_MODEL,), jnp.float32), 'Wo': mk(ks[4]), 'bo': jnp.zeros((D_MODEL,), jnp.float32)}
    _L0_attn_in = _L0_attn_setup()

    def _L0_ffn_setup():
        import jax, jax.numpy as jnp
        import numpy as np
        E = 8
        H = 256
        M = 512
        K = 2
        SE = 1
        BSZ, SEQ = (2, 256)
        W_SCALE = 0.02
        key = jax.random.key(seed)
        ks = jax.random.split(key, 9)
        return {'x': jax.random.normal(ks[0], (BSZ, SEQ, H), jnp.float32), 'gate_w': jax.random.normal(ks[1], (E, H), jnp.float32) * W_SCALE, 'beta': jnp.zeros((E,), jnp.float32), 'gate_proj_w': jax.random.normal(ks[2], (E, H, M), jnp.float32) * W_SCALE, 'up_proj_w': jax.random.normal(ks[3], (E, H, M), jnp.float32) * W_SCALE, 'down_proj_w': jax.random.normal(ks[4], (E, M, H), jnp.float32) * W_SCALE, 'shared_gate_w': jax.random.normal(ks[5], (SE, H, M), jnp.float32) * W_SCALE, 'shared_up_w': jax.random.normal(ks[6], (SE, H, M), jnp.float32) * W_SCALE, 'shared_down_w': jax.random.normal(ks[7], (SE, M, H), jnp.float32) * W_SCALE}
    _L0_ffn_in = _L0_ffn_setup()
    _d = {'L0_attn_x': _L0_attn_in['x'], 'L0_attn_Wq': _L0_attn_in['Wq'], 'L0_attn_bq': _L0_attn_in['bq'], 'L0_attn_Wk': _L0_attn_in['Wk'], 'L0_attn_bk': _L0_attn_in['bk'], 'L0_attn_Wv': _L0_attn_in['Wv'], 'L0_attn_bv': _L0_attn_in['bv'], 'L0_attn_Wo': _L0_attn_in['Wo'], 'L0_attn_bo': _L0_attn_in['bo'], 'L0_ffn_gate_w': _L0_ffn_in['gate_w'], 'L0_ffn_beta': _L0_ffn_in['beta'], 'L0_ffn_gate_proj_w': _L0_ffn_in['gate_proj_w'], 'L0_ffn_up_proj_w': _L0_ffn_in['up_proj_w'], 'L0_ffn_down_proj_w': _L0_ffn_in['down_proj_w'], 'L0_ffn_shared_gate_w': _L0_ffn_in['shared_gate_w'], 'L0_ffn_shared_up_w': _L0_ffn_in['shared_up_w'], 'L0_ffn_shared_down_w': _L0_ffn_in['shared_down_w']}
    _x0 = _d['L0_attn_x']
    _d['L0_attn_x'] = jax.random.normal(jax.random.fold_in(jax.random.key(seed), 1), (16, 512, 256), dtype=_x0.dtype)
    del _x0
    return _d

def reference(L0_attn_x, L0_attn_Wq, L0_attn_bq, L0_attn_Wk, L0_attn_bk, L0_attn_Wv, L0_attn_bv, L0_attn_Wo, L0_attn_bo, L0_ffn_gate_w, L0_ffn_beta, L0_ffn_gate_proj_w, L0_ffn_up_proj_w, L0_ffn_down_proj_w, L0_ffn_shared_gate_w, L0_ffn_shared_up_w, L0_ffn_shared_down_w):

    def _L0_attn_ref(x, Wq, bq, Wk, bk, Wv, bv, Wo, bo):
        import jax, jax.numpy as jnp
        import numpy as np
        D_MODEL = 256
        N_HEADS = 16
        D_K = D_MODEL // N_HEADS
        SEQ = 1024
        BATCH = 2
        LOCAL_WINDOW = 128
        SCALE = 1.0 / float(np.sqrt(D_K))
        INIT = 1.0 / float(np.sqrt(D_MODEL))

        def _local_mask(seq_len: int) -> jnp.ndarray:
            i = jnp.arange(seq_len)[:, None]
            j = jnp.arange(seq_len)[None, :]
            return (j <= i) & (j >= i - LOCAL_WINDOW)
        B, S, _ = x.shape
        q = (x @ Wq.T + bq).reshape(B, S, N_HEADS, D_K)
        k = (x @ Wk.T + bk).reshape(B, S, N_HEADS, D_K)
        v = (x @ Wv.T + bv).reshape(B, S, N_HEADS, D_K)
        scores = jnp.einsum('bqhd,bkhd->bhqk', q, k) * SCALE
        mask = _local_mask(S)[None, None]
        scores = jnp.where(mask, scores, jnp.float32(-10000.0))
        attn = jax.nn.softmax(scores, axis=-1) + jnp.float32(1e-09)
        ctx = jnp.einsum('bhqk,bkhd->bqhd', attn, v).reshape(B, S, D_MODEL)
        return ctx @ Wo.T + bo

    def _L0_ffn_ref(x, gate_w, beta, gate_proj_w, up_proj_w, down_proj_w, shared_gate_w, shared_up_w, shared_down_w):
        import jax, jax.numpy as jnp
        import numpy as np
        E = 8
        H = 256
        M = 512
        K = 2
        SE = 1
        BSZ, SEQ = (2, 256)
        W_SCALE = 0.02
        B0, S0, H0 = x.shape
        xt = x.reshape(-1, H0)
        B = xt.shape[0]
        logits = xt @ gate_w.T
        _, idx = jax.lax.top_k(logits + beta, K)
        probs = jax.nn.sigmoid(jnp.take_along_axis(logits, idx, axis=-1))
        c = jnp.zeros((B, E), xt.dtype).at[jnp.arange(B)[:, None], idx].add(probs)
        g = jnp.einsum('bh,ehm->bem', xt, gate_proj_w)
        u = jnp.einsum('bh,ehm->bem', xt, up_proj_w)
        h = jax.nn.silu(g) * u
        eo = jnp.einsum('bem,emh->beh', h, down_proj_w)
        combined = jnp.einsum('beh,be->bh', eo, c)
        sg = jnp.einsum('bh,ehm->bem', xt, shared_gate_w)
        su = jnp.einsum('bh,ehm->bem', xt, shared_up_w)
        sh = jax.nn.silu(sg) * su
        shared_out = jnp.einsum('bem,emh->beh', sh, shared_down_w).sum(axis=1)
        return (combined + shared_out).reshape(B0, S0, H0)
    x = L0_attn_x
    xn = _layernorm(x, axis=-1)
    x = x + _L0_attn_ref(xn, L0_attn_Wq, L0_attn_bq, L0_attn_Wk, L0_attn_bk, L0_attn_Wv, L0_attn_bv, L0_attn_Wo, L0_attn_bo) + _L0_ffn_ref(xn, L0_ffn_gate_w, L0_ffn_beta, L0_ffn_gate_proj_w, L0_ffn_up_proj_w, L0_ffn_down_proj_w, L0_ffn_shared_gate_w, L0_ffn_shared_up_w, L0_ffn_shared_down_w)
    return x

_drawn_inputs = setup_inputs


def setup_inputs(seed=0):
    import zlib

    import numpy as np

    out = dict(_drawn_inputs(seed))
    spreads = {'L0_attn_bq': (0.0, 0.507),
     'L0_attn_bk': (0.0, 2.0),
     'L0_attn_bv': (0.0, 0.1),
     'L0_attn_bo': (0.0, 0.1),
     'L0_ffn_beta': (0.0, 0.654)}
    factors = {'L0_ffn_gate_w': 3.443,
     'L0_ffn_gate_proj_w': 2.948,
     'L0_ffn_up_proj_w': 2.922,
     'L0_ffn_down_proj_w': 2.916,
     'L0_ffn_shared_gate_w': 2.991,
     'L0_ffn_shared_up_w': 2.944,
     'L0_ffn_shared_down_w': 2.956}
    for name, (base, spread) in spreads.items():
        noise = np.random.default_rng([zlib.crc32(name.encode()), seed]).standard_normal(out[name].shape)
        drawn = base * np.exp(spread * noise) if base else spread * noise
        out[name] = jnp.asarray(drawn.astype(out[name].dtype))
    for name, factor in factors.items():
        out[name] = (out[name] * factor).astype(out[name].dtype)
    return out
```

```python
from contextlib import ExitStack

import concourse.bass as bass
from concourse import mybir

F32 = mybir.dt.float32
F32R = mybir.dt.float32r
BF16 = mybir.dt.bfloat16
U32 = mybir.dt.uint32
I32 = mybir.dt.int32
ALU = mybir.AluOpType
ACT = mybir.ActivationFunctionType
AX = mybir.AxisListType
ds = bass.ds

P = 128
PLAIN_WORDS = 12800
SPLIT_WORDS = 33792
EPS = 1e-5
ATTN_EPS = 1e-9
MASKED = -10000.0


def moe_attention_layer(nc, x, wq_t, wk_t, wv_t, wo_t, bq, bk, bv, bo, gate_t, beta,
                        gate_w, up_w, down_w, sh_gate, sh_up, sh_down, out):
    B, S, D = x.shape
    E = gate_w.shape[0]
    M = gate_w.shape[2]
    KD = D // P
    MC = M // P
    T = S // P
    NT = B * T
    H = 16
    DH = D // H
    SCALE = 1.0 / float(DH) ** 0.5
    HG = 4
    G = H // HG
    BLK = S
    NBLK = (2 * B * S + E * (BLK - 1)) // BLK
    NBLK += NBLK % 2
    ROWS = NBLK * BLK
    TE = NT * E

    xf = x.rearrange("b s d -> (b s) d")
    of = out.rearrange("b s d -> (b s) d")
    xn_d = nc.dram_tensor("xn_d", (B * S, D), F32).ap()
    sorted_d = nc.dram_tensor("sorted_d", (ROWS + BLK, D), F32).ap()
    y_d = nc.dram_tensor("y_d", (ROWS, D), F32).ap()
    q_d = nc.dram_tensor("q_d", (B, 2, D, S), F32).ap()
    k_d = nc.dram_tensor("k_d", (B, 2, D, S), F32).ap()
    v_d = nc.dram_tensor("v_d", (B, P, T, 2 * D), F32).ap()

    ctx = ExitStack()
    with ctx:
        def sb(name, shape, dt):
            return ctx.enter_context(nc.sbuf_tensor(name, shape, dt))

        def sem(name):
            return ctx.enter_context(nc.semaphore(name))

        psum = ctx.enter_context(nc.psum_tensor("psum", [P, 8, 512], F32))

        plain_arena = sb("plain_arena", [P, PLAIN_WORDS], F32)
        split_arena = sb("split_arena", [P, SPLIT_WORDS], F32R)

        def layout(arena, words):
            at = [0]

            def take(*shape):
                n = 1
                for m in shape:
                    n *= m
                assert at[0] + n <= words, (at[0] + n, words)
                view = arena[:, at[0]:at[0] + n]
                at[0] += n
                names = "abcde"[:len(shape)]
                sizes = {c: m for c, m in zip(names, shape)}
                return view.rearrange(f"p ({' '.join(names)}) -> p {' '.join(names)}", **sizes)
            return take

        split_take = layout(split_arena, SPLIT_WORDS)
        ident = sb("ident", [P, P], F32)
        before = sb("before", [P, P], BF16)
        ones = sb("ones", [P, P], BF16)
        tiny = sb("tiny", [P, 1], F32)
        mask = sb("mask", [P, 2 * P], F32)
        wo = split_take(2, G, D)
        gate_sb = sb("gate_sb", [P, KD, E], F32)
        beta_sb = sb("beta_sb", [P, E], F32)
        bqk = sb("bqk", [P, 2, KD], F32)
        bv_sb = sb("bv_sb", [P, D], F32)
        bo_sb = sb("bo_sb", [P, D], F32)
        logits = sb("logits", [P, NT, E], F32)
        slot = sb("slot", [P, NT, 2], U32)
        coef = sb("coef", [P, NT, 2], F32)
        owner = sb("owner", [P, NBLK + 1], I32)
        vtot = sb("vtot", [P, B, G], F32)

        s_w = sem("weights_loaded")
        s_const = sem("constants_ready")
        s_bar = sem("phase_barrier")

        block = ctx.enter_context(nc.Block())
        s_passed = sem("waits_passed")

        def hold(eng, semaphore, value):
            eng.wait_ge(semaphore, value)
            eng.sem_inc(s_passed, 1)

        def wall(eng, n):
            eng.drain().then_inc(s_bar, 1)
            eng.wait_ge(s_bar, 5 * n)

        PASSES = ((0, 0), (0, 1), (1, 0))

        def split_products(pe, out, chunks):
            for c, (lhs_t, rhs) in enumerate(chunks):
                for k, (p, q) in enumerate(PASSES):
                    last = pe.matmul(out, lhs_t(p), rhs(q), start=(c == 0 and k == 0),
                                     stop=(c == len(chunks) - 1 and k == 2))
            return last

        plain_take = layout(plain_arena, PLAIN_WORDS)
        wraw = plain_take(3, 1024)
        wqkv = split_take(2, 3, KD, D)
        zero = split_take(2048)
        s_whi = sem("weights_hi")

        def start_sync(sp):
            sp.dma_start(gate_sb[:, :, :], gate_t.rearrange("(k p) e -> p k e", p=P)).then_inc(s_w, 16)
            sp.dma_start(beta_sb[:, :], beta.partition_broadcast(P)).then_inc(s_w, 16)
            for n, b in enumerate((bq, bk)):
                sp.dma_start(bqk[:, n, :], b.rearrange("(k p) -> p k", p=P),
                             allow_slow_non_contiguous=True).then_inc(s_w, 16)
            sp.dma_start(bv_sb[:, :], bv.partition_broadcast(P)).then_inc(s_w, 16)
            sp.dma_start(bo_sb[:, :], bo.partition_broadcast(P)).then_inc(s_w, 16)
            for n, w in enumerate((wq_t, wk_t, wv_t)):
                sp.dma_start(wraw[:, n, 0:KD * D].rearrange("p (k n) -> p k n", k=KD),
                             w.rearrange("(k p) n -> p k n", p=P)).then_inc(s_w, 16)
            for g in range(G):
                for r in range(HG):
                    for half in range(2):
                        row = (g * HG + r) * DH
                        sp.dma_start(wraw[32 * r + 16 * half:32 * r + 16 * half + 16, g % 3,
                                          512 + (g // 3) * D:512 + (g // 3 + 1) * D],
                                     wo_t[row:row + DH, :]).then_inc(s_w, 16)

        N_W = 16 * (6 + 3 + 2 * H)

        def wo_raw(g):
            return wraw[:, g % 3, 512 + (g // 3) * D:512 + (g // 3 + 1) * D]

        def start_scalar(act):
            act.wait_ge(s_w, N_W)
            for n in range(3):
                act.copy(wqkv[:, 0, n, :, :].rearrange("p k n -> p (k n)"),
                         wraw[:, n, 0:KD * D]).then_inc(s_whi, 1)
            for g in range(G):
                act.copy(wo[:, 0, g, :], wo_raw(g)).then_inc(s_whi, 1)

        def start_vector(dve):
            dve.wait_ge(s_w, N_W)
            for n in range(3):
                dve.wait_ge(s_whi, n + 1)
                dve.tensor_tensor(wqkv[:, 1, n, :, :].rearrange("p k n -> p (k n)"),
                                  wraw[:, n, 0:KD * D],
                                  wqkv[:, 0, n, :, :].rearrange("p k n -> p (k n)").bitcast(F32),
                                  ALU.subtract)
            for g in range(G):
                dve.wait_ge(s_whi, 3 + g + 1)
                dve.tensor_tensor(wo[:, 1, g, :], wo_raw(g), wo[:, 0, g, :].bitcast(F32), ALU.subtract)

        s_pz = sem("pool_zeroed")
        s_zero = sem("sorted_rows_zeroed")
        ZCH = P * 2048 // D
        lower = sb("lower", [P, E * E], F32)

        N_ZERO = 16 * -(-(ROWS + BLK) // (P * 2048 // D))

        def start_gpsimd(pool):
            pool.memset(eps[:, :], EPS).then_inc(s_const, 1)
            pool.memset(zero.bitcast(F32), 0.0).then_inc(s_pz, 1)
            pool.memset(ident[:, :], 0.0).then_inc(s_pz, 1)
            pool.memset(before[:, :], 1.0).then_inc(s_pz, 1)
            pool.memset(mask[:, :], 0.0).then_inc(s_pz, 1)
            pool.memset(lower[:, :], 1.0).then_inc(s_pz, 1)
            pool.memset(ones[:, :], 1.0).then_inc(s_const, 1)
            pool.memset(tiny[:, :], ATTN_EPS).then_inc(s_const, 1)
            pool.wait_ge(s_pz, 5)
            for r in range(0, ROWS + BLK, ZCH):
                n = min(ZCH, ROWS + BLK - r)
                pool.dma_start(sorted_d[r:r + n, :].rearrange("(p a) d -> p (a d)", p=P),
                               zero[:, 0:n * D // P].bitcast(F32)).then_inc(s_zero, 16)
            pool.affine_select(out=ident[:, :], in_=ident[:, :], compare_op=ALU.not_equal, fill=1.0,
                               base=0, pattern=[[-1, P]], channel_multiplier=1).then_inc(s_const, 1)
            pool.affine_select(out=before[:, :], in_=before[:, :], compare_op=ALU.is_gt, fill=0.0,
                               base=0, pattern=[[1, P]], channel_multiplier=-1).then_inc(s_const, 1)
            pool.affine_select(out=mask[:, 0:P], in_=mask[:, 0:P], compare_op=ALU.is_ge,
                               fill=MASKED / SCALE, base=0, pattern=[[1, P]],
                               channel_multiplier=-1).then_inc(s_const, 1)
            pool.affine_select(out=mask[:, P:2 * P], in_=mask[:, P:2 * P], compare_op=ALU.is_ge,
                               fill=MASKED / SCALE, base=0, pattern=[[-1, P]],
                               channel_multiplier=1).then_inc(s_const, 1)
            pool.affine_select(out=lower[:, :].rearrange("p (a b) -> p a b", a=E),
                               in_=lower[:, :].rearrange("p (a b) -> p a b", a=E),
                               compare_op=ALU.is_gt, fill=0.0, base=0, pattern=[[1, E], [-1, E]],
                               channel_multiplier=0).then_inc(s_const, 1)


        plain_take = layout(plain_arena, PLAIN_WORDS)
        xa = plain_take(2, T, D)
        xna = plain_take(2, T, D)
        xt_f = plain_take(2, KD, S)
        stats = sb("stats", [P, 2, T, 6], F32)
        part = sb("part", [P, 2, 4, T], F32)
        mean = sb("mean", [P, 2, T], F32)
        vary = sb("vary", [P, 2, T], F32)
        root = sb("root", [P, 2, T], F32)
        rs = sb("rs", [P, 2, 4, T], F32)
        a_ld = [sem(f"a_x_loaded{u}") for u in range(2)]
        a_free = sem("a_x_free")
        a_var = sem("a_variance")
        a_root = sem("a_root")
        a_dve = sem("a_dve_chain")
        a_xn = sem("a_xn_ready")
        a_st = [sem(f"a_xn_stored{u}") for u in range(2)]
        a_tr = sem("a_transposed")
        a_xt = sem("a_xt_ready")
        a_lg = sem("a_logits_done")
        a_lc = sem("a_logits_copied")

        def a_sync(sp):
            with sp.Fori(0, B // 2) as i:
                for u in range(2):
                    b = 2 * i + u
                    sp.wait_ge(a_free, b + 1)
                    sp.dma_start(xa[:, u, :, :],
                                 xf[ds(b * S, S), :].rearrange("(a p) d -> p a d", p=P)).then_inc(a_ld[u], 16)

        def a_store(act, i, u):
            act.wait_ge(a_xn, (2 * i + u) + 1)
            act.dma_start(xn_d[ds((2 * i + u) * S, S), :].rearrange("(a p) d -> p a d", p=P),
                          xna[:, u, :, :]).then_inc(a_st[u], 16)

        A_CH = 10

        def a_vector(dve):
            dve.sem_inc(a_free, 2)
            with dve.Fori(0, B // 2) as i:
                for u in range(2):
                    b = 2 * i + u
                    k = [0]

                    def then(ins):
                        k[0] += 1
                        ins.then_inc(a_dve, 1)
                        dve.wait_ge(a_dve, b * A_CH + k[0])
                    dve.wait_ge(a_ld[u], 16 * i + 16)
                    for a in range(T):
                        last = dve.bn_stats(stats[:, u, a, :], xa[:, u, a, :])
                    then(last)
                    m0, q0, m1, q1 = (stats[:, u, :, c] for c in (1, 2, 4, 5))
                    dve.tensor_tensor(part[:, u, 0, :], m0, m1, ALU.add)
                    dve.tensor_tensor(part[:, u, 1, :], m0, m1, ALU.subtract)
                    then(dve.tensor_tensor(part[:, u, 2, :], q0, q1, ALU.add))
                    dve.tensor_scalar(mean[:, u, :], part[:, u, 0, :], 0.5, None, ALU.mult)
                    then(dve.scalar_tensor_tensor(out=part[:, u, 3, :], in0=part[:, u, 1, :], scalar=0.25,
                                                  in1=part[:, u, 1, :], op0=ALU.mult, op1=ALU.mult))
                    var = vary[:, u, :]
                    then(dve.scalar_tensor_tensor(out=var, in0=part[:, u, 2, :], scalar=1.0 / D,
                                                  in1=part[:, u, 3, :], op0=ALU.mult, op1=ALU.add))
                    dve.sem_inc(a_var, 1)
                    dve.wait_ge(a_root, b + 1)
                    then(dve.reciprocal(rs[:, u, 0, :], root[:, u, :]))
                    then(dve.scalar_tensor_tensor(out=rs[:, u, 1, :], in0=var, scalar=EPS,
                                                  in1=rs[:, u, 0, :], op0=ALU.add, op1=ALU.mult))
                    then(dve.tensor_tensor(rs[:, u, 2, :], rs[:, u, 1, :], rs[:, u, 0, :], ALU.mult))
                    then(dve.tensor_scalar(rs[:, u, 3, :], rs[:, u, 2, :], -0.5, 1.5, ALU.mult, ALU.add))
                    then(dve.tensor_tensor(rs[:, u, 1, :], rs[:, u, 3, :], rs[:, u, 0, :], ALU.mult))
                    dve.wait_ge(a_st[u], 16 * i + 16)
                    dve.wait_ge(a_tr, b + 1)
                    for a in range(T):
                        last = dve.tensor_scalar(xna[:, u, a, :], xa[:, u, a, :], mean[:, u, a:a + 1],
                                                 rs[:, u, 1, a:a + 1], ALU.subtract, ALU.mult)
                    then(last)
                    dve.sem_inc(a_free, 1)
                    dve.sem_inc(a_xn, 1)
                    dve.wait_ge(a_lg, b + 1)
                    dve.tensor_copy(logits[:, ds(b * T, T), :].rearrange("p a e -> p (a e)"),
                                    psum[:, 4 + u, 0:T * E]).then_inc(a_lc, 1)
                    assert k[0] == A_CH

        def a_scalar(act):
            act.sem_inc(a_st[0], 16)
            act.sem_inc(a_st[1], 16)
            with act.Fori(0, B // 2) as i:
                for u in range(2):
                    b = 2 * i + u
                    act.wait_ge(a_var, b + 1)
                    act.activation(root[:, u, :], vary[:, u, :], ACT.Sqrt, bias=eps[:, 0:1]).then_inc(a_root, 1)
                    a_store(act, i, u)
                    act.wait_ge(a_tr, b + 3)
                    for c in range(KD):
                        last = act.copy(xt_f[:, u, c, :], psum[:, 2 * u + c, :])
                    last.then_inc(a_xt, 1)
            for u in range(2):
                act.wait_ge(a_st[u], 16 * (B // 2) + 16)

        eps = sb("eps", [P, 1], F32)

        def a_tensor(pe):
            pe.sem_inc(a_tr, 2)
            with pe.Fori(0, B // 2) as i:
                for u in range(2):
                    b = 2 * i + u
                    pe.wait_ge(a_xn, b + 1)
                    for c in range(KD):
                        for a in range(T):
                            last = pe.transpose(psum[:, 2 * u + c, a * P:(a + 1) * P],
                                                xna[:, u, a, c * P:(c + 1) * P], ident[:, :])
                    last.then_inc(a_tr, 1)
                    pe.wait_ge(a_xt, b + 1)
                    for a in range(T):
                        for c in range(KD):
                            last = pe.matmul(psum[:, 4 + u, a * E:(a + 1) * E],
                                             xt_f[:, u, c, a * P:(a + 1) * P], gate_sb[:, c, :],
                                             start=(c == 0), stop=(c == KD - 1))
                    last.then_inc(a_lg, 1)

        plain_take = layout(plain_arena, PLAIN_WORDS)
        LANES = B
        lb = plain_take(NT, E)
        cmp = plain_take(NT, E, E)
        rank = plain_take(NT, E)
        top = plain_take(2, NT, E)
        member = sb("member", [P, NT * E], BF16)
        totals = plain_take(E, NT)
        upto = plain_take(E, NT)
        steps = plain_take(max(NBLK + 1, LANES))
        steps_i = sb("steps_i", [P, max(NBLK + 1, LANES)], I32)
        used = plain_take(E, LANES)
        nblk = plain_take(E)
        first = plain_take(E)
        base = plain_take(E)
        position = plain_take(NT, E)
        pick = plain_take(NT, E)
        slot_f = plain_take(NT, 2)
        chosen = plain_take(NT, 2)
        own_cmp = plain_take(NBLK + 1, E)
        own_f = plain_take(NBLK + 1)
        zero_row = plain_take(TE)
        r_iota = sem("r_iota")
        r_dve = sem("r_dve_chain")
        r_member = sem("r_member")
        r_pre = sem("r_prefix")
        r_chosen = sem("r_chosen")

        def r_gpsimd(pool):
            pool.iota(steps_i[:, :], [[1, max(NBLK + 1, LANES)]], base=0, channel_multiplier=0).then_inc(r_iota, 1)
            pool.memset(zero_row[:, :], 0.0).then_inc(r_iota, 1)

        def r_tensor(pe):
            pe.wait_ge(r_member, 1)
            pe.matmul(psum[:, 0, :], before[:, :], member[:, :], start=True, stop=True)
            pe.matmul(psum[:, 1, :], ones[:, :], member[:, :], start=True, stop=True).then_inc(r_pre, 1)

        def r_scalar(act):
            act.wait_ge(r_chosen, 1)
            act.activation(coef[:, :, :].rearrange("p t k -> p (t k)"),
                           chosen[:, :, :].rearrange("p t k -> p (t k)"), ACT.Sigmoid)

        def r_vector(dve):
            k = [0]

            def then(ins):
                k[0] += 1
                ins.then_inc(r_dve, 1)
                dve.wait_ge(r_dve, k[0])

            def over_experts(v):
                return v.unsqueeze(2).to_broadcast([P, NT, E, E])
            dve.wait_ge(r_iota, 2)
            then(dve.tensor_copy(steps[:, :], steps_i[:, :]))
            then(dve.tensor_tensor(lb[:, :, :], logits[:, :, :],
                                   beta_sb[:, :].unsqueeze(1).to_broadcast([P, NT, E]), ALU.add))
            theirs = lb[:, :, :].unsqueeze(2).to_broadcast([P, NT, E, E])
            mine = lb[:, :, :].unsqueeze(3).to_broadcast([P, NT, E, E])
            then(dve.tensor_tensor(cmp[:, :, :, :], theirs, mine, ALU.is_gt))
            then(dve.tensor_reduce(rank[:, :, :], cmp[:, :, :, :], AX.X, ALU.add))
            then(dve.tensor_tensor(cmp[:, :, :, :], theirs, mine, ALU.is_equal))
            then(dve.tensor_tensor(cmp[:, :, :, :].rearrange("p t a b -> p t (a b)"),
                                   cmp[:, :, :, :].rearrange("p t a b -> p t (a b)"),
                                   lower[:, :].unsqueeze(1).to_broadcast([P, NT, E * E]), ALU.mult))
            then(dve.tensor_reduce(pick[:, :, :], cmp[:, :, :, :], AX.X, ALU.add))
            then(dve.tensor_tensor(rank[:, :, :], rank[:, :, :], pick[:, :, :], ALU.add))
            for n in range(2):
                then(dve.tensor_scalar(top[:, n, :, :], rank[:, :, :], float(n), None, ALU.is_equal))
            flat = lambda v: v.rearrange("p t e -> p (t e)")
            k[0] += 1
            dve.tensor_scalar(member[:, :], flat(rank[:, :, :]), 1.0, None, ALU.is_le).then_inc(r_member, 1)
            k[0] -= 1
            for n in range(2):
                then(dve.tensor_tensor(pick[:, :, :], top[:, n, :, :], logits[:, :, :], ALU.mult))
                then(dve.tensor_reduce(chosen[:, :, n], pick[:, :, :], AX.X, ALU.add))
            dve.sem_inc(r_chosen, 1)
            dve.wait_ge(r_pre, 1)
            then(dve.tensor_copy(totals[:, :, :], psum[:, 1, :].rearrange("p (t e) -> p e t", e=E)))
            then(dve.tensor_tensor_scan(upto[:, :, :].rearrange("p e t -> p (e t)"),
                                        totals[:, :, :].rearrange("p e t -> p (e t)"),
                                        zero_row[:, :], 0.0, ALU.add, ALU.add))
            then(dve.tensor_tensor(totals[:, :, :], upto[:, :, :], totals[:, :, :], ALU.subtract))
            then(dve.tensor_tensor(nblk[:, :], upto[:, :, NT - 1], totals[:, :, 0], ALU.subtract))
            then(dve.tensor_scalar(own_f[:, 0:LANES], steps[:, 0:LANES], float(BLK), None, ALU.mult))
            then(dve.tensor_tensor(used[:, :, :], nblk[:, :].unsqueeze(2).to_broadcast([P, E, LANES]),
                                   own_f[:, 0:LANES].unsqueeze(1).to_broadcast([P, E, LANES]), ALU.is_gt))
            then(dve.tensor_reduce(nblk[:, :], used[:, :, :], AX.X, ALU.add))
            then(dve.tensor_tensor_scan(first[:, :], nblk[:, :], zero_row[:, 0:E], 0.0, ALU.add, ALU.add))
            then(dve.tensor_tensor(first[:, :], first[:, :], nblk[:, :], ALU.subtract))
            then(dve.scalar_tensor_tensor(out=base[:, :], in0=first[:, :], scalar=float(BLK),
                                          in1=totals[:, :, 0], op0=ALU.mult, op1=ALU.subtract))
            then(dve.tensor_tensor(position[:, :, :].rearrange("p t e -> p e t"), totals[:, :, :],
                                   base[:, :].unsqueeze(2).to_broadcast([P, E, NT]), ALU.add))
            then(dve.tensor_tensor(flat(position[:, :, :]), psum[:, 0, :], flat(position[:, :, :]), ALU.add))
            for n in range(2):
                then(dve.tensor_tensor(pick[:, :, :], top[:, n, :, :], position[:, :, :], ALU.mult))
                then(dve.tensor_reduce(slot_f[:, :, n], pick[:, :, :], AX.X, ALU.add))
            then(dve.tensor_copy(slot[:, :, :], slot_f[:, :, :]))
            then(dve.tensor_tensor(own_cmp[:, :, :], steps[:, 0:NBLK + 1].unsqueeze(2).to_broadcast([P, NBLK + 1, E]),
                                   first[:, :].unsqueeze(1).to_broadcast([P, NBLK + 1, E]), ALU.is_ge))
            then(dve.tensor_reduce(own_f[:, :], own_cmp[:, :, :], AX.X, ALU.add))
            then(dve.tensor_scalar(owner[:, :], own_f[:, :], -1.0, None, ALU.add))


        split_take = layout(split_arena, SPLIT_WORDS)
        split_take(2, G, D)
        split_take(2, 3, KD, D)
        q_xt = split_take(2, 2, KD, S)
        q_qk = split_take(2, 2, KD, S)
        q_v = split_take(2, T, H, 2, DH)
        plain_take = layout(plain_arena, PLAIN_WORDS)
        q_x = plain_take(2, T, D)
        q_vf = plain_take(T, D)
        q_vs = plain_take(2, 2 * D)
        q_idx = sb("q_idx", [P, 2, T, 2], U32)
        q_ld = [sem(f"q_rows_loaded{u}") for u in range(2)]
        q_xfree = sem("q_rows_free")
        q_tr = sem("q_transposed")
        q_xhi = sem("q_xt_hi")
        q_xlo = sem("q_xt_lo")
        q_mm = sem("q_projected")
        q_hi = sem("q_proj_hi")
        q_lo = sem("q_proj_lo")
        q_vb = sem("q_v_biased")
        q_vhi = sem("q_v_hi")
        q_vlo = sem("q_v_lo")
        q_vsum = sem("q_v_summed")
        q_vt = sem("q_v_total")
        q_vtc = sem("q_v_total_copied")
        q_st = sem("q_qk_stored")
        q_vst = [sem(f"q_v_stored{u}") for u in range(2)]
        q_ix = sem("q_index_staged")
        q_free = sem("q_index_slot_free")
        q_sc = [sem(f"q_scattered{u}") for u in range(2)]
        q_dve = sem("q_dve_chain")

        def q_sync(sp):
            def rows(b, u):
                sp.dma_start(q_x[:, u, :, :],
                             xn_d[ds(b * S, S), :].rearrange("(a p) d -> p a d", p=P)).then_inc(q_ld[u], 16)
            sp.sem_inc(q_free, 2)
            rows(0, 0)
            rows(1, 1)
            with sp.Fori(0, B // 2 - 1) as i:
                for u in range(2):
                    b = 2 * i + u
                    sp.wait_ge(q_tr, b + 1)
                    sp.wait_ge(q_sc[u], 16 * 2 * T * i + 16 * 2 * T)
                    sp.sem_inc(q_free, 1)
                    rows(b + 2, u)

        def q_gpsimd(pool):
            with pool.Fori(0, B // 2) as i:
                for u in range(2):
                    pool.wait_ge(q_ld[u], 16 * i + 16)
                    hold(pool, q_ix, 2 * i + u + 1)
                    for a in range(T):
                        for n in range(2):
                            pool.indirect_dma_start(
                                sorted_d, bass.IndirectOffsetOnAxis(q_idx[:, u, a, n:n + 1], 0),
                                q_x[:, u, a, :], None).then_inc(q_sc[u], 16)
            for u in range(2):
                pool.wait_ge(q_sc[u], 16 * 2 * T * (B // 2))

        def q_tensor(pe):
            pe.sem_inc(q_vt, 1)
            with pe.Fori(0, B // 2) as i:
                for u in range(2):
                    b = 2 * i + u
                    pe.wait_ge(q_ld[u], 16 * i + 16)
                    pe.wait_ge(q_xlo, b + 1)
                    if u == 0:
                        pe.wait_ge(q_vtc, 2 * i + 1)
                    for c in range(KD):
                        for a in range(T):
                            last = pe.transpose(psum[:, c, a * P:(a + 1) * P],
                                                q_x[:, u, a, c * P:(c + 1) * P], ident[:, :])
                    last.then_inc(q_tr, 1)
                    pe.wait_ge(q_xlo, b + 2)
                    for n in range(2):
                        for m in range(KD):
                            bank = 2 + 2 * n + m
                            pe.wait_ge(q_lo, 4 * b + 2 * n + m + 1)
                            split_products(pe, psum[:, bank, :], [
                                (lambda part, c=c: wqkv[:, part, n, c, m * P:(m + 1) * P],
                                 lambda part, c=c: q_xt[:, u, part, c, :]) for c in range(KD)]
                            ).then_inc(q_mm, 1)
                    for h in range(2):
                        pe.wait_ge(q_vb, 2 * b + h + 1)
                        for a in (2 * h, 2 * h + 1):
                            last = split_products(pe, psum[:, 6 + h, (a % 2) * D:(a % 2 + 1) * D], [
                                (lambda part, c=c: q_xt[:, u, part, c, a * P:(a + 1) * P],
                                 lambda part, c=c: wqkv[:, part, 2, c, :]) for c in range(KD)])
                        last.then_inc(q_mm, 1)
                    if u == 1:
                        for w in range(2):
                            pe.wait_ge(q_vsum, 2 * i + w + 1)
                            pe.wait_ge(q_vtc, 2 * i + w + 1)
                            for g in range(G):
                                last = pe.matmul(psum[:, 0, g:g + 1], q_vs[:, w, g * P:(g + 1) * P],
                                                 tiny[:, :], start=True, stop=True)
                            last.then_inc(q_vt, 1)

        def q_scalar(act):
            for u in range(2):
                act.sem_inc(q_vst[u], 16)
            act.sem_inc(q_st, 64)
            with act.Fori(0, B // 2) as i:
                for u in range(2):
                    b = 2 * i + u
                    act.wait_ge(q_tr, b + 1)
                    for c in range(KD):
                        act.copy(q_xt[:, u, 0, c, :], psum[:, c, :]).then_inc(q_xhi, 1)
                    act.wait_ge(q_st, 64 * b + 64)
                    for n in range(2):
                        for m in range(KD):
                            act.wait_ge(q_mm, 6 * b + 2 * n + m + 1)
                            act.activation(q_qk[:, n, 0, m, :], psum[:, 2 + 2 * n + m, :], ACT.Identity,
                                           bias=bqk[:, n, m:m + 1]).then_inc(q_hi, 1)
                    act.wait_ge(q_vst[u], 16 * i + 16)
                    for h in range(2):
                        act.wait_ge(q_vb, 2 * b + h + 3)
                        act.copy(q_v[:, u, 2 * h:2 * h + 2, :, 0, :],
                                 q_vf[:, 2 * h:2 * h + 2, :].rearrange("p a (h d) -> p a h d", h=H)
                                 ).then_inc(q_vhi, 1)
                    act.wait_ge(q_lo, 4 * b + 8)
                    for n, dram in enumerate((q_d, k_d)):
                        for part in range(2):
                            act.dma_start(dram[ds(b, 1), part, :, :].rearrange("o (m p) s -> p (o m) s", p=P),
                                          q_qk[:, n, part, :, :].bitcast(F32)).then_inc(q_st, 16)
                    act.wait_ge(q_vlo, 2 * b + 4)
                    act.dma_start(v_d[ds(b, 1), :, :, :].rearrange("o p a c -> p (o a) c"),
                                  q_v[:, u, :, :, :, :].rearrange("p a h s d -> p a (h s d)").bitcast(F32)
                                  ).then_inc(q_vst[u], 16)
            act.wait_ge(q_st, 64 * B + 64)
            for u in range(2):
                act.wait_ge(q_vst[u], 16 * (B // 2) + 16)

        Q_CH = 3

        def q_vector(dve):
            dve.sem_inc(q_xlo, 1)
            dve.sem_inc(q_lo, 4)
            dve.sem_inc(q_vb, 2)
            dve.sem_inc(q_vlo, 2)
            dve.sem_inc(q_vtc, 1)
            with dve.Fori(0, B // 2) as i:
                for u in range(2):
                    b = 2 * i + u
                    dve.wait_ge(q_free, b + 1)
                    dve.tensor_copy(q_idx[:, u, :, :], slot[:, ds(b * T, T), :]).then_inc(q_ix, 1)
                    for c in range(KD):
                        dve.wait_ge(q_xhi, 2 * b + c + 1)
                        last = dve.tensor_tensor(q_xt[:, u, 1, c, :], psum[:, c, :],
                                                 q_xt[:, u, 0, c, :].bitcast(F32), ALU.subtract)
                    last.then_inc(q_xlo, 1)
                    for n in range(2):
                        for m in range(KD):
                            dve.wait_ge(q_hi, 4 * b + 2 * n + m + 1)
                            dve.scalar_tensor_tensor(out=q_qk[:, n, 1, m, :], in0=psum[:, 2 + 2 * n + m, :],
                                                     scalar=bqk[:, n, m:m + 1],
                                                     in1=q_qk[:, n, 0, m, :].bitcast(F32),
                                                     op0=ALU.add, op1=ALU.subtract).then_inc(q_lo, 1)
                    for h in range(2):
                        dve.wait_ge(q_mm, 6 * b + 4 + h + 1)
                        dve.wait_ge(q_vlo, 2 * b + h + 1)
                        dve.tensor_tensor(q_vf[:, 2 * h:2 * h + 2, :],
                                          psum[:, 6 + h, :].rearrange("p (a d) -> p a d", a=2),
                                          bv_sb[:, :].unsqueeze(1).to_broadcast([P, 2, D]),
                                          ALU.add).then_inc(q_vb, 1)
                    for h in range(2):
                        dve.wait_ge(q_vhi, 2 * b + h + 1)
                        dve.tensor_tensor(q_v[:, u, 2 * h:2 * h + 2, :, 1, :],
                                          q_vf[:, 2 * h:2 * h + 2, :].rearrange("p a (h d) -> p a h d", h=H),
                                          q_v[:, u, 2 * h:2 * h + 2, :, 0, :].bitcast(F32),
                                          ALU.subtract).then_inc(q_vlo, 1)
                    vt = [q_v[:, u, a, :, :, :].rearrange("p h s d -> p (h s d)").bitcast(F32) for a in range(T)]
                    total = q_vs[:, u, :]
                    dve.wait_ge(q_vlo, 2 * b + 4)
                    dve.wait_ge(q_vt, 2 * i + 1)
                    dve.tensor_tensor(total, vt[0], vt[1], ALU.add).then_inc(q_dve, 1)
                    for a in (2, 3):
                        dve.wait_ge(q_dve, Q_CH * b + a - 1)
                        dve.tensor_tensor(total, total, vt[a], ALU.add).then_inc(q_dve, 1)
                    dve.wait_ge(q_dve, Q_CH * b + 3)
                    dve.sem_inc(q_vsum, 1)
                    if u == 1:
                        for w in range(2):
                            dve.wait_ge(q_vt, 2 * i + w + 2)
                            dve.tensor_copy(vtot[:, ds(2 * i + w, 1), :].rearrange("p o g -> p (o g)"),
                                            psum[:, 0, 0:G]).then_inc(q_vtc, 1)

        split_take = layout(split_arena, SPLIT_WORDS)
        split_take(2, G, D)
        c_w = split_take(2, 2, 3, 1024)
        c_xt = split_take(2, 2, KD, S)
        c_h = split_take(2, 2, MC, S)
        plain_take = layout(plain_arena, PLAIN_WORDS)
        c_raw = plain_take(3, 1024)
        c_x = plain_take(T, D)
        c_sg = plain_take(2, S)
        c_hf = plain_take(2, S)
        c_y = plain_take(2, T, D)
        c_ldw = [sem(f"c_raw_loaded{n}") for n in range(3)]
        c_ldx = sem("c_rows_loaded")
        c_tr = sem("c_transposed")
        c_xhi = sem("c_xt_hi")
        c_xlo = sem("c_xt_lo")
        c_whi = sem("c_w_hi")
        c_wlo = sem("c_w_lo")
        c_gu = sem("c_gate_up")
        c_silu = sem("c_silu")
        c_mul = sem("c_hidden")
        c_hhi = sem("c_hidden_hi")
        c_hlo = sem("c_hidden_lo")
        c_dn = sem("c_down")
        c_yc = sem("c_y_copied")
        c_st = [sem(f"c_y_stored{u}") for u in range(2)]

        def gate_up(pe, m, banks, w, xt):
            for n in range(2):
                last = split_products(pe, psum[:, banks[n], :], [
                    (lambda part, c=c: w(part, n, c * M + m * P, P), lambda part, c=c: xt(part, c))
                    for c in range(KD)])
            return last

        def down(pe, m, h, w, first):
            for a in range(T):
                for k, (p, q) in enumerate(PASSES):
                    last = pe.matmul(psum[:, 6 + a // 2, (a % 2) * D:(a % 2 + 1) * D],
                                     h(p, m, a), w(q, 2, m * D, D),
                                     start=(first and k == 0 and a % 2 == 0), stop=(m == MC - 1 and k == 2),
                                     skip_group_check=True)
            return last

        def c_sync(sp):
            def rows(blk):
                sp.dma_start(c_x[:, :, :], sorted_d[ds(blk * BLK, BLK), :].rearrange("(a p) d -> p a d", p=P)
                             ).then_inc(c_ldx, 16)

            def weights(e, k):
                for n, w in enumerate((gate_w, up_w, down_w)):
                    sp.wait_ge(c_wlo, k + n)
                    rowsz = w.shape[2]
                    sp.dma_start(c_raw[:, n, :].rearrange("p (k n) -> p k n", n=rowsz),
                                 w[ds(e, 1), :, :].rearrange("o (k p) n -> p (o k) n", p=P)).then_inc(c_ldw[n], 16)
            rows(0)
            e0 = sp.value_load(owner[0:1, 0:1], min_val=0, max_val=E - 1)
            weights(e0, 1)
            with sp.Fori(0, NBLK // 2) as i:
                for u in range(2):
                    blk = 2 * i + u
                    sp.wait_ge(c_tr, blk + 1)
                    rows(blk + 1)
                    e = sp.value_load(owner[0:1, ds(blk + 1, 1)], min_val=0, max_val=E - 1)
                    weights(e, 3 * blk + 4)

        def c_tensor(pe):
            def turn():
                for c in range(KD):
                    for a in range(T):
                        last = pe.transpose(psum[:, 4 + c, a * P:(a + 1) * P],
                                            c_x[:, a, c * P:(c + 1) * P], ident[:, :])
                last.then_inc(c_tr, 1)
            pe.wait_ge(c_ldx, 16)
            turn()
            with pe.Fori(0, NBLK // 2) as i:
                for u in range(2):
                    blk = 2 * i + u
                    w = lambda part, n, at, cols: c_w[:, u, part, n, at:at + cols]
                    pe.wait_ge(c_xlo, blk + 1)
                    pe.wait_ge(c_wlo, 3 * blk + 6)
                    for m in range(MC):
                        pe.wait_ge(c_mul, 4 * blk + m + 1)
                        gate_up(pe, m, (2 * (m % 2), 2 * (m % 2) + 1), w,
                                lambda part, c: c_xt[:, u, part, c, :]).then_inc(c_gu, 1)
                    pe.wait_ge(c_ldx, 16 * blk + 32)
                    turn()
                    pe.wait_ge(c_yc, 2 * blk + 2)
                    for m in range(MC):
                        pe.wait_ge(c_hlo, 4 * blk + m + 3)
                        last = down(pe, m, lambda part, m, a: c_h[:, u, part, m, a * P:(a + 1) * P], w, m == 0)
                    last.then_inc(c_dn, 1)

        def c_scalar(act):
            def w_hi(v, n, k):
                act.wait_ge(c_ldw[n], k)
                act.copy(c_w[:, v, 0, n, :], c_raw[:, n, :]).then_inc(c_whi, 1)

            def x_hi(v, k):
                act.wait_ge(c_tr, k)
                for c in range(KD):
                    act.copy(c_xt[:, v, 0, c, :], psum[:, 4 + c, :]).then_inc(c_xhi, 1)
            act.sem_inc(c_dn, 1)
            act.sem_inc(c_st[0], 16)
            act.sem_inc(c_st[1], 16)
            for n in range(3):
                w_hi(0, n, 16)
            x_hi(0, 1)
            with act.Fori(0, NBLK // 2) as i:
                for u in range(2):
                    blk = 2 * i + u

                    def hid_hi(m):
                        act.wait_ge(c_mul, 4 * blk + m + 3)
                        act.copy(c_h[:, u, 0, m, :], c_hf[:, m % 2, :]).then_inc(c_hhi, 1)
                    for m in range(MC):
                        act.wait_ge(c_gu, 4 * blk + m + 1)
                        act.activation(c_sg[:, m % 2, :], psum[:, 2 * (m % 2), :], ACT.Silu).then_inc(c_silu, 1)
                        if m == 0:
                            act.wait_ge(c_dn, blk + 1)
                        if m >= 1:
                            hid_hi(m - 1)
                        if m < 3:
                            w_hi(1 - u, m, 16 * blk + 32)
                    hid_hi(MC - 1)
                    x_hi(1 - u, blk + 2)
                    act.wait_ge(c_yc, 2 * blk + 4)
                    act.dma_start(y_d[ds(blk * BLK, BLK), :].rearrange("(a p) d -> p a d", p=P),
                                  c_y[:, u, :, :]).then_inc(c_st[u], 16)
            for u in range(2):
                act.wait_ge(c_st[u], 16 * (NBLK // 2) + 16)

        def c_vector(dve):
            def w_lo(v, n, k):
                dve.wait_ge(c_whi, k)
                dve.tensor_tensor(c_w[:, v, 1, n, :], c_raw[:, n, :], c_w[:, v, 0, n, :].bitcast(F32),
                                  ALU.subtract).then_inc(c_wlo, 1)

            def x_lo(v, k):
                for c in range(KD):
                    dve.wait_ge(c_xhi, k + c)
                    last = dve.tensor_tensor(c_xt[:, v, 1, c, :], psum[:, 4 + c, :],
                                             c_xt[:, v, 0, c, :].bitcast(F32), ALU.subtract)
                last.then_inc(c_xlo, 1)
            dve.sem_inc(c_wlo, 3)
            dve.sem_inc(c_mul, 2)
            dve.sem_inc(c_hlo, 2)
            dve.sem_inc(c_yc, 2)
            for n in range(3):
                w_lo(0, n, n + 1)
            x_lo(0, 1)
            with dve.Fori(0, NBLK // 2) as i:
                for u in range(2):
                    blk = 2 * i + u

                    def hid_lo(m):
                        dve.wait_ge(c_hhi, 4 * blk + m + 1)
                        dve.tensor_tensor(c_h[:, u, 1, m, :], c_hf[:, m % 2, :],
                                          c_h[:, u, 0, m, :].bitcast(F32), ALU.subtract).then_inc(c_hlo, 1)
                    for m in range(MC):
                        dve.wait_ge(c_silu, 4 * blk + m + 1)
                        dve.wait_ge(c_hlo, 4 * blk + m + 1)
                        dve.tensor_tensor(c_hf[:, m % 2, :], psum[:, 2 * (m % 2) + 1, :], c_sg[:, m % 2, :],
                                          ALU.mult).then_inc(c_mul, 1)
                        if m >= 1:
                            hid_lo(m - 1)
                        if m < 3:
                            w_lo(1 - u, m, 3 * blk + m + 4)
                    hid_lo(MC - 1)
                    x_lo(1 - u, 2 * blk + 3)
                    dve.wait_ge(c_dn, blk + 2)
                    dve.wait_ge(c_st[u], 16 * i + 16)
                    for h in range(2):
                        dve.tensor_copy(c_y[:, u, 2 * h:2 * h + 2, :].rearrange("p a d -> p (a d)"),
                                        psum[:, 6 + h, :]).then_inc(c_yc, 1)

        split_take = layout(split_arena, SPLIT_WORDS)
        split_take(2, G, D)
        b_w = split_take(2, 3, 1024)
        b_xt = split_take(2, KD, S)
        b_h = split_take(2, MC, S)
        b_q = split_take(2, 2, S)
        b_k = split_take(2, 2, 2, S)
        b_v = split_take(2, T, HG, P)
        b_pt = split_take(2, 2, 8, P)
        b_cx = split_take(2, G, S)
        plain_take = layout(plain_arena, PLAIN_WORDS)
        b_raw = plain_take(3, 1024)
        plain_take = layout(plain_arena, PLAIN_WORDS)
        b_x = plain_take(T, D)
        b_o = plain_take(T, D)
        b_y = plain_take(2, T, D)
        b_p = plain_take(4, T, 2 * P)
        b_sg = plain_take(2, S)
        b_hf = plain_take(2, S)
        b_nm = sb("b_nm", [P, 4, T], F32)
        b_zs = sb("b_zs", [P, 4, T], F32)
        b_rz = sb("b_rz", [P, 4, T], F32)
        b_vt = sb("b_vt", [P, G], F32)
        b_cf = sb("b_cf", [P, T, 2], F32)
        b_ix = sb("b_ix", [P, T, 2], U32)
        b_ldw = sem("b_shared_loaded")
        b_whi = sem("b_shared_hi")
        b_wlo = sem("b_shared_lo")
        b_zeroed = sem("b_zeroed")
        b_ldx = sem("b_rows_loaded")
        b_ldo = sem("b_x_loaded")
        b_kv = [sem(f"b_qkv_loaded{s}") for s in range(2)]
        b_tr = sem("b_transposed")
        b_xhi = sem("b_xt_hi")
        b_xlo = sem("b_xt_lo")
        b_gu = sem("b_gate_up")
        b_silu = sem("b_silu")
        b_mul = sem("b_hidden")
        b_hhi = sem("b_hidden_hi")
        b_hlo = sem("b_hidden_lo")
        b_s = sem("b_scores")
        b_mx = sem("b_masked_max")
        b_ex = sem("b_exp")
        b_rc = sem("b_reciprocal")
        b_nr = sem("b_normalised")
        b_pT = sem("b_probs_transposed")
        b_phi = sem("b_probs_hi")
        b_plo = sem("b_probs_lo")
        b_pv = sem("b_values_summed")
        b_chi = sem("b_context_hi")
        b_clo = sem("b_context_lo")
        b_mm = sem("b_products_done")
        b_stg = sem("b_staged")
        b_ga = sem("b_gathered")
        b_xb = sem("b_x_biased")
        b_f = sem("b_sum_chain")
        b_fin = sem("b_result_ready")
        b_st = sem("b_result_stored")
        LAG_T, LAG_V = 2, 3
        BLOCK = {(0, 0): 1, (1, 0): 2, (1, 1): 3, (2, 1): 4, (2, 2): 5, (3, 2): 6, (3, 3): 7}

        def b_sync(sp):
            for n, w in enumerate((sh_gate, sh_up, sh_down)):
                sp.dma_start(b_raw[:, n, :].rearrange("p (k n) -> p k n", n=w.shape[2]),
                             w.rearrange("o (k p) n -> p (o k) n", p=P)).then_inc(b_ldw, 16)
            sp.wait_ge(b_zeroed, 1)
            sp.wait_ge(b_whi, 6)

            def group(b, g):
                s = g % 2
                sp.wait_ge(b_pv, 16 * b + 4 * g + 4)
                for c in range(4):
                    sp.dma_start(b_q[32 * c:32 * c + 32, s, :, :].bitcast(F32),
                                 q_d[ds(b, 1), c // 2, g * 64:(g + 1) * 64, :].rearrange(
                                     "o (h w) s -> w (o h) s", h=2)).then_inc(b_kv[s], 16)
                    for w in range(2):
                        sp.dma_start(b_k[32 * c + 16 * w:32 * c + 16 * w + 16, s, :, w, :].bitcast(F32),
                                     k_d[ds(b, 1), c % 2, g * 64:(g + 1) * 64, :].rearrange(
                                         "o (h w d) s -> w d (o h) s", h=2, w=2)[w]).then_inc(b_kv[s], 16)
                    sp.dma_start(b_v[:, s, :, c, 32 * c:32 * c + 32].bitcast(F32),
                                 v_d[ds(b, 1), :, :, g * P + 32 * c:g * P + 32 * c + 32].rearrange(
                                     "o p a c -> p (o a) c")).then_inc(b_kv[s], 16)
            with sp.Fori(0, B) as b:
                sp.wait_ge(b_tr, b + 1)
                sp.dma_start(b_x[:, :, :], xn_d[ds(b * S, S), :].rearrange("(a p) d -> p a d", p=P)
                             ).then_inc(b_ldx, 16)
                group(b, 0)
                group(b, 1)
                sp.wait_ge(b_st, 16 * b + 16)
                sp.dma_start(b_o[:, :, :], xf[ds(b * S, S), :].rearrange("(a p) d -> p a d", p=P)
                             ).then_inc(b_ldo, 16)
                group(b, 2)
                group(b, 3)

        def b_gpsimd(pool):
            pool.memset(b_k.bitcast(F32), 0.0)
            pool.memset(b_v.bitcast(F32), 0.0)
            pool.memset(b_pt[:, :, :, 0, :].bitcast(F32), 0.0).then_inc(b_zeroed, 1)
            pool.wait_ge(b_zeroed, 1)
            with pool.Fori(0, B) as b:
                for h in range(H + 1):
                    if h >= 1:
                        n = h - 1
                        hold(pool, b_rc, 16 * b + n + 1)
                        for i in range(T):
                            v = b_p[:, n % 4, i, 0:(P if i == 0 else 2 * P)]
                            last = pool.tensor_scalar(v, v, b_rz[:, n % 4, i:i + 1], 0.0, ALU.mult, ALU.add)
                        last.then_inc(b_nr, 1)
                    if h in (4, 5, 6, 7):
                        a = h - 4
                        if h == 4:
                            pool.wait_ge(b_stg, b + 1)
                            hold(pool, b_fin, b + 1)
                        for n in range(2):
                            pool.indirect_dma_start(b_y[:, n, a, :], None, y_d,
                                                    bass.IndirectOffsetOnAxis(b_ix[:, a, n:n + 1], 0)
                                                    ).then_inc(b_ga, 16)
                    if h in (9, 10, 11, 12):
                        a = h - 9
                        if h == 9:
                            pool.wait_ge(b_ldo, 16 * b + 16)
                        pool.tensor_tensor(b_o[:, a, :], b_o[:, a, :], bo_sb[:, :], ALU.add).then_inc(b_xb, 1)

        def b_tensor(pe):
            pe.sem_inc(b_tr, 1)
            pe.sem_inc(b_pv, 8)
            w = lambda part, n, at, cols: b_w[:, part, n, at:at + cols]

            def scores(b, h):
                g, r = h // HG, h % HG
                if r == 0:
                    pe.wait_ge(b_kv[g % 2], 256 * (2 * b + g // 2) + 256)
                if h == 0:
                    pe.wait_ge(b_mul, 4 * b + 3)
                pe.wait_ge(b_mx, 16 * b + h + 1)
                for i in range(T):
                    last = pe.matmul(psum[:, i // 2, (i % 2) * 2 * P:(i % 2 + 1) * 2 * P],
                                     b_q[:, g % 2, r // 2, i * P:(i + 1) * P],
                                     b_k[:, g % 2, r // 2, r % 2, max(i - 1, 0) * P:(max(i - 1, 0) + 2) * P],
                                     start=True, stop=True)
                last.then_inc(b_s, 1)

            def turn_probs(b, h):
                if h == 0:
                    pe.wait_ge(b_mul, 4 * b + 4)
                pe.wait_ge(b_plo, 16 * b + h + 1)
                pe.wait_ge(b_nr, 16 * b + h + 1)
                for (i, j), s in BLOCK.items():
                    half = j if i == 0 else j - i + 1
                    last = pe.transpose(psum[:, 2 + (s - 1) // 4, ((s - 1) % 4) * P:((s - 1) % 4 + 1) * P],
                                        b_p[:, h % 4, i, half * P:(half + 1) * P], ident[:, :])
                last.then_inc(b_pT, 1)

            def values(b, h):
                g, r = h // HG, h % HG
                if r == 0:
                    pe.wait_ge(b_clo, 4 * b + g + 1)
                pe.wait_ge(b_plo, 16 * b + h + 2)
                for j in range(T):
                    at = j if j < T - 1 else T - 2
                    for part in range(2):
                        blocks = (b_pt[:, h % 2, part, 2 * j + 1:2 * j + 3, :] if j < T - 1
                                  else b_pt[:, h % 2, part, 0:8:7, :])
                        last = pe.matmul(psum[:, 4 + g % 2, at * P:(at + 2) * P],
                                         b_v[:, g % 2, j, r, :], blocks,
                                         start=(r == 0 and j == 0 and part == 0),
                                         stop=(r == HG - 1 and j == T - 1 and part == 1),
                                         skip_group_check=True)
                last.then_inc(b_pv, 1)

            def project(b, g):
                pe.wait_ge(b_clo, 4 * b + g + 3)
                for a in range(T):
                    for k, (p, q) in enumerate(PASSES):
                        last = pe.matmul(psum[:, 6 + a // 2, (a % 2) * D:(a % 2 + 1) * D],
                                         b_cx[:, p, g, a * P:(a + 1) * P], wo[:, q, g, :],
                                         start=False, stop=(g == G - 1 and k == 2), skip_group_check=True)
                return last
            pe.wait_ge(b_whi, 6)
            with pe.Fori(0, B) as b:
                pe.wait_ge(b_ldx, 16 * b + 16)
                pe.wait_ge(b_clo, 4 * b + 2)
                for c in range(KD):
                    for a in range(T):
                        last = pe.transpose(psum[:, 4 + c, a * P:(a + 1) * P],
                                            b_x[:, a, c * P:(c + 1) * P], ident[:, :])
                last.then_inc(b_tr, 1)
                pe.wait_ge(b_xlo, b + 1)
                for m in range(MC):
                    if m == 0:
                        pe.wait_ge(b_mx, 16 * b + 1)
                    if m == 1:
                        pe.wait_ge(b_plo, 16 * b + 1)
                    if m >= 2:
                        pe.wait_ge(b_mul, 4 * b + m - 1)
                    gate_up(pe, m, (2 * (m % 2), 2 * (m % 2) + 1), w,
                            lambda part, c: b_xt[:, part, c, :]).then_inc(b_gu, 1)
                pe.wait_ge(b_fin, b + 1)
                for m in range(MC):
                    pe.wait_ge(b_hlo, 4 * b + m + 3)
                    down(pe, m, lambda part, m, a: b_h[:, part, m, a * P:(a + 1) * P], w, m == 0)
                for h in range(H + LAG_V):
                    if h < H:
                        scores(b, h)
                    if LAG_T <= h < H + LAG_T:
                        turn_probs(b, h - LAG_T)
                    if h >= LAG_V:
                        values(b, h - LAG_V)
                        if (h - LAG_V) % HG == 1 and h - LAG_V > HG:
                            project(b, (h - LAG_V) // HG - 1)
                project(b, G - 1).then_inc(b_mm, 1)

        def b_scalar(act):
            act.wait_ge(b_ldw, 48)
            for n in range(3):
                act.copy(b_w[:, 0, n, :], b_raw[:, n, :]).then_inc(b_whi, 1)
            act.sem_inc(b_st, 16)
            with act.Fori(0, B) as b:
                act.wait_ge(b_tr, b + 2)
                for c in range(KD):
                    act.copy(b_xt[:, 0, c, :], psum[:, 4 + c, :]).then_inc(b_xhi, 1)

                def hid_hi(m):
                    act.wait_ge(b_mul, 4 * b + m + 1)
                    act.copy(b_h[:, 0, m, :], b_hf[:, m % 2, :]).then_inc(b_hhi, 1)
                for m in range(MC):
                    act.wait_ge(b_gu, 4 * b + m + 1)
                    act.activation(b_sg[:, m % 2, :], psum[:, 2 * (m % 2), :], ACT.Silu).then_inc(b_silu, 1)
                    if m >= 1:
                        hid_hi(m - 1)
                hid_hi(MC - 1)
                for h in range(H + LAG_V + 1):
                    if h < H:
                        act.wait_ge(b_mx, 16 * b + h + 2)
                        for i in range(T):
                            v = b_p[:, h % 4, i, 0:(P if i == 0 else 2 * P)]
                            last = act.activation(v, v, ACT.Exp, bias=b_nm[:, h % 4, i:i + 1], scale=-1.0,
                                                  accum_out=b_zs[:, h % 4, i:i + 1])
                        last.then_inc(b_ex, 1)
                    n = h - LAG_T
                    if 0 <= n < H:
                        act.wait_ge(b_pT, 16 * b + n + 1)
                        act.wait_ge(b_pv, 16 * b + n + 7)
                        act.copy(b_pt[:, n % 2, 0, 1:5, :].rearrange("p a b -> p (a b)"),
                                 psum[:, 2, :]).then_inc(b_phi, 1)
                        act.copy(b_pt[:, n % 2, 0, 5:8, :].rearrange("p a b -> p (a b)"),
                                 psum[:, 3, 0:3 * P]).then_inc(b_phi, 1)
                    n = h - LAG_V - 1
                    if n >= 0 and n % HG == HG - 1:
                        g = n // HG
                        act.wait_ge(b_pv, 16 * b + n + 9)
                        if g == 0:
                            act.wait_ge(b_stg, b + 1)
                            act.wait_ge(b_mm, b + 1)
                        act.activation(b_cx[:, 0, g, :], psum[:, 4 + g % 2, :], ACT.Identity,
                                       bias=b_vt[:, g:g + 1]).then_inc(b_chi, 1)
                act.wait_ge(b_fin, b + 2)
                act.dma_start(of[ds(b * S, S), :].rearrange("(a p) d -> p a d", p=P), b_o[:, :, :]
                              ).then_inc(b_st, 16)
            act.wait_ge(b_st, 16 * B + 16)

        def b_vector(dve):
            for n in range(3):
                dve.wait_ge(b_whi, n + 1)
                dve.tensor_tensor(b_w[:, 1, n, :], b_raw[:, n, :], b_w[:, 0, n, :].bitcast(F32),
                                  ALU.subtract).then_inc(b_wlo, 1)
            dve.wait_ge(b_wlo, 3)
            dve.sem_inc(b_whi, 3)
            dve.sem_inc(b_mx, 1)
            dve.sem_inc(b_hlo, 2)
            dve.sem_inc(b_plo, 1)
            dve.sem_inc(b_clo, 2)
            dve.sem_inc(b_fin, 1)
            dve.sem_inc(b_mm, 1)
            with dve.Fori(0, B) as b:
                dve.tensor_copy(b_ix[:, :, :], slot[:, ds(b * T, T), :])
                dve.tensor_copy(b_cf[:, :, :], coef[:, ds(b * T, T), :])
                dve.tensor_copy(b_vt[:, :], vtot[:, ds(b, 1), :].rearrange("p o g -> p (o g)")).then_inc(b_stg, 1)
                for c in range(KD):
                    dve.wait_ge(b_xhi, 2 * b + c + 1)
                    last = dve.tensor_tensor(b_xt[:, 1, c, :], psum[:, 4 + c, :],
                                             b_xt[:, 0, c, :].bitcast(F32), ALU.subtract)
                last.then_inc(b_xlo, 1)

                def hid_lo(m):
                    dve.wait_ge(b_hhi, 4 * b + m + 1)
                    dve.tensor_tensor(b_h[:, 1, m, :], b_hf[:, m % 2, :], b_h[:, 0, m, :].bitcast(F32),
                                      ALU.subtract).then_inc(b_hlo, 1)
                for m in range(MC):
                    dve.wait_ge(b_silu, 4 * b + m + 1)
                    dve.wait_ge(b_hlo, 4 * b + m + 1)
                    dve.tensor_tensor(b_hf[:, m % 2, :], psum[:, 2 * (m % 2) + 1, :], b_sg[:, m % 2, :],
                                      ALU.mult).then_inc(b_mul, 1)
                    if m >= 1:
                        hid_lo(m - 1)
                hid_lo(MC - 1)
                for h in range(H + LAG_V + 1):
                    if h < H:
                        hold(dve, b_s, 16 * b + h + 1)
                        for i in range(T):
                            cols = P if i == 0 else 2 * P
                            at = (i % 2) * 2 * P
                            last = dve.tensor_tensor_reduce(
                                b_p[:, h % 4, i, 0:cols], psum[:, i // 2, at:at + cols],
                                mask[:, 2 * P - cols:2 * P], -SCALE, 3e38, ALU.add, ALU.min,
                                b_nm[:, h % 4, i:i + 1])
                        last.then_inc(b_mx, 1)
                    n = h - 1
                    if 0 <= n < H:
                        dve.wait_ge(b_ex, 16 * b + n + 1)
                        dve.reciprocal(b_rz[:, n % 4, :], b_zs[:, n % 4, :]).then_inc(b_rc, 1)
                    n = h - LAG_T
                    if 0 <= n < H:
                        dve.wait_ge(b_phi, 2 * (16 * b + n) + 1)
                        dve.tensor_tensor(b_pt[:, n % 2, 1, 1:5, :].rearrange("p a b -> p (a b)"), psum[:, 2, :],
                                          b_pt[:, n % 2, 0, 1:5, :].rearrange("p a b -> p (a b)").bitcast(F32),
                                          ALU.subtract)
                        dve.wait_ge(b_phi, 2 * (16 * b + n) + 2)
                        dve.tensor_tensor(b_pt[:, n % 2, 1, 5:8, :].rearrange("p a b -> p (a b)"),
                                          psum[:, 3, 0:3 * P],
                                          b_pt[:, n % 2, 0, 5:8, :].rearrange("p a b -> p (a b)").bitcast(F32),
                                          ALU.subtract).then_inc(b_plo, 1)
                    n = h - LAG_V - 1
                    if n >= 0 and n % HG == HG - 1:
                        g = n // HG
                        dve.wait_ge(b_chi, 4 * b + g + 1)
                        dve.scalar_tensor_tensor(out=b_cx[:, 1, g, :], in0=psum[:, 4 + g % 2, :],
                                                 scalar=b_vt[:, g:g + 1], in1=b_cx[:, 0, g, :].bitcast(F32),
                                                 op0=ALU.add, op1=ALU.subtract).then_inc(b_clo, 1)
                    if h == H - 1:
                        dve.wait_ge(b_ga, 16 * 2 * T * b + 16 * 2 * T)
                        for n in range(2):
                            if n == 0:
                                dve.wait_ge(b_xb, T * b + T)
                            else:
                                dve.wait_ge(b_f, 2 * T * b + T)
                            for a in range(T):
                                dve.scalar_tensor_tensor(out=b_o[:, a, :], in0=b_y[:, n, a, :],
                                                         scalar=b_cf[:, a, n:n + 1], in1=b_o[:, a, :],
                                                         op0=ALU.mult, op1=ALU.add).then_inc(b_f, 1)
                dve.wait_ge(b_mm, b + 2)
                dve.wait_ge(b_f, 2 * T * b + 2 * T)
                for a in range(2):
                    v = b_o[:, 2 * a:2 * a + 2, :].rearrange("p a d -> p (a d)")
                    last = dve.tensor_tensor(v, psum[:, 6 + a, :], v, ALU.add)
                last.then_inc(b_fin, 1)

        @block.sync
        def _(sp):
            start_sync(sp)
            wall(sp, 1)
            a_sync(sp)
            wall(sp, 2)
            wall(sp, 3)
            q_sync(sp)
            wall(sp, 4)
            c_sync(sp)
            wall(sp, 5)
            b_sync(sp)

        @block.gpsimd
        def _(pool):
            start_gpsimd(pool)
            wall(pool, 1)
            wall(pool, 2)
            r_gpsimd(pool)
            pool.wait_ge(s_zero, N_ZERO)
            wall(pool, 3)
            q_gpsimd(pool)
            wall(pool, 4)
            wall(pool, 5)
            b_gpsimd(pool)

        @block.scalar
        def _(act):
            start_scalar(act)
            wall(act, 1)
            a_scalar(act)
            wall(act, 2)
            r_scalar(act)
            wall(act, 3)
            q_scalar(act)
            wall(act, 4)
            c_scalar(act)
            wall(act, 5)
            b_scalar(act)

        @block.vector
        def _(dve):
            start_vector(dve)
            wall(dve, 1)
            a_vector(dve)
            wall(dve, 2)
            r_vector(dve)
            wall(dve, 3)
            q_vector(dve)
            wall(dve, 4)
            c_vector(dve)
            wall(dve, 5)
            b_vector(dve)

        @block.tensor
        def _(pe):
            wall(pe, 1)
            a_tensor(pe)
            wall(pe, 2)
            r_tensor(pe)
            wall(pe, 3)
            q_tensor(pe)
            wall(pe, 4)
            c_tensor(pe)
            wall(pe, 5)
            b_tensor(pe)


def kernel(**inputs):
    import numpy as _np
    import concourse.bacc as _bacc
    from concourse.bass_utils import run_bass_kernel_spmd as _run

    pre = {n: _np.asarray(a) for n, a in inputs.items()}
    laid = {
        "x": pre["L0_attn_x"],
        "wq_t": pre["L0_attn_Wq"].T, "wk_t": pre["L0_attn_Wk"].T,
        "wv_t": pre["L0_attn_Wv"].T, "wo_t": pre["L0_attn_Wo"].T,
        "bq": pre["L0_attn_bq"], "bk": pre["L0_attn_bk"], "bv": pre["L0_attn_bv"], "bo": pre["L0_attn_bo"],
        "gate_t": pre["L0_ffn_gate_w"].T, "beta": pre["L0_ffn_beta"],
        "gate_w": pre["L0_ffn_gate_proj_w"], "up_w": pre["L0_ffn_up_proj_w"],
        "down_w": pre["L0_ffn_down_proj_w"],
        "sh_gate": pre["L0_ffn_shared_gate_w"], "sh_up": pre["L0_ffn_shared_up_w"],
        "sh_down": pre["L0_ffn_shared_down_w"],
    }
    nc = _bacc.Bacc("TRN2", target_bir_lowering=False, num_devices=1)
    arrays, args = {}, []
    for name, a in laid.items():
        a = _np.ascontiguousarray(a)
        arrays[f"in_{name}"] = a
        args.append(nc.dram_tensor(f"in_{name}", a.shape, mybir.dt.from_np(a.dtype), kind="ExternalInput").ap())
    args.append(nc.dram_tensor("out_0", pre["L0_attn_x"].shape, F32, kind="ExternalOutput").ap())
    moe_attention_layer(nc, *args)
    r = _run(nc, [arrays], core_ids=[0])
    return r.results[0]["out_0"]
```

```python
from contextlib import ExitStack

import concourse.bass as bass
from concourse import mybir

F32 = mybir.dt.float32
F32R = mybir.dt.float32r
BF16 = mybir.dt.bfloat16
U32 = mybir.dt.uint32
I32 = mybir.dt.int32
ALU = mybir.AluOpType
ACT = mybir.ActivationFunctionType
AX = mybir.AxisListType
ds = bass.ds

P = 128
PLAIN_WORDS = 12800
SPLIT_WORDS = 33792
EPS = 1e-5
ATTN_EPS = 1e-9
MASKED = -10000.0


def moe_attention_layer(nc, x, wq_t, wk_t, wv_t, wo_t, bq, bk, bv, bo, gate_t, beta,
                        gate_w, up_w, down_w, sh_gate, sh_up, sh_down, out):
    B, S, D = x.shape
    E = gate_w.shape[0]
    M = gate_w.shape[2]
    KD = D // P
    MC = M // P
    T = S // P
    NT = B * T
    H = 16
    DH = D // H
    SCALE = 1.0 / float(DH) ** 0.5
    HG = 4
    G = H // HG
    BLK = S
    NBLK = (2 * B * S + E * (BLK - 1)) // BLK
    NBLK += NBLK % 2
    ROWS = NBLK * BLK
    TE = NT * E

    xf = x.rearrange("b s d -> (b s) d")
    of = out.rearrange("b s d -> (b s) d")
    xn_d = nc.dram_tensor("xn_d", (B * S, D), F32).ap()
    sorted_d = nc.dram_tensor("sorted_d", (ROWS + BLK, D), F32).ap()
    y_d = nc.dram_tensor("y_d", (ROWS, D), F32).ap()
    q_d = nc.dram_tensor("q_d", (B, 2, D, S), F32).ap()
    k_d = nc.dram_tensor("k_d", (B, 2, D, S), F32).ap()
    v_d = nc.dram_tensor("v_d", (B, P, T, 2 * D), F32).ap()

    ctx = ExitStack()
    with ctx:
        def sb(name, shape, dt):
            return ctx.enter_context(nc.sbuf_tensor(name, shape, dt))

        def sem(name):
            return ctx.enter_context(nc.semaphore(name))

        psum = ctx.enter_context(nc.psum_tensor("psum", [P, 8, 512], F32))

        plain_arena = sb("plain_arena", [P, PLAIN_WORDS], F32)
        split_arena = sb("split_arena", [P, SPLIT_WORDS], F32R)

        def layout(arena, words):
            at = [0]

            def take(*shape):
                n = 1
                for m in shape:
                    n *= m
                assert at[0] + n <= words, (at[0] + n, words)
                view = arena[:, at[0]:at[0] + n]
                at[0] += n
                names = "abcde"[:len(shape)]
                sizes = {c: m for c, m in zip(names, shape)}
                return view.rearrange(f"p ({' '.join(names)}) -> p {' '.join(names)}", **sizes)
            return take

        split_take = layout(split_arena, SPLIT_WORDS)
        ident = sb("ident", [P, P], F32)
        before = sb("before", [P, P], BF16)
        ones = sb("ones", [P, P], BF16)
        tiny = sb("tiny", [P, 1], F32)
        mask = sb("mask", [P, 2 * P], F32)
        wo = split_take(2, G, D)
        gate_sb = sb("gate_sb", [P, KD, E], F32)
        beta_sb = sb("beta_sb", [P, E], F32)
        bqk = sb("bqk", [P, 2, KD], F32)
        bv_sb = sb("bv_sb", [P, D], F32)
        bo_sb = sb("bo_sb", [P, D], F32)
        logits = sb("logits", [P, NT, E], F32)
        slot = sb("slot", [P, NT, 2], U32)
        coef = sb("coef", [P, NT, 2], F32)
        owner = sb("owner", [P, NBLK + 1], I32)
        vtot = sb("vtot", [P, B, G], F32)

        s_w = sem("weights_loaded")
        s_const = sem("constants_ready")
        s_bar = sem("phase_barrier")

        block = ctx.enter_context(nc.Block())
        s_passed = sem("waits_passed")

        def hold(eng, semaphore, value):
            eng.wait_ge(semaphore, value)
            eng.sem_inc(s_passed, 1)

        def wall(eng, n):
            eng.drain().then_inc(s_bar, 1)
            eng.wait_ge(s_bar, 5 * n)

        PASSES = ((0, 0), (0, 1), (1, 0))

        def split_products(pe, out, chunks):
            for c, (lhs_t, rhs) in enumerate(chunks):
                for k, (p, q) in enumerate(PASSES):
                    last = pe.matmul(out, lhs_t(p), rhs(q), start=(c == 0 and k == 0),
                                     stop=(c == len(chunks) - 1 and k == 2))
            return last

        plain_take = layout(plain_arena, PLAIN_WORDS)
        wraw = plain_take(3, 1024)
        wqkv = split_take(2, 3, KD, D)
        zero = split_take(2048)
        s_whi = sem("weights_hi")

        def start_sync(sp):
            sp.dma_start(gate_sb[:, :, :], gate_t.rearrange("(k p) e -> p k e", p=P)).then_inc(s_w, 16)
            sp.dma_start(beta_sb[:, :], beta.partition_broadcast(P)).then_inc(s_w, 16)
            for n, b in enumerate((bq, bk)):
                sp.dma_start(bqk[:, n, :], b.rearrange("(k p) -> p k", p=P),
                             allow_slow_non_contiguous=True).then_inc(s_w, 16)
            sp.dma_start(bv_sb[:, :], bv.partition_broadcast(P)).then_inc(s_w, 16)
            sp.dma_start(bo_sb[:, :], bo.partition_broadcast(P)).then_inc(s_w, 16)
            for n, w in enumerate((wq_t, wk_t, wv_t)):
                sp.dma_start(wraw[:, n, 0:KD * D].rearrange("p (k n) -> p k n", k=KD),
                             w.rearrange("(k p) n -> p k n", p=P)).then_inc(s_w, 16)
            for g in range(G):
                for r in range(HG):
                    for half in range(2):
                        row = (g * HG + r) * DH
                        sp.dma_start(wraw[32 * r + 16 * half:32 * r + 16 * half + 16, g % 3,
                                          512 + (g // 3) * D:512 + (g // 3 + 1) * D],
                                     wo_t[row:row + DH, :]).then_inc(s_w, 16)

        N_W = 16 * (6 + 3 + 2 * H)

        def wo_raw(g):
            return wraw[:, g % 3, 512 + (g // 3) * D:512 + (g // 3 + 1) * D]

        def start_scalar(act):
            act.wait_ge(s_w, N_W)
            for n in range(3):
                act.copy(wqkv[:, 0, n, :, :].rearrange("p k n -> p (k n)"),
                         wraw[:, n, 0:KD * D]).then_inc(s_whi, 1)
            for g in range(G):
                act.copy(wo[:, 0, g, :], wo_raw(g)).then_inc(s_whi, 1)

        def start_vector(dve):
            dve.wait_ge(s_w, N_W)
            for n in range(3):
                dve.wait_ge(s_whi, n + 1)
                dve.tensor_tensor(wqkv[:, 1, n, :, :].rearrange("p k n -> p (k n)"),
                                  wraw[:, n, 0:KD * D],
                                  wqkv[:, 0, n, :, :].rearrange("p k n -> p (k n)").bitcast(F32),
                                  ALU.subtract)
            for g in range(G):
                dve.wait_ge(s_whi, 3 + g + 1)
                dve.tensor_tensor(wo[:, 1, g, :], wo_raw(g), wo[:, 0, g, :].bitcast(F32), ALU.subtract)

        s_pz = sem("pool_zeroed")
        s_zero = sem("sorted_rows_zeroed")
        ZCH = P * 2048 // D
        lower = sb("lower", [P, E * E], F32)

        N_ZERO = 16 * -(-(ROWS + BLK) // (P * 2048 // D))

        def start_gpsimd(pool):
            pool.memset(eps[:, :], EPS).then_inc(s_const, 1)
            pool.memset(zero.bitcast(F32), 0.0).then_inc(s_pz, 1)
            pool.memset(ident[:, :], 0.0).then_inc(s_pz, 1)
            pool.memset(before[:, :], 1.0).then_inc(s_pz, 1)
            pool.memset(mask[:, :], 0.0).then_inc(s_pz, 1)
            pool.memset(lower[:, :], 1.0).then_inc(s_pz, 1)
            pool.memset(ones[:, :], 1.0).then_inc(s_const, 1)
            pool.memset(tiny[:, :], ATTN_EPS).then_inc(s_const, 1)
            pool.wait_ge(s_pz, 5)
            for r in range(0, ROWS + BLK, ZCH):
                n = min(ZCH, ROWS + BLK - r)
                pool.dma_start(sorted_d[r:r + n, :].rearrange("(p a) d -> p (a d)", p=P),
                               zero[:, 0:n * D // P].bitcast(F32)).then_inc(s_zero, 16)
            pool.affine_select(out=ident[:, :], in_=ident[:, :], compare_op=ALU.not_equal, fill=1.0,
                               base=0, pattern=[[-1, P]], channel_multiplier=1).then_inc(s_const, 1)
            pool.affine_select(out=before[:, :], in_=before[:, :], compare_op=ALU.is_gt, fill=0.0,
                               base=0, pattern=[[1, P]], channel_multiplier=-1).then_inc(s_const, 1)
            pool.affine_select(out=mask[:, 0:P], in_=mask[:, 0:P], compare_op=ALU.is_ge,
                               fill=MASKED / SCALE, base=0, pattern=[[1, P]],
                               channel_multiplier=-1).then_inc(s_const, 1)
            pool.affine_select(out=mask[:, P:2 * P], in_=mask[:, P:2 * P], compare_op=ALU.is_ge,
                               fill=MASKED / SCALE, base=0, pattern=[[-1, P]],
                               channel_multiplier=1).then_inc(s_const, 1)
            pool.affine_select(out=lower[:, :].rearrange("p (a b) -> p a b", a=E),
                               in_=lower[:, :].rearrange("p (a b) -> p a b", a=E),
                               compare_op=ALU.is_gt, fill=0.0, base=0, pattern=[[1, E], [-1, E]],
                               channel_multiplier=0).then_inc(s_const, 1)


        plain_take = layout(plain_arena, PLAIN_WORDS)
        xa = plain_take(2, T, D)
        xna = plain_take(2, T, D)
        xt_f = plain_take(2, KD, S)
        stats = sb("stats", [P, 2, T, 6], F32)
        part = sb("part", [P, 2, 4, T], F32)
        mean = sb("mean", [P, 2, T], F32)
        vary = sb("vary", [P, 2, T], F32)
        root = sb("root", [P, 2, T], F32)
        rs = sb("rs", [P, 2, 4, T], F32)
        a_ld = [sem(f"a_x_loaded{u}") for u in range(2)]
        a_free = sem("a_x_free")
        a_var = sem("a_variance")
        a_root = sem("a_root")
        a_dve = sem("a_dve_chain")
        a_xn = sem("a_xn_ready")
        a_st = [sem(f"a_xn_stored{u}") for u in range(2)]
        a_tr = sem("a_transposed")
        a_xt = sem("a_xt_ready")
        a_lg = sem("a_logits_done")
        a_lc = sem("a_logits_copied")

        def a_sync(sp):
            with sp.Fori(0, B // 2) as i:
                for u in range(2):
                    b = 2 * i + u
                    sp.wait_ge(a_free, b + 1)
                    sp.dma_start(xa[:, u, :, :],
                                 xf[ds(b * S, S), :].rearrange("(a p) d -> p a d", p=P)).then_inc(a_ld[u], 16)

        def a_store(act, i, u):
            act.wait_ge(a_xn, (2 * i + u) + 1)
            act.dma_start(xn_d[ds((2 * i + u) * S, S), :].rearrange("(a p) d -> p a d", p=P),
                          xna[:, u, :, :]).then_inc(a_st[u], 16)

        A_CH = 10

        def a_vector(dve):
            dve.sem_inc(a_free, 2)
            with dve.Fori(0, B // 2) as i:
                for u in range(2):
                    b = 2 * i + u
                    k = [0]

                    def then(ins):
                        k[0] += 1
                        ins.then_inc(a_dve, 1)
                        dve.wait_ge(a_dve, b * A_CH + k[0])
                    dve.wait_ge(a_ld[u], 16 * i + 16)
                    for a in range(T):
                        last = dve.bn_stats(stats[:, u, a, :], xa[:, u, a, :])
                    then(last)
                    m0, q0, m1, q1 = (stats[:, u, :, c] for c in (1, 2, 4, 5))
                    dve.tensor_tensor(part[:, u, 0, :], m0, m1, ALU.add)
                    dve.tensor_tensor(part[:, u, 1, :], m0, m1, ALU.subtract)
                    then(dve.tensor_tensor(part[:, u, 2, :], q0, q1, ALU.add))
                    dve.tensor_scalar(mean[:, u, :], part[:, u, 0, :], 0.5, None, ALU.mult)
                    then(dve.scalar_tensor_tensor(out=part[:, u, 3, :], in0=part[:, u, 1, :], scalar=0.25,
                                                  in1=part[:, u, 1, :], op0=ALU.mult, op1=ALU.mult))
                    var = vary[:, u, :]
                    then(dve.scalar_tensor_tensor(out=var, in0=part[:, u, 2, :], scalar=1.0 / D,
                                                  in1=part[:, u, 3, :], op0=ALU.mult, op1=ALU.add))
                    dve.sem_inc(a_var, 1)
                    dve.wait_ge(a_root, b + 1)
                    then(dve.reciprocal(rs[:, u, 0, :], root[:, u, :]))
                    then(dve.scalar_tensor_tensor(out=rs[:, u, 1, :], in0=var, scalar=EPS,
                                                  in1=rs[:, u, 0, :], op0=ALU.add, op1=ALU.mult))
                    then(dve.tensor_tensor(rs[:, u, 2, :], rs[:, u, 1, :], rs[:, u, 0, :], ALU.mult))
                    then(dve.tensor_scalar(rs[:, u, 3, :], rs[:, u, 2, :], -0.5, 1.5, ALU.mult, ALU.add))
                    then(dve.tensor_tensor(rs[:, u, 1, :], rs[:, u, 3, :], rs[:, u, 0, :], ALU.mult))
                    dve.wait_ge(a_st[u], 16 * i + 16)
                    dve.wait_ge(a_tr, b + 1)
                    for a in range(T):
                        last = dve.tensor_scalar(xna[:, u, a, :], xa[:, u, a, :], mean[:, u, a:a + 1],
                                                 rs[:, u, 1, a:a + 1], ALU.subtract, ALU.mult)
                    then(last)
                    dve.sem_inc(a_free, 1)
                    dve.sem_inc(a_xn, 1)
                    dve.wait_ge(a_lg, b + 1)
                    dve.tensor_copy(logits[:, ds(b * T, T), :].rearrange("p a e -> p (a e)"),
                                    psum[:, 4 + u, 0:T * E]).then_inc(a_lc, 1)
                    assert k[0] == A_CH

        def a_scalar(act):
            act.sem_inc(a_st[0], 16)
            act.sem_inc(a_st[1], 16)
            with act.Fori(0, B // 2) as i:
                for u in range(2):
                    b = 2 * i + u
                    act.wait_ge(a_var, b + 1)
                    act.activation(root[:, u, :], vary[:, u, :], ACT.Sqrt, bias=eps[:, 0:1]).then_inc(a_root, 1)
                    a_store(act, i, u)
                    act.wait_ge(a_tr, b + 3)
                    for c in range(KD):
                        last = act.copy(xt_f[:, u, c, :], psum[:, 2 * u + c, :])
                    last.then_inc(a_xt, 1)
            for u in range(2):
                act.wait_ge(a_st[u], 16 * (B // 2) + 16)

        eps = sb("eps", [P, 1], F32)

        def a_tensor(pe):
            pe.sem_inc(a_tr, 2)
            with pe.Fori(0, B // 2) as i:
                for u in range(2):
                    b = 2 * i + u
                    pe.wait_ge(a_xn, b + 1)
                    for c in range(KD):
                        for a in range(T):
                            last = pe.transpose(psum[:, 2 * u + c, a * P:(a + 1) * P],
                                                xna[:, u, a, c * P:(c + 1) * P], ident[:, :])
                    last.then_inc(a_tr, 1)
                    pe.wait_ge(a_xt, b + 1)
                    for a in range(T):
                        for c in range(KD):
                            last = pe.matmul(psum[:, 4 + u, a * E:(a + 1) * E],
                                             xt_f[:, u, c, a * P:(a + 1) * P], gate_sb[:, c, :],
                                             start=(c == 0), stop=(c == KD - 1))
                    last.then_inc(a_lg, 1)

        plain_take = layout(plain_arena, PLAIN_WORDS)
        LANES = B
        lb = plain_take(NT, E)
        cmp = plain_take(NT, E, E)
        rank = plain_take(NT, E)
        top = plain_take(2, NT, E)
        member = sb("member", [P, NT * E], BF16)
        totals = plain_take(E, NT)
        upto = plain_take(E, NT)
        steps = plain_take(max(NBLK + 1, LANES))
        steps_i = sb("steps_i", [P, max(NBLK + 1, LANES)], I32)
        used = plain_take(E, LANES)
        nblk = plain_take(E)
        first = plain_take(E)
        base = plain_take(E)
        position = plain_take(NT, E)
        pick = plain_take(NT, E)
        slot_f = plain_take(NT, 2)
        chosen = plain_take(NT, 2)
        own_cmp = plain_take(NBLK + 1, E)
        own_f = plain_take(NBLK + 1)
        zero_row = plain_take(TE)
        r_iota = sem("r_iota")
        r_dve = sem("r_dve_chain")
        r_member = sem("r_member")
        r_pre = sem("r_prefix")
        r_chosen = sem("r_chosen")

        def r_gpsimd(pool):
            pool.iota(steps_i[:, :], [[1, max(NBLK + 1, LANES)]], base=0, channel_multiplier=0).then_inc(r_iota, 1)
            pool.memset(zero_row[:, :], 0.0).then_inc(r_iota, 1)

        def r_tensor(pe):
            pe.wait_ge(r_member, 1)
            pe.matmul(psum[:, 0, :], before[:, :], member[:, :], start=True, stop=True)
            pe.matmul(psum[:, 1, :], ones[:, :], member[:, :], start=True, stop=True).then_inc(r_pre, 1)

        def r_scalar(act):
            act.wait_ge(r_chosen, 1)
            act.activation(coef[:, :, :].rearrange("p t k -> p (t k)"),
                           chosen[:, :, :].rearrange("p t k -> p (t k)"), ACT.Sigmoid)

        def r_vector(dve):
            k = [0]

            def then(ins):
                k[0] += 1
                ins.then_inc(r_dve, 1)
                dve.wait_ge(r_dve, k[0])

            def over_experts(v):
                return v.unsqueeze(2).to_broadcast([P, NT, E, E])
            dve.wait_ge(r_iota, 2)
            then(dve.tensor_copy(steps[:, :], steps_i[:, :]))
            then(dve.tensor_tensor(lb[:, :, :], logits[:, :, :],
                                   beta_sb[:, :].unsqueeze(1).to_broadcast([P, NT, E]), ALU.add))
            theirs = lb[:, :, :].unsqueeze(2).to_broadcast([P, NT, E, E])
            mine = lb[:, :, :].unsqueeze(3).to_broadcast([P, NT, E, E])
            then(dve.tensor_tensor(cmp[:, :, :, :], theirs, mine, ALU.is_gt))
            then(dve.tensor_reduce(rank[:, :, :], cmp[:, :, :, :], AX.X, ALU.add))
            then(dve.tensor_tensor(cmp[:, :, :, :], theirs, mine, ALU.is_equal))
            then(dve.tensor_tensor(cmp[:, :, :, :].rearrange("p t a b -> p t (a b)"),
                                   cmp[:, :, :, :].rearrange("p t a b -> p t (a b)"),
                                   lower[:, :].unsqueeze(1).to_broadcast([P, NT, E * E]), ALU.mult))
            then(dve.tensor_reduce(pick[:, :, :], cmp[:, :, :, :], AX.X, ALU.add))
            then(dve.tensor_tensor(rank[:, :, :], rank[:, :, :], pick[:, :, :], ALU.add))
            for n in range(2):
                then(dve.tensor_scalar(top[:, n, :, :], rank[:, :, :], float(n), None, ALU.is_equal))
            flat = lambda v: v.rearrange("p t e -> p (t e)")
            k[0] += 1
            dve.tensor_scalar(member[:, :], flat(rank[:, :, :]), 1.0, None, ALU.is_le).then_inc(r_member, 1)
            k[0] -= 1
            for n in range(2):
                then(dve.tensor_tensor(pick[:, :, :], top[:, n, :, :], logits[:, :, :], ALU.mult))
                then(dve.tensor_reduce(chosen[:, :, n], pick[:, :, :], AX.X, ALU.add))
            dve.sem_inc(r_chosen, 1)
            dve.wait_ge(r_pre, 1)
            then(dve.tensor_copy(totals[:, :, :], psum[:, 1, :].rearrange("p (t e) -> p e t", e=E)))
            then(dve.tensor_tensor_scan(upto[:, :, :].rearrange("p e t -> p (e t)"),
                                        totals[:, :, :].rearrange("p e t -> p (e t)"),
                                        zero_row[:, :], 0.0, ALU.add, ALU.add))
            then(dve.tensor_tensor(totals[:, :, :], upto[:, :, :], totals[:, :, :], ALU.subtract))
            then(dve.tensor_tensor(nblk[:, :], upto[:, :, NT - 1], totals[:, :, 0], ALU.subtract))
            then(dve.tensor_scalar(own_f[:, 0:LANES], steps[:, 0:LANES], float(BLK), None, ALU.mult))
            then(dve.tensor_tensor(used[:, :, :], nblk[:, :].unsqueeze(2).to_broadcast([P, E, LANES]),
                                   own_f[:, 0:LANES].unsqueeze(1).to_broadcast([P, E, LANES]), ALU.is_gt))
            then(dve.tensor_reduce(nblk[:, :], used[:, :, :], AX.X, ALU.add))
            then(dve.tensor_tensor_scan(first[:, :], nblk[:, :], zero_row[:, 0:E], 0.0, ALU.add, ALU.add))
            then(dve.tensor_tensor(first[:, :], first[:, :], nblk[:, :], ALU.subtract))
            then(dve.scalar_tensor_tensor(out=base[:, :], in0=first[:, :], scalar=float(BLK),
                                          in1=totals[:, :, 0], op0=ALU.mult, op1=ALU.subtract))
            then(dve.tensor_tensor(position[:, :, :].rearrange("p t e -> p e t"), totals[:, :, :],
                                   base[:, :].unsqueeze(2).to_broadcast([P, E, NT]), ALU.add))
            then(dve.tensor_tensor(flat(position[:, :, :]), psum[:, 0, :], flat(position[:, :, :]), ALU.add))
            for n in range(2):
                then(dve.tensor_tensor(pick[:, :, :], top[:, n, :, :], position[:, :, :], ALU.mult))
                then(dve.tensor_reduce(slot_f[:, :, n], pick[:, :, :], AX.X, ALU.add))
            then(dve.tensor_copy(slot[:, :, :], slot_f[:, :, :]))
            then(dve.tensor_tensor(own_cmp[:, :, :], steps[:, 0:NBLK + 1].unsqueeze(2).to_broadcast([P, NBLK + 1, E]),
                                   first[:, :].unsqueeze(1).to_broadcast([P, NBLK + 1, E]), ALU.is_ge))
            then(dve.tensor_reduce(own_f[:, :], own_cmp[:, :, :], AX.X, ALU.add))
            then(dve.tensor_scalar(owner[:, :], own_f[:, :], -1.0, None, ALU.add))


        split_take = layout(split_arena, SPLIT_WORDS)
        split_take(2, G, D)
        split_take(2, 3, KD, D)
        q_xt = split_take(2, 2, KD, S)
        q_qk = split_take(2, 2, KD, S)
        q_v = split_take(2, T, H, 2, DH)
        plain_take = layout(plain_arena, PLAIN_WORDS)
        q_x = plain_take(2, T, D)
        q_vf = plain_take(T, D)
        q_vs = plain_take(2, 2 * D)
        q_idx = sb("q_idx", [P, 2, T, 2], U32)
        q_ld = [sem(f"q_rows_loaded{u}") for u in range(2)]
        q_xfree = sem("q_rows_free")
        q_tr = sem("q_transposed")
        q_xhi = sem("q_xt_hi")
        q_xlo = sem("q_xt_lo")
        q_mm = sem("q_projected")
        q_hi = sem("q_proj_hi")
        q_lo = sem("q_proj_lo")
        q_vb = sem("q_v_biased")
        q_vhi = sem("q_v_hi")
        q_vlo = sem("q_v_lo")
        q_vsum = sem("q_v_summed")
        q_vt = sem("q_v_total")
        q_vtc = sem("q_v_total_copied")
        q_st = sem("q_qk_stored")
        q_vst = [sem(f"q_v_stored{u}") for u in range(2)]
        q_ix = sem("q_index_staged")
        q_free = sem("q_index_slot_free")
        q_sc = [sem(f"q_scattered{u}") for u in range(2)]
        q_dve = sem("q_dve_chain")

        def q_sync(sp):
            def rows(b, u):
                sp.dma_start(q_x[:, u, :, :],
                             xn_d[ds(b * S, S), :].rearrange("(a p) d -> p a d", p=P)).then_inc(q_ld[u], 16)
            sp.sem_inc(q_free, 2)
            rows(0, 0)
            rows(1, 1)
            with sp.Fori(0, B // 2 - 1) as i:
                for u in range(2):
                    b = 2 * i + u
                    sp.wait_ge(q_tr, b + 1)
                    sp.wait_ge(q_sc[u], 16 * 2 * T * i + 16 * 2 * T)
                    sp.sem_inc(q_free, 1)
                    rows(b + 2, u)

        def q_gpsimd(pool):
            with pool.Fori(0, B // 2) as i:
                for u in range(2):
                    pool.wait_ge(q_ld[u], 16 * i + 16)
                    hold(pool, q_ix, 2 * i + u + 1)
                    for a in range(T):
                        for n in range(2):
                            pool.indirect_dma_start(
                                sorted_d, bass.IndirectOffsetOnAxis(q_idx[:, u, a, n:n + 1], 0),
                                q_x[:, u, a, :], None).then_inc(q_sc[u], 16)
            for u in range(2):
                pool.wait_ge(q_sc[u], 16 * 2 * T * (B // 2))

        def q_tensor(pe):
            pe.sem_inc(q_vt, 1)
            with pe.Fori(0, B // 2) as i:
                for u in range(2):
                    b = 2 * i + u
                    pe.wait_ge(q_ld[u], 16 * i + 16)
                    pe.wait_ge(q_xlo, b + 1)
                    if u == 0:
                        pe.wait_ge(q_vtc, 2 * i + 1)
                    for c in range(KD):
                        for a in range(T):
                            last = pe.transpose(psum[:, c, a * P:(a + 1) * P],
                                                q_x[:, u, a, c * P:(c + 1) * P], ident[:, :])
                    last.then_inc(q_tr, 1)
                    pe.wait_ge(q_xlo, b + 2)
                    for n in range(2):
                        for m in range(KD):
                            bank = 2 + 2 * n + m
                            pe.wait_ge(q_lo, 4 * b + 2 * n + m + 1)
                            split_products(pe, psum[:, bank, :], [
                                (lambda part, c=c: wqkv[:, part, n, c, m * P:(m + 1) * P],
                                 lambda part, c=c: q_xt[:, u, part, c, :]) for c in range(KD)]
                            ).then_inc(q_mm, 1)
                    for h in range(2):
                        pe.wait_ge(q_vb, 2 * b + h + 1)
                        for a in (2 * h, 2 * h + 1):
                            last = split_products(pe, psum[:, 6 + h, (a % 2) * D:(a % 2 + 1) * D], [
                                (lambda part, c=c: q_xt[:, u, part, c, a * P:(a + 1) * P],
                                 lambda part, c=c: wqkv[:, part, 2, c, :]) for c in range(KD)])
                        last.then_inc(q_mm, 1)
                    if u == 1:
                        for w in range(2):
                            pe.wait_ge(q_vsum, 2 * i + w + 1)
                            pe.wait_ge(q_vtc, 2 * i + w + 1)
                            for g in range(G):
                                last = pe.matmul(psum[:, 0, g:g + 1], q_vs[:, w, g * P:(g + 1) * P],
                                                 tiny[:, :], start=True, stop=True)
                            last.then_inc(q_vt, 1)

        def q_scalar(act):
            for u in range(2):
                act.sem_inc(q_vst[u], 16)
            act.sem_inc(q_st, 64)
            with act.Fori(0, B // 2) as i:
                for u in range(2):
                    b = 2 * i + u
                    act.wait_ge(q_tr, b + 1)
                    for c in range(KD):
                        act.copy(q_xt[:, u, 0, c, :], psum[:, c, :]).then_inc(q_xhi, 1)
                    act.wait_ge(q_st, 64 * b + 64)
                    for n in range(2):
                        for m in range(KD):
                            act.wait_ge(q_mm, 6 * b + 2 * n + m + 1)
                            act.activation(q_qk[:, n, 0, m, :], psum[:, 2 + 2 * n + m, :], ACT.Identity,
                                           bias=bqk[:, n, m:m + 1]).then_inc(q_hi, 1)
                    act.wait_ge(q_vst[u], 16 * i + 16)
                    for h in range(2):
                        act.wait_ge(q_vb, 2 * b + h + 3)
                        act.copy(q_v[:, u, 2 * h:2 * h + 2, :, 0, :],
                                 q_vf[:, 2 * h:2 * h + 2, :].rearrange("p a (h d) -> p a h d", h=H)
                                 ).then_inc(q_vhi, 1)
                    act.wait_ge(q_lo, 4 * b + 8)
                    for n, dram in enumerate((q_d, k_d)):
                        for part in range(2):
                            act.dma_start(dram[ds(b, 1), part, :, :].rearrange("o (m p) s -> p (o m) s", p=P),
                                          q_qk[:, n, part, :, :].bitcast(F32)).then_inc(q_st, 16)
                    act.wait_ge(q_vlo, 2 * b + 4)
                    act.dma_start(v_d[ds(b, 1), :, :, :].rearrange("o p a c -> p (o a) c"),
                                  q_v[:, u, :, :, :, :].rearrange("p a h s d -> p a (h s d)").bitcast(F32)
                                  ).then_inc(q_vst[u], 16)
            act.wait_ge(q_st, 64 * B + 64)
            for u in range(2):
                act.wait_ge(q_vst[u], 16 * (B // 2) + 16)

        Q_CH = 3

        def q_vector(dve):
            dve.sem_inc(q_xlo, 1)
            dve.sem_inc(q_lo, 4)
            dve.sem_inc(q_vb, 2)
            dve.sem_inc(q_vlo, 2)
            dve.sem_inc(q_vtc, 1)
            with dve.Fori(0, B // 2) as i:
                for u in range(2):
                    b = 2 * i + u
                    dve.wait_ge(q_free, b + 1)
                    dve.tensor_copy(q_idx[:, u, :, :], slot[:, ds(b * T, T), :]).then_inc(q_ix, 1)
                    for c in range(KD):
                        dve.wait_ge(q_xhi, 2 * b + c + 1)
                        last = dve.tensor_tensor(q_xt[:, u, 1, c, :], psum[:, c, :],
                                                 q_xt[:, u, 0, c, :].bitcast(F32), ALU.subtract)
                    last.then_inc(q_xlo, 1)
                    for n in range(2):
                        for m in range(KD):
                            dve.wait_ge(q_hi, 4 * b + 2 * n + m + 1)
                            dve.scalar_tensor_tensor(out=q_qk[:, n, 1, m, :], in0=psum[:, 2 + 2 * n + m, :],
                                                     scalar=bqk[:, n, m:m + 1],
                                                     in1=q_qk[:, n, 0, m, :].bitcast(F32),
                                                     op0=ALU.add, op1=ALU.subtract).then_inc(q_lo, 1)
                    for h in range(2):
                        dve.wait_ge(q_mm, 6 * b + 4 + h + 1)
                        dve.wait_ge(q_vlo, 2 * b + h + 1)
                        dve.tensor_tensor(q_vf[:, 2 * h:2 * h + 2, :],
                                          psum[:, 6 + h, :].rearrange("p (a d) -> p a d", a=2),
                                          bv_sb[:, :].unsqueeze(1).to_broadcast([P, 2, D]),
                                          ALU.add).then_inc(q_vb, 1)
                    for h in range(2):
                        dve.wait_ge(q_vhi, 2 * b + h + 1)
                        dve.tensor_tensor(q_v[:, u, 2 * h:2 * h + 2, :, 1, :],
                                          q_vf[:, 2 * h:2 * h + 2, :].rearrange("p a (h d) -> p a h d", h=H),
                                          q_v[:, u, 2 * h:2 * h + 2, :, 0, :].bitcast(F32),
                                          ALU.subtract).then_inc(q_vlo, 1)
                    vt = [q_v[:, u, a, :, :, :].rearrange("p h s d -> p (h s d)").bitcast(F32) for a in range(T)]
                    total = q_vs[:, u, :]
                    dve.wait_ge(q_vlo, 2 * b + 4)
                    dve.wait_ge(q_vt, 2 * i + 1)
                    dve.tensor_tensor(total, vt[0], vt[1], ALU.add).then_inc(q_dve, 1)
                    for a in (2, 3):
                        dve.wait_ge(q_dve, Q_CH * b + a - 1)
                        dve.tensor_tensor(total, total, vt[a], ALU.add).then_inc(q_dve, 1)
                    dve.wait_ge(q_dve, Q_CH * b + 3)
                    dve.sem_inc(q_vsum, 1)
                    if u == 1:
                        for w in range(2):
                            dve.wait_ge(q_vt, 2 * i + w + 2)
                            dve.tensor_copy(vtot[:, ds(2 * i + w, 1), :].rearrange("p o g -> p (o g)"),
                                            psum[:, 0, 0:G]).then_inc(q_vtc, 1)

        split_take = layout(split_arena, SPLIT_WORDS)
        split_take(2, G, D)
        c_w = split_take(2, 2, 3, 1024)
        c_xt = split_take(2, 2, KD, S)
        c_h = split_take(2, 2, MC, S)
        plain_take = layout(plain_arena, PLAIN_WORDS)
        c_raw = plain_take(3, 1024)
        c_x = plain_take(T, D)
        c_sg = plain_take(2, S)
        c_hf = plain_take(2, S)
        c_y = plain_take(2, T, D)
        c_ldw = [sem(f"c_raw_loaded{n}") for n in range(3)]
        c_ldx = sem("c_rows_loaded")
        c_tr = sem("c_transposed")
        c_xhi = sem("c_xt_hi")
        c_xlo = sem("c_xt_lo")
        c_whi = sem("c_w_hi")
        c_wlo = sem("c_w_lo")
        c_gu = sem("c_gate_up")
        c_silu = sem("c_silu")
        c_mul = sem("c_hidden")
        c_hhi = sem("c_hidden_hi")
        c_hlo = sem("c_hidden_lo")
        c_dn = sem("c_down")
        c_yc = sem("c_y_copied")
        c_st = [sem(f"c_y_stored{u}") for u in range(2)]

        def gate_up(pe, m, banks, w, xt):
            for n in range(2):
                last = split_products(pe, psum[:, banks[n], :], [
                    (lambda part, c=c: w(part, n, c * M + m * P, P), lambda part, c=c: xt(part, c))
                    for c in range(KD)])
            return last

        def down(pe, m, h, w, first):
            for a in range(T):
                for k, (p, q) in enumerate(PASSES):
                    last = pe.matmul(psum[:, 6 + a // 2, (a % 2) * D:(a % 2 + 1) * D],
                                     h(p, m, a), w(q, 2, m * D, D),
                                     start=(first and k == 0 and a % 2 == 0), stop=(m == MC - 1 and k == 2),
                                     skip_group_check=True)
            return last

        def c_sync(sp):
            def rows(blk):
                sp.dma_start(c_x[:, :, :], sorted_d[ds(blk * BLK, BLK), :].rearrange("(a p) d -> p a d", p=P)
                             ).then_inc(c_ldx, 16)

            def weights(e, k):
                for n, w in enumerate((gate_w, up_w, down_w)):
                    sp.wait_ge(c_wlo, k + n)
                    rowsz = w.shape[2]
                    sp.dma_start(c_raw[:, n, :].rearrange("p (k n) -> p k n", n=rowsz),
                                 w[ds(e, 1), :, :].rearrange("o (k p) n -> p (o k) n", p=P)).then_inc(c_ldw[n], 16)
            rows(0)
            e0 = sp.value_load(owner[0:1, 0:1], min_val=0, max_val=E - 1)
            weights(e0, 1)
            with sp.Fori(0, NBLK // 2) as i:
                for u in range(2):
                    blk = 2 * i + u
                    sp.wait_ge(c_tr, blk + 1)
                    rows(blk + 1)
                    e = sp.value_load(owner[0:1, ds(blk + 1, 1)], min_val=0, max_val=E - 1)
                    weights(e, 3 * blk + 4)

        def c_tensor(pe):
            def turn():
                for c in range(KD):
                    for a in range(T):
                        last = pe.transpose(psum[:, 4 + c, a * P:(a + 1) * P],
                                            c_x[:, a, c * P:(c + 1) * P], ident[:, :])
                last.then_inc(c_tr, 1)
            pe.wait_ge(c_ldx, 16)
            turn()
            with pe.Fori(0, NBLK // 2) as i:
                for u in range(2):
                    blk = 2 * i + u
                    w = lambda part, n, at, cols: c_w[:, u, part, n, at:at + cols]
                    pe.wait_ge(c_xlo, blk + 1)
                    pe.wait_ge(c_wlo, 3 * blk + 6)
                    for m in range(MC):
                        pe.wait_ge(c_mul, 4 * blk + m + 1)
                        gate_up(pe, m, (2 * (m % 2), 2 * (m % 2) + 1), w,
                                lambda part, c: c_xt[:, u, part, c, :]).then_inc(c_gu, 1)
                    pe.wait_ge(c_ldx, 16 * blk + 32)
                    turn()
                    pe.wait_ge(c_yc, 2 * blk + 2)
                    for m in range(MC):
                        pe.wait_ge(c_hlo, 4 * blk + m + 3)
                        last = down(pe, m, lambda part, m, a: c_h[:, u, part, m, a * P:(a + 1) * P], w, m == 0)
                    last.then_inc(c_dn, 1)

        def c_scalar(act):
            def w_hi(v, n, k):
                act.wait_ge(c_ldw[n], k)
                act.copy(c_w[:, v, 0, n, :], c_raw[:, n, :]).then_inc(c_whi, 1)

            def x_hi(v, k):
                act.wait_ge(c_tr, k)
                for c in range(KD):
                    act.copy(c_xt[:, v, 0, c, :], psum[:, 4 + c, :]).then_inc(c_xhi, 1)
            act.sem_inc(c_dn, 1)
            act.sem_inc(c_st[0], 16)
            act.sem_inc(c_st[1], 16)
            for n in range(3):
                w_hi(0, n, 16)
            x_hi(0, 1)
            with act.Fori(0, NBLK // 2) as i:
                for u in range(2):
                    blk = 2 * i + u

                    def hid_hi(m):
                        act.wait_ge(c_mul, 4 * blk + m + 3)
                        act.copy(c_h[:, u, 0, m, :], c_hf[:, m % 2, :]).then_inc(c_hhi, 1)
                    for m in range(MC):
                        act.wait_ge(c_gu, 4 * blk + m + 1)
                        act.activation(c_sg[:, m % 2, :], psum[:, 2 * (m % 2), :], ACT.Silu).then_inc(c_silu, 1)
                        if m == 0:
                            act.wait_ge(c_dn, blk + 1)
                        if m >= 1:
                            hid_hi(m - 1)
                        if m < 3:
                            w_hi(1 - u, m, 16 * blk + 32)
                    hid_hi(MC - 1)
                    x_hi(1 - u, blk + 2)
                    act.wait_ge(c_yc, 2 * blk + 4)
                    act.dma_start(y_d[ds(blk * BLK, BLK), :].rearrange("(a p) d -> p a d", p=P),
                                  c_y[:, u, :, :]).then_inc(c_st[u], 16)
            for u in range(2):
                act.wait_ge(c_st[u], 16 * (NBLK // 2) + 16)

        def c_vector(dve):
            def w_lo(v, n, k):
                dve.wait_ge(c_whi, k)
                dve.tensor_tensor(c_w[:, v, 1, n, :], c_raw[:, n, :], c_w[:, v, 0, n, :].bitcast(F32),
                                  ALU.subtract).then_inc(c_wlo, 1)

            def x_lo(v, k):
                for c in range(KD):
                    dve.wait_ge(c_xhi, k + c)
                    last = dve.tensor_tensor(c_xt[:, v, 1, c, :], psum[:, 4 + c, :],
                                             c_xt[:, v, 0, c, :].bitcast(F32), ALU.subtract)
                last.then_inc(c_xlo, 1)
            dve.sem_inc(c_wlo, 3)
            dve.sem_inc(c_mul, 2)
            dve.sem_inc(c_hlo, 2)
            dve.sem_inc(c_yc, 2)
            for n in range(3):
                w_lo(0, n, n + 1)
            x_lo(0, 1)
            with dve.Fori(0, NBLK // 2) as i:
                for u in range(2):
                    blk = 2 * i + u

                    def hid_lo(m):
                        dve.wait_ge(c_hhi, 4 * blk + m + 1)
                        dve.tensor_tensor(c_h[:, u, 1, m, :], c_hf[:, m % 2, :],
                                          c_h[:, u, 0, m, :].bitcast(F32), ALU.subtract).then_inc(c_hlo, 1)
                    for m in range(MC):
                        dve.wait_ge(c_silu, 4 * blk + m + 1)
                        dve.wait_ge(c_hlo, 4 * blk + m + 1)
                        dve.tensor_tensor(c_hf[:, m % 2, :], psum[:, 2 * (m % 2) + 1, :], c_sg[:, m % 2, :],
                                          ALU.mult).then_inc(c_mul, 1)
                        if m >= 1:
                            hid_lo(m - 1)
                        if m < 3:
                            w_lo(1 - u, m, 3 * blk + m + 4)
                    hid_lo(MC - 1)
                    x_lo(1 - u, 2 * blk + 3)
                    dve.wait_ge(c_dn, blk + 2)
                    dve.wait_ge(c_st[u], 16 * i + 16)
                    for h in range(2):
                        dve.tensor_copy(c_y[:, u, 2 * h:2 * h + 2, :].rearrange("p a d -> p (a d)"),
                                        psum[:, 6 + h, :]).then_inc(c_yc, 1)

        split_take = layout(split_arena, SPLIT_WORDS)
        split_take(2, G, D)
        b_w = split_take(2, 3, 1024)
        b_xt = split_take(2, KD, S)
        b_h = split_take(2, MC, S)
        b_q = split_take(2, 2, S)
        b_k = split_take(2, 2, 2, S)
        b_v = split_take(2, T, HG, P)
        b_pt = split_take(2, 2, 8, P)
        b_cx = split_take(2, G, S)
        plain_take = layout(plain_arena, PLAIN_WORDS)
        b_raw = plain_take(3, 1024)
        plain_take = layout(plain_arena, PLAIN_WORDS)
        b_x = plain_take(T, D)
        b_o = plain_take(T, D)
        b_y = plain_take(2, T, D)
        b_p = plain_take(4, T, 2 * P)
        b_sg = plain_take(2, S // 2)
        b_hf = plain_take(2, S)
        b_nm = sb("b_nm", [P, 4, T], F32)
        b_zs = sb("b_zs", [P, 4, T], F32)
        b_rz = sb("b_rz", [P, 4, T], F32)
        b_vt = sb("b_vt", [P, G], F32)
        b_cf = sb("b_cf", [P, T, 2], F32)
        b_ix = sb("b_ix", [P, T, 2], U32)
        b_ldw = sem("b_shared_loaded")
        b_whi = sem("b_shared_hi")
        b_wlo = sem("b_shared_lo")
        b_zeroed = sem("b_zeroed")
        b_ldx = sem("b_rows_loaded")
        b_ldo = sem("b_x_loaded")
        b_ldqk = [sem(f"b_qk_loaded{s}") for s in range(2)]
        b_ldv = [sem(f"b_v_loaded{s}") for s in range(2)]
        b_tr = sem("b_rows_transposed")
        b_xhi = sem("b_xt_hi")
        b_xlo = sem("b_xt_lo")
        b_gu = sem("b_gate_up")
        b_silu = sem("b_silu")
        b_mul = sem("b_hidden")
        b_hhi = sem("b_hidden_hi")
        b_hlo = sem("b_hidden_lo")
        b_s = sem("b_scores")
        b_mx = sem("b_masked_max")
        b_ex = sem("b_exp")
        b_rc = sem("b_reciprocal")
        b_nr = sem("b_normalised")
        b_pT = sem("b_probs_transposed")
        b_phi = sem("b_probs_hi")
        b_plo = sem("b_probs_lo")
        b_pv = sem("b_values_summed")
        b_chi = sem("b_context_hi")
        b_clo = sem("b_context_lo")
        b_yy = sem("b_rows_projected")
        b_stg = sem("b_staged")
        b_ga = sem("b_gathered")
        b_xb = sem("b_x_biased")
        b_f = sem("b_routed_added")
        b_fin = sem("b_result_half_ready")
        b_st = sem("b_result_stored")
        BLOCKS = [(0, 0), (1, 0), (1, 1), (2, 1), (2, 2), (3, 2), (3, 3)]

        def after(eng, semaphore, value):
            if not (isinstance(value, int) and value <= 0):
                eng.wait_ge(semaphore, value)

        def turns(eng, turn):
            turn(0, True, False)
            with eng.Fori(1, B) as b:
                turn(b, True, True)
            turn(B, False, True)

        def lagging(h, lag, new, old):
            n = h - lag
            return n if (new if n >= 0 else old) else None

        def b_sync(sp):
            for n, w in enumerate((sh_gate, sh_up, sh_down)):
                sp.dma_start(b_raw[:, n, :].rearrange("p (k n) -> p k n", n=w.shape[2]),
                             w.rearrange("o (k p) n -> p (o k) n", p=P)).then_inc(b_ldw, 16)
            sp.wait_ge(b_zeroed, 1)
            sp.wait_ge(b_wlo, 3)

            def load_qk(b, g):
                s = g % 2
                after(sp, b_s, 32 * b + 8 * g - 8)
                for c in range(4):
                    sp.dma_start(b_q[32 * c:32 * c + 32, s, :, :].bitcast(F32),
                                 q_d[ds(b, 1), c // 2, g * 64:(g + 1) * 64, :].rearrange(
                                     "o (h w) s -> w (o h) s", h=2)).then_inc(b_ldqk[s], 16)
                    for w in range(2):
                        sp.dma_start(b_k[32 * c + 16 * w:32 * c + 16 * w + 16, s, :, w, :].bitcast(F32),
                                     k_d[ds(b, 1), c % 2, g * 64:(g + 1) * 64, :].rearrange(
                                         "o (h w d) s -> w d (o h) s", h=2, w=2)[w]).then_inc(b_ldqk[s], 16)

            def load_v(b, g):
                s = g % 2
                after(sp, b_pv, 16 * b + 4 * g - 4)
                for c in range(4):
                    sp.dma_start(b_v[:, s, :, c, 32 * c:32 * c + 32].bitcast(F32),
                                 v_d[ds(b, 1), :, :, g * P + 32 * c:g * P + 32 * c + 32].rearrange(
                                     "o p a c -> p (o a) c")).then_inc(b_ldv[s], 16)

            def turn(b, new, old):
                if not new:
                    return
                after(sp, b_tr, b)
                sp.dma_start(b_x[:, :, :], xn_d[ds(b * S, S), :].rearrange("(a p) d -> p a d", p=P)
                             ).then_inc(b_ldx, 16)
                for g in range(G):
                    load_qk(b, g)
                    if g == G - 1:
                        after(sp, b_st, 16 * b)
                        sp.dma_start(b_o[:, :, :], xf[ds(b * S, S), :].rearrange("(a p) d -> p a d", p=P)
                                     ).then_inc(b_ldo, 16)
                    load_v(b, g)
            turns(sp, turn)

        def b_gpsimd(pool):
            pool.memset(b_k.bitcast(F32), 0.0)
            pool.memset(b_v.bitcast(F32), 0.0)
            pool.memset(b_pt[:, :, :, 0, :].bitcast(F32), 0.0).then_inc(b_zeroed, 1)
            pool.wait_ge(b_zeroed, 1)

            def turn(b, new, old):
                for h in range(H):
                    n = lagging(h, 2, new, old)
                    if n is not None:
                        hold(pool, b_rc, 16 * b + n + 1)
                        for i in range(T):
                            v = b_p[:, n % 4, i, 0:(P if i == 0 else 2 * P)]
                            last = pool.tensor_scalar(v, v, b_rz[:, n % 4, i:i + 1], 0.0, ALU.mult, ALU.add)
                        last.then_inc(b_nr, 1)
                    if old and h < T:
                        if h == 0:
                            pool.wait_ge(b_ldo, 16 * b)
                        pool.tensor_tensor(b_o[:, h, :], b_o[:, h, :], bo_sb[:, :], ALU.add).then_inc(b_xb, 1)
                    if new and h in (8, 9, 10, 11, 12, 13, 14, 15):
                        if h == 8:
                            hold(pool, b_stg, b + 1)
                        k = h - 8
                        pool.indirect_dma_start(b_y[:, k % 2, k // 2, :], None, y_d,
                                                bass.IndirectOffsetOnAxis(b_ix[:, k // 2, k % 2:k % 2 + 1], 0)
                                                ).then_inc(b_ga, 16)
            turns(pool, turn)

        def b_tensor(pe):
            def scores(b, h):
                g, r = h // HG, h % HG
                if r == 0:
                    pe.wait_ge(b_ldqk[g % 2], 192 * (2 * b + g // 2) + 192)
                for i in range(T):
                    if i % 2 == 0:
                        after(pe, b_mx, 32 * b + 2 * h + i // 2 - 1)
                    last = pe.matmul(psum[:, i // 2, (i % 2) * 2 * P:(i % 2 + 1) * 2 * P],
                                     b_q[:, g % 2, r // 2, i * P:(i + 1) * P],
                                     b_k[:, g % 2, r // 2, r % 2, max(i - 1, 0) * P:(max(i - 1, 0) + 2) * P],
                                     start=True, stop=True)
                    if i % 2 == 1:
                        last.then_inc(b_s, 1)

            def turn_probs(b, n):
                pe.wait_ge(b_nr, 16 * b + n + 1)
                for k, (i, j) in enumerate(BLOCKS):
                    if k % 4 == 0:
                        after(pe, b_plo, 32 * b + 2 * n - 1 + k // 4)
                    half = j if i == 0 else j - i + 1
                    last = pe.transpose(psum[:, 2 + k // 4, (k % 4) * P:(k % 4 + 1) * P],
                                        b_p[:, n % 4, i, half * P:(half + 1) * P], ident[:, :])
                    if k in (3, 6):
                        last.then_inc(b_pT, 1)

            def values(b, n):
                g, r = n % H // HG, n % HG
                if r == 0:
                    pe.wait_ge(b_ldv[g % 2], 64 * (2 * (b if n >= 0 else b - 1) + g // 2) + 64)
                    after(pe, b_clo, 4 * b + n // HG - 1)
                pe.wait_ge(b_plo, 32 * b + 2 * n + 2)
                for j in range(T):
                    at = j if j < T - 1 else T - 2
                    for part in range(2):
                        blocks = (b_pt[:, n % 2, part, 2 * j + 1:2 * j + 3, :] if j < T - 1
                                  else b_pt[:, n % 2, part, 0:8:7, :])
                        last = pe.matmul(psum[:, 4 + g % 2, at * P:(at + 2) * P],
                                         b_v[:, g % 2, j, r, :], blocks,
                                         start=(r == 0 and j == 0 and part == 0),
                                         stop=(r == HG - 1 and j == T - 1 and part == 1),
                                         skip_group_check=True)
                last.then_inc(b_pv, 1)

            def turn_rows(b):
                pe.wait_ge(b_ldx, 16 * b + 16)
                after(pe, b_fin, 2 * b)
                for c in range(KD):
                    for a in range(T):
                        last = pe.transpose(psum[:, 6 + c, a * P:(a + 1) * P],
                                            b_x[:, a, c * P:(c + 1) * P], ident[:, :])
                last.then_inc(b_tr, 1)

            def gate_up_half(b, k):
                m, half = k // 2, (k % 2) * (S // 2)
                if k < 2:
                    pe.wait_ge(b_xlo, 2 * b + 2)
                else:
                    pe.wait_ge(b_mul, 8 * b + k - 1)
                for n in range(2):
                    last = split_products(pe, psum[:, 6 + k % 2, n * (S // 2):(n + 1) * (S // 2)], [
                        (lambda part, c=c: b_w[:, part, n, c * M + m * P:c * M + (m + 1) * P],
                         lambda part, c=c: b_xt[:, part, c, half:half + S // 2]) for c in range(KD)])
                last.then_inc(b_gu, 1)

            def project_rows(b, a):
                if a == 0:
                    pe.wait_ge(b_hlo, 4 * b + 4)
                    pe.wait_ge(b_clo, 4 * b + 4)
                split_products(pe, psum[:, 7 - a // 2, (a % 2) * D:(a % 2 + 1) * D], [
                    (lambda part, m=m: b_h[:, part, m, a * P:(a + 1) * P],
                     lambda part, m=m: b_w[:, part, 2, m * D:(m + 1) * D]) for m in range(MC)] + [
                    (lambda part, g=g: b_cx[:, part, g, a * P:(a + 1) * P],
                     lambda part, g=g: wo[:, part, g, :]) for g in range(G)]).then_inc(b_yy, 1)

            def turn(b, new, old):
                for h in range(H):
                    if new:
                        scores(b, h)
                    n = lagging(h, 3, new, old)
                    if n is not None:
                        turn_probs(b, n)
                    n = lagging(h, 4, new, old)
                    if n is not None:
                        values(b, n)
                    if old and h < 2:
                        gate_up_half(b - 1, 6 + h)
                    if old and 5 <= h < 9:
                        project_rows(b - 1, h - 5)
                    if new and h == 9:
                        turn_rows(b)
                    if new and h >= 10:
                        gate_up_half(b, h - 10)
            pe.wait_ge(b_wlo, 3)
            turns(pe, turn)

        def b_scalar(act):
            act.wait_ge(b_ldw, 48)
            for n in range(3):
                act.copy(b_w[:, 0, n, :], b_raw[:, n, :]).then_inc(b_whi, 1)

            def exponentials(b, n, tiles):
                act.wait_ge(b_mx, 32 * b + 2 * n + 1 + tiles[0] // 2)
                for i in tiles:
                    v = b_p[:, n % 4, i, 0:(P if i == 0 else 2 * P)]
                    last = act.activation(v, v, ACT.Exp, bias=b_nm[:, n % 4, i:i + 1], scale=-1.0,
                                          accum_out=b_zs[:, n % 4, i:i + 1])
                if tiles[-1] == T - 1:
                    last.then_inc(b_ex, 1)

            def probs_hi(b, n, part):
                act.wait_ge(b_pT, 32 * b + 2 * n + 1 + part)
                after(act, b_pv, 16 * b + n - 1)
                blocks = slice(1, 5) if part == 0 else slice(5, 8)
                cols = 4 * P if part == 0 else 3 * P
                act.copy(b_pt[:, n % 2, 0, blocks, :].rearrange("p a b -> p (a b)"),
                         psum[:, 2 + part, 0:cols]).then_inc(b_phi, 1)

            def silu(b, k):
                act.wait_ge(b_gu, 8 * b + k + 1)
                after(act, b_mul, 8 * b + k - 1)
                act.activation(b_sg[:, k % 2, :], psum[:, 6 + k % 2, 0:S // 2], ACT.Silu).then_inc(b_silu, 1)

            def hidden_hi(b, m):
                act.wait_ge(b_mul, 8 * b + 2 * m + 2)
                act.copy(b_h[:, 0, m, :], b_hf[:, m % 2, :]).then_inc(b_hhi, 1)

            def context_hi(b, g):
                act.wait_ge(b_pv, 16 * b + 4 * g + 4)
                if g == 0:
                    act.wait_ge(b_stg, b + 1)
                    after(act, b_yy, 4 * b)
                act.activation(b_cx[:, 0, g, :], psum[:, 4 + g % 2, :], ACT.Identity,
                               bias=b_vt[:, g:g + 1]).then_inc(b_chi, 1)

            def turn(b, new, old):
                for h in range(H):
                    e, p = lagging(h, 1, new, old), lagging(h, 3, new, old)
                    for part in range(2):
                        if e is not None:
                            exponentials(b, e, (2 * part, 2 * part + 1))
                        if p is not None:
                            probs_hi(b, p, part)
                    if old and h < 2:
                        silu(b - 1, 6 + h)
                    if old and h in (0, 2):
                        hidden_hi(b - 1, 2 + h // 2)
                    if old and h in (0, 4):
                        context_hi(b - 1, 2 + h // 4)
                    if old and h == 9:
                        act.wait_ge(b_fin, 2 * b)
                        act.dma_start(of[ds((b - 1) * S, S), :].rearrange("(a p) d -> p a d", p=P),
                                      b_o[:, :, :]).then_inc(b_st, 16)
                    if new and h == 9:
                        act.wait_ge(b_tr, b + 1)
                        for c in range(KD):
                            act.copy(b_xt[:, 0, c, :], psum[:, 6 + c, :]).then_inc(b_xhi, 1)
                        context_hi(b, 0)
                    if new and h >= 10:
                        silu(b, h - 10)
                    if new and h in (12, 14):
                        hidden_hi(b, (h - 12) // 2)
                    if new and h == 12:
                        context_hi(b, 1)
            turns(act, turn)
            act.wait_ge(b_st, 16 * B)

        def b_vector(dve):
            for n in range(3):
                dve.wait_ge(b_whi, n + 1)
                dve.tensor_tensor(b_w[:, 1, n, :], b_raw[:, n, :], b_w[:, 0, n, :].bitcast(F32),
                                  ALU.subtract).then_inc(b_wlo, 1)

            def masked_max(b, h, part):
                hold(dve, b_s, 32 * b + 2 * h + 1 + part)
                for i in (2 * part, 2 * part + 1):
                    cols = P if i == 0 else 2 * P
                    at = (i % 2) * 2 * P
                    last = dve.tensor_tensor_reduce(
                        b_p[:, h % 4, i, 0:cols], psum[:, i // 2, at:at + cols],
                        mask[:, 2 * P - cols:2 * P], -SCALE, 3e38, ALU.add, ALU.min,
                        b_nm[:, h % 4, i:i + 1])
                last.then_inc(b_mx, 1)

            def probs_lo(b, n, part):
                dve.wait_ge(b_phi, 32 * b + 2 * n + 1 + part)
                blocks = slice(1, 5) if part == 0 else slice(5, 8)
                cols = 4 * P if part == 0 else 3 * P
                dve.tensor_tensor(b_pt[:, n % 2, 1, blocks, :].rearrange("p a b -> p (a b)"),
                                  psum[:, 2 + part, 0:cols],
                                  b_pt[:, n % 2, 0, blocks, :].rearrange("p a b -> p (a b)").bitcast(F32),
                                  ALU.subtract).then_inc(b_plo, 1)

            def hidden(b, k):
                m, half = k // 2, (k % 2) * (S // 2)
                dve.wait_ge(b_silu, 8 * b + k + 1)
                after(dve, b_hlo, 4 * b + m - 1)
                dve.tensor_tensor(b_hf[:, m % 2, half:half + S // 2], psum[:, 6 + k % 2, S // 2:S],
                                  b_sg[:, k % 2, :], ALU.mult).then_inc(b_mul, 1)

            def hidden_lo(b, m):
                dve.wait_ge(b_hhi, 4 * b + m + 1)
                dve.tensor_tensor(b_h[:, 1, m, :], b_hf[:, m % 2, :], b_h[:, 0, m, :].bitcast(F32),
                                  ALU.subtract).then_inc(b_hlo, 1)

            def context_lo(b, g):
                dve.wait_ge(b_chi, 4 * b + g + 1)
                dve.scalar_tensor_tensor(out=b_cx[:, 1, g, :], in0=psum[:, 4 + g % 2, :],
                                         scalar=b_vt[:, g:g + 1], in1=b_cx[:, 0, g, :].bitcast(F32),
                                         op0=ALU.add, op1=ALU.subtract).then_inc(b_clo, 1)

            def add_routed(b, n):
                dve.wait_ge(b_ga, 16 * 2 * T * b + 16 * 2 * T)
                if n == 0:
                    dve.wait_ge(b_xb, T * b + T)
                else:
                    dve.wait_ge(b_f, 2 * T * b + T)
                for a in range(T):
                    dve.scalar_tensor_tensor(out=b_o[:, a, :], in0=b_y[:, n, a, :],
                                             scalar=b_cf[:, a, n:n + 1], in1=b_o[:, a, :],
                                             op0=ALU.mult, op1=ALU.add).then_inc(b_f, 1)

            def finish(b, half):
                dve.wait_ge(b_yy, 4 * b + 2 * half + 2)
                dve.wait_ge(b_f, 2 * T * b + 2 * T)
                v = b_o[:, 2 * half:2 * half + 2, :].rearrange("p a d -> p (a d)")
                dve.tensor_tensor(v, psum[:, 7 - half, :], v, ALU.add).then_inc(b_fin, 1)

            def turn(b, new, old):
                for h in range(H):
                    p, r = lagging(h, 3, new, old), lagging(h, 1, new, old)
                    if old and h == 9:
                        finish(b - 1, 1)
                    for part in range(2):
                        if new:
                            masked_max(b, h, part)
                        if p is not None:
                            probs_lo(b, p, part)
                    if r is not None:
                        dve.wait_ge(b_ex, 16 * b + r + 1)
                        dve.reciprocal(b_rz[:, r % 4, :], b_zs[:, r % 4, :]).then_inc(b_rc, 1)
                    if old and h < 2:
                        hidden(b - 1, 6 + h)
                    if old and h in (0, 2):
                        hidden_lo(b - 1, 2 + h // 2)
                    if old and h in (0, 4):
                        context_lo(b - 1, 2 + h // 4)
                    if old and h in (4, 6):
                        add_routed(b - 1, (h - 4) // 2)
                    if old and h == 7:
                        finish(b - 1, 0)
                    if new and h == 7:
                        dve.tensor_copy(b_ix[:, :, :], slot[:, ds(b * T, T), :])
                        dve.tensor_copy(b_cf[:, :, :], coef[:, ds(b * T, T), :])
                        after(dve, b_f, 2 * T * b)
                        dve.tensor_copy(b_vt[:, :], vtot[:, ds(b, 1), :].rearrange("p o g -> p (o g)")
                                        ).then_inc(b_stg, 1)
                    if new and h == 9:
                        for c in range(KD):
                            dve.wait_ge(b_xhi, 2 * b + c + 1)
                            dve.tensor_tensor(b_xt[:, 1, c, :], psum[:, 6 + c, :],
                                              b_xt[:, 0, c, :].bitcast(F32), ALU.subtract).then_inc(b_xlo, 1)
                        context_lo(b, 0)
                    if new and h >= 10:
                        hidden(b, h - 10)
                    if new and h in (12, 14):
                        hidden_lo(b, (h - 12) // 2)
                    if new and h == 12:
                        context_lo(b, 1)
            turns(dve, turn)

        @block.sync
        def _(sp):
            start_sync(sp)
            wall(sp, 1)
            a_sync(sp)
            wall(sp, 2)
            wall(sp, 3)
            q_sync(sp)
            wall(sp, 4)
            c_sync(sp)
            wall(sp, 5)
            b_sync(sp)

        @block.gpsimd
        def _(pool):
            start_gpsimd(pool)
            wall(pool, 1)
            wall(pool, 2)
            r_gpsimd(pool)
            pool.wait_ge(s_zero, N_ZERO)
            wall(pool, 3)
            q_gpsimd(pool)
            wall(pool, 4)
            wall(pool, 5)
            b_gpsimd(pool)

        @block.scalar
        def _(act):
            start_scalar(act)
            wall(act, 1)
            a_scalar(act)
            wall(act, 2)
            r_scalar(act)
            wall(act, 3)
            q_scalar(act)
            wall(act, 4)
            c_scalar(act)
            wall(act, 5)
            b_scalar(act)

        @block.vector
        def _(dve):
            start_vector(dve)
            wall(dve, 1)
            a_vector(dve)
            wall(dve, 2)
            r_vector(dve)
            wall(dve, 3)
            q_vector(dve)
            wall(dve, 4)
            c_vector(dve)
            wall(dve, 5)
            b_vector(dve)

        @block.tensor
        def _(pe):
            wall(pe, 1)
            a_tensor(pe)
            wall(pe, 2)
            r_tensor(pe)
            wall(pe, 3)
            q_tensor(pe)
            wall(pe, 4)
            c_tensor(pe)
            wall(pe, 5)
            b_tensor(pe)


def kernel(**inputs):
    import numpy as _np
    import concourse.bacc as _bacc
    from concourse.bass_utils import run_bass_kernel_spmd as _run

    pre = {n: _np.asarray(a) for n, a in inputs.items()}
    laid = {
        "x": pre["L0_attn_x"],
        "wq_t": pre["L0_attn_Wq"].T, "wk_t": pre["L0_attn_Wk"].T,
        "wv_t": pre["L0_attn_Wv"].T, "wo_t": pre["L0_attn_Wo"].T,
        "bq": pre["L0_attn_bq"], "bk": pre["L0_attn_bk"], "bv": pre["L0_attn_bv"], "bo": pre["L0_attn_bo"],
        "gate_t": pre["L0_ffn_gate_w"].T, "beta": pre["L0_ffn_beta"],
        "gate_w": pre["L0_ffn_gate_proj_w"], "up_w": pre["L0_ffn_up_proj_w"],
        "down_w": pre["L0_ffn_down_proj_w"],
        "sh_gate": pre["L0_ffn_shared_gate_w"], "sh_up": pre["L0_ffn_shared_up_w"],
        "sh_down": pre["L0_ffn_shared_down_w"],
    }
    nc = _bacc.Bacc("TRN2", target_bir_lowering=False, num_devices=1)
    arrays, args = {}, []
    for name, a in laid.items():
        a = _np.ascontiguousarray(a)
        arrays[f"in_{name}"] = a
        args.append(nc.dram_tensor(f"in_{name}", a.shape, mybir.dt.from_np(a.dtype), kind="ExternalInput").ap())
    args.append(nc.dram_tensor("out_0", pre["L0_attn_x"].shape, F32, kind="ExternalOutput").ap())
    moe_attention_layer(nc, *args)
    r = _run(nc, [arrays], core_ids=[0])
    return r.results[0]["out_0"]
```

```python
from contextlib import ExitStack

import concourse.bass as bass
from concourse import mybir

F32 = mybir.dt.float32
F32R = mybir.dt.float32r
BF16 = mybir.dt.bfloat16
U32 = mybir.dt.uint32
I32 = mybir.dt.int32
ALU = mybir.AluOpType
ACT = mybir.ActivationFunctionType
AX = mybir.AxisListType
ds = bass.ds

P = 128
PLAIN_WORDS = 12800
SPLIT_WORDS = 33792
EPS = 1e-5
ATTN_EPS = 1e-9
MASKED = -10000.0


def moe_attention_layer(nc, x, wq_t, wk_t, wv_t, wo_t, bq, bk, bv, bo, gate_t, beta,
                        gate_w, up_w, down_w, sh_gate, sh_up, sh_down, out):
    B, S, D = x.shape
    E = gate_w.shape[0]
    M = gate_w.shape[2]
    KD = D // P
    MC = M // P
    T = S // P
    NT = B * T
    H = 16
    DH = D // H
    SCALE = 1.0 / float(DH) ** 0.5
    HG = 4
    G = H // HG
    BLK = S
    NBLK = (2 * B * S + E * (BLK - 1)) // BLK
    ROWS = NBLK * BLK
    TE = NT * E

    xf = x.rearrange("b s d -> (b s) d")
    of = out.rearrange("b s d -> (b s) d")
    xn_d = nc.dram_tensor("xn_d", (B * S, D), F32).ap()
    sorted_d = nc.dram_tensor("sorted_d", (ROWS, D), F32).ap()
    y_d = nc.dram_tensor("y_d", (ROWS, D), F32).ap()
    q_d = nc.dram_tensor("q_d", (B, 2, D, S), F32).ap()
    k_d = nc.dram_tensor("k_d", (B, 2, D, S), F32).ap()
    v_d = nc.dram_tensor("v_d", (B, P, T, 2 * D), F32).ap()

    ctx = ExitStack()
    with ctx:
        def sb(name, shape, dt):
            return ctx.enter_context(nc.sbuf_tensor(name, shape, dt))

        def sem(name):
            return ctx.enter_context(nc.semaphore(name))

        psum = ctx.enter_context(nc.psum_tensor("psum", [P, 8, 512], F32))

        plain_arena = sb("plain_arena", [P, PLAIN_WORDS], F32)
        split_arena = sb("split_arena", [P, SPLIT_WORDS], F32R)

        def layout(arena, words):
            at = [0]

            def take(*shape):
                n = 1
                for m in shape:
                    n *= m
                assert at[0] + n <= words, (at[0] + n, words)
                view = arena[:, at[0]:at[0] + n]
                at[0] += n
                names = "abcde"[:len(shape)]
                sizes = {c: m for c, m in zip(names, shape)}
                return view.rearrange(f"p ({' '.join(names)}) -> p {' '.join(names)}", **sizes)
            return take

        split_take = layout(split_arena, SPLIT_WORDS)
        ident = sb("ident", [P, P], F32)
        before = sb("before", [P, P], BF16)
        ones = sb("ones", [P, P], BF16)
        half_tiny = sb("half_tiny", [P, 1], F32)
        mask = sb("mask", [P, 2 * P], F32)
        wo = split_take(2, G, D)
        gate_sb = sb("gate_sb", [P, KD, E], F32)
        beta_sb = sb("beta_sb", [P, E], F32)
        bqk = sb("bqk", [P, 2, KD], F32)
        bv_sb = sb("bv_sb", [P, D], F32)
        bo_sb = sb("bo_sb", [P, D], F32)
        logits = sb("logits", [P, NT, E], F32)
        slot = sb("slot", [P, NT, 2], U32)
        coef = sb("coef", [P, NT, 2], F32)
        owner = sb("owner", [P, NBLK], I32)
        final = sb("final", [P, E], I32)
        vtot = sb("vtot", [P, B, G], F32)

        s_w = sem("weights_loaded")
        s_const = sem("constants_ready")
        s_bar = sem("phase_barrier")

        block = ctx.enter_context(nc.Block())
        s_passed = sem("waits_passed")

        def hold(eng, semaphore, value):
            eng.wait_ge(semaphore, value)
            eng.sem_inc(s_passed, 1)

        def after(eng, semaphore, value):
            if not (isinstance(value, int) and value <= 0):
                eng.wait_ge(semaphore, value)

        def is_first(b):
            return isinstance(b, int) and b == 0

        def wall(eng, n):
            eng.drain().then_inc(s_bar, 1)
            eng.wait_ge(s_bar, 5 * n)

        PASSES = ((0, 0), (0, 1), (1, 0))

        def split_products(pe, out, chunks, begins=True, ends=True):
            for c, (lhs_t, rhs) in enumerate(chunks):
                for k, (p, q) in enumerate(PASSES):
                    last = pe.matmul(out, lhs_t(p), rhs(q), start=(begins and c == 0 and k == 0),
                                     stop=(ends and c == len(chunks) - 1 and k == 2),
                                     skip_group_check=not (begins and ends))
            return last

        ROW_SLOTS = 4
        plain_take = layout(plain_arena, PLAIN_WORDS)
        wqkv_raw = plain_take(3, KD * D)
        wo_raw = plain_take(G, D)
        wqkv = split_take(2, 3, KD, D)
        zero = split_take(BLK * D // P)
        s_gate = sem("gate_loaded")
        s_whi = sem("weights_hi")
        s_zbuf = sem("zero_buffer_ready")
        s_zero = sem("padding_rows_zeroed")
        FULL = 2 * B * S // BLK
        N_ZERO = 16 * (NBLK - FULL)
        a_ld = [sem(f"a_x_loaded{u}") for u in range(ROW_SLOTS)]

        def start_sync(sp):
            sp.dma_start(gate_sb[:, :, :], gate_t.rearrange("(k p) e -> p k e", p=P)).then_inc(s_gate, 16)
            for u in range(ROW_SLOTS):
                a_load(sp, u, u)
            for n, w in enumerate((wq_t, wk_t, wv_t)):
                sp.dma_start(wqkv_raw[:, n, :].rearrange("p (k n) -> p k n", k=KD),
                             w.rearrange("(k p) n -> p k n", p=P)).then_inc(s_w, 16)
            for r in range(HG):
                for half in range(2):
                    sp.dma_start(wo_raw[32 * r + 16 * half:32 * r + 16 * half + 16, :, :],
                                 wo_t.rearrange("(g r d) n -> r d g n", r=HG, d=DH)[r]).then_inc(s_w, 16)
            sp.dma_start(beta_sb[:, :], beta.partition_broadcast(P)).then_inc(s_w, 16)
            for n, b in enumerate((bq, bk)):
                sp.dma_start(bqk[:, n, :], b.rearrange("(k p) -> p k", p=P),
                             allow_slow_non_contiguous=True).then_inc(s_w, 16)
            sp.dma_start(bv_sb[:, :], bv.partition_broadcast(P)).then_inc(s_w, 16)
            sp.dma_start(bo_sb[:, :], bo.partition_broadcast(P)).then_inc(s_w, 16)
            sp.wait_ge(s_zbuf, 1)
            for blk in range(FULL, NBLK):
                zero_block(sp, blk)

        N_W = 16 * (3 + 2 * HG + 5)

        def zero_block(sp, blk):
            sp.dma_start(sorted_d[ds(blk * BLK, BLK), :].rearrange("(p a) d -> p (a d)", p=P),
                         zero[:, :].bitcast(F32)).then_inc(s_zero, 16)

        def split_weights_scalar(act):
            act.wait_ge(s_w, N_W)
            for n in range(3):
                act.copy(wqkv[:, 0, n, :, :].rearrange("p k n -> p (k n)"), wqkv_raw[:, n, :]).then_inc(s_whi, 1)
            act.copy(wo[:, 0, :, :], wo_raw[:, :, :]).then_inc(s_whi, 1)

        def split_weights_vector(dve):
            for n in range(3):
                dve.wait_ge(s_whi, n + 1)
                dve.tensor_tensor(wqkv[:, 1, n, :, :].rearrange("p k n -> p (k n)"), wqkv_raw[:, n, :],
                                  wqkv[:, 0, n, :, :].rearrange("p k n -> p (k n)").bitcast(F32),
                                  ALU.subtract)
            dve.wait_ge(s_whi, 4)
            dve.tensor_tensor(wo[:, 1, :, :], wo_raw[:, :, :], wo[:, 0, :, :].bitcast(F32), ALU.subtract)

        s_pz = sem("pool_zeroed")

        def start_gpsimd(pool):
            pool.memset(eps[:, :], EPS).then_inc(s_const, 1)
            pool.memset(ident[:, :], 0.0).then_inc(s_pz, 1)
            pool.memset(zero.bitcast(F32), 0.0).then_inc(s_zbuf, 1)
            pool.wait_ge(s_pz, 1)
            pool.affine_select(out=ident[:, :], in_=ident[:, :], compare_op=ALU.not_equal, fill=1.0,
                               base=0, pattern=[[-1, P]], channel_multiplier=1).then_inc(s_const, 1)

        def constants_gpsimd(pool):
            pool.memset(before[:, :], 1.0).then_inc(s_pz, 1)
            pool.memset(mask[:, :], 0.0).then_inc(s_pz, 1)
            pool.memset(ones[:, :], 1.0).then_inc(s_const, 1)
            pool.memset(half_tiny[:, :], ATTN_EPS / 2).then_inc(s_const, 1)
            pool.wait_ge(s_pz, 3)
            pool.affine_select(out=before[:, :], in_=before[:, :], compare_op=ALU.is_gt, fill=0.0,
                               base=0, pattern=[[1, P]], channel_multiplier=-1).then_inc(s_const, 1)
            pool.affine_select(out=mask[:, 0:P], in_=mask[:, 0:P], compare_op=ALU.is_ge,
                               fill=MASKED / SCALE, base=0, pattern=[[1, P]],
                               channel_multiplier=-1).then_inc(s_const, 1)
            pool.affine_select(out=mask[:, P:2 * P], in_=mask[:, P:2 * P], compare_op=ALU.is_ge,
                               fill=MASKED / SCALE, base=0, pattern=[[-1, P]],
                               channel_multiplier=1).then_inc(s_const, 1)

        a_x = plain_take(ROW_SLOTS, T, D)
        a_xn = plain_take(2, T, D)
        a_xt = plain_take(2, KD, S)
        stats = sb("stats", [P, 2, T, 6], F32)
        part = sb("part", [P, 10, T], F32)
        eps = sb("eps", [P, 1], F32)
        mean = sb("mean", [P, T], F32)
        rstd = sb("rstd", [P, T], F32)
        a_stat = sem("a_statistics")
        a_dve = sem("a_dve_chain")
        a_var = sem("a_variance")
        a_root = sem("a_root")
        a_xnr = sem("a_xn_ready")
        a_st = [sem(f"a_xn_stored{v}") for v in range(2)]
        a_tr = sem("a_transposed")
        a_cp = sem("a_xt_copied")
        a_lg = sem("a_logits_done")
        a_lc = sem("a_logits_copied")

        def over_rows(eng, step):
            step(0, 0, 0, True)
            with eng.Fori(0, B // ROW_SLOTS - 1) as i:
                for j in range(1, ROW_SLOTS + 1):
                    step(ROW_SLOTS * i + j, j % ROW_SLOTS, i + j // ROW_SLOTS, True)
            for u in range(1, ROW_SLOTS):
                step(B - ROW_SLOTS + u, u, B // ROW_SLOTS - 1, u < ROW_SLOTS - 1)

        def a_load(sp, b, u):
            sp.dma_start(a_x[:, u, :, :],
                         xf[ds(b * S, S), :].rearrange("(a p) d -> p a d", p=P)).then_inc(a_ld[u], 16)

        def a_sync(sp):
            with sp.Fori(0, B // ROW_SLOTS - 1) as i:
                for u in range(ROW_SLOTS):
                    sp.wait_ge(a_xnr, ROW_SLOTS * i + u + 1)
                    a_load(sp, ROW_SLOTS * i + u + ROW_SLOTS, u)

        A_CH = 8

        def a_vector(dve):
            def stat(u, a):
                return dve.bn_stats(stats[:, u % 2, a, :], a_x[:, u, a, :])

            def step(b, u, n, more):
                k = [0]
                v = u % 2
                dve.wait_ge(a_stat, b + 1)
                if more:
                    dve.wait_ge(a_ld[(u + 1) % ROW_SLOTS], 16 * (n + (u + 1) // ROW_SLOTS) + 16)

                def then(ins):
                    k[0] += 1
                    ins.then_inc(a_dve, 1)
                    if more and k[0] in (1, 2, 4):
                        stat((u + 1) % ROW_SLOTS, k[0] - 1)
                        if k[0] == 4:
                            dve.sem_inc(a_stat, 1)
                    dve.wait_ge(a_dve, A_CH * b + k[0])
                m0, q0, m1, q1 = (stats[:, v, :, c] for c in (1, 2, 4, 5))
                dve.tensor_tensor(part[:, 0, :], m0, m1, ALU.add)
                dve.tensor_tensor(part[:, 1, :], m0, m1, ALU.subtract)
                then(dve.tensor_tensor(part[:, 2, :], q0, q1, ALU.add))
                if not is_first(b):
                    dve.wait_ge(a_xnr, b)
                dve.tensor_scalar(mean[:, :], part[:, 0, :], 0.5, None, ALU.mult)
                then(dve.scalar_tensor_tensor(out=part[:, 3, :], in0=part[:, 1, :], scalar=0.25,
                                              in1=part[:, 1, :], op0=ALU.mult, op1=ALU.mult))
                var = part[:, 4, :]
                then(dve.scalar_tensor_tensor(out=var, in0=part[:, 2, :], scalar=1.0 / D,
                                              in1=part[:, 3, :], op0=ALU.mult, op1=ALU.add))
                raw = part[:, 5, :]
                dve.sem_inc(a_var, 1)
                if more:
                    stat((u + 1) % ROW_SLOTS, 2)
                dve.wait_ge(a_root, b + 1)
                then(dve.reciprocal(raw, part[:, 9, :]))
                then(dve.scalar_tensor_tensor(out=part[:, 6, :], in0=var, scalar=EPS,
                                              in1=raw, op0=ALU.add, op1=ALU.mult))
                then(dve.tensor_tensor(part[:, 7, :], part[:, 6, :], raw, ALU.mult))
                then(dve.tensor_scalar(part[:, 8, :], part[:, 7, :], -0.5, 1.5, ALU.mult, ALU.add))
                then(dve.tensor_tensor(rstd[:, :], part[:, 8, :], raw, ALU.mult))
                assert k[0] == A_CH
                dve.wait_ge(a_st[v], 16 * (2 * n + u // 2) + 16)
                dve.wait_ge(a_tr, b + 1)
                for a in range(T):
                    last = dve.tensor_scalar(a_xn[:, v, a, :], a_x[:, u, a, :], mean[:, a:a + 1],
                                             rstd[:, a:a + 1], ALU.subtract, ALU.mult)
                last.then_inc(a_xnr, 1)
            dve.wait_ge(a_ld[0], 16)
            for a in range(T):
                last = stat(0, a)
            last.then_inc(a_stat, 1)
            over_rows(dve, step)

        def a_scalar(act):
            def copy_logits(b, v):
                act.wait_ge(a_lg, b + 3)
                act.copy(logits[:, ds(b * T, T), :].rearrange("p a e -> p (a e)"),
                         psum[:, 4 + v, 0:T * E]).then_inc(a_lc, 1)

            def root(b):
                act.wait_ge(a_var, b + 1)
                act.activation(part[:, 9, :], part[:, 4, :], ACT.Sqrt, bias=eps[:, 0:1]).then_inc(a_root, 1)

            def step(b, u, n, more):
                v = u % 2
                if more:
                    root(b + 1)
                act.wait_ge(a_xnr, b + 1)
                act.wait_ge(a_st[v], 16 * (2 * n + u // 2) + 16)
                act.dma_start(xn_d[ds(b * S, S), :].rearrange("(a p) d -> p a d", p=P),
                              a_xn[:, v, :, :]).then_inc(a_st[v], 16)
                act.wait_ge(a_tr, b + 3)
                act.wait_ge(a_lg, b + 1)
                for c in range(KD):
                    last = act.copy(a_xt[:, v, c, :], psum[:, 2 * v + c, :])
                last.then_inc(a_cp, 1)
                if not is_first(b):
                    copy_logits(b - 1, 1 - v)
            act.sem_inc(a_lg, 2)
            for v in range(2):
                act.sem_inc(a_st[v], 16)
            act.wait_ge(s_const, 1)
            root(0)
            over_rows(act, step)
            copy_logits(B - 1, 1)
            for v in range(2):
                act.wait_ge(a_st[v], 16 * (B // 2) + 16)

        def a_tensor(pe):
            def turn_rows(b, v):
                pe.wait_ge(a_xnr, b + 1)
                pe.wait_ge(a_cp, b + 1)
                for c in range(KD):
                    for a in range(T):
                        last = pe.transpose(psum[:, 2 * v + c, a * P:(a + 1) * P],
                                            a_xn[:, v, a, c * P:(c + 1) * P], ident[:, :])
                last.then_inc(a_tr, 1)

            def step(b, u, n, more):
                v = u % 2
                if more:
                    turn_rows(b + 1, 1 - v)
                pe.wait_ge(a_lc, b + 1)
                pe.wait_ge(a_cp, b + 3)
                for a in range(T):
                    for c in range(KD):
                        last = pe.matmul(psum[:, 4 + v, a * E:(a + 1) * E], a_xt[:, v, c, a * P:(a + 1) * P],
                                         gate_sb[:, c, :], start=(c == 0), stop=(c == KD - 1))
                last.then_inc(a_lg, 1)
            pe.sem_inc(a_tr, 2)
            pe.sem_inc(a_cp, 2)
            pe.sem_inc(a_lc, 2)
            pe.wait_ge(s_const, 2)
            pe.wait_ge(s_gate, 16)
            turn_rows(0, 0)
            over_rows(pe, step)

        plain_take = layout(plain_arena, PLAIN_WORDS)
        LANES = B
        lb = plain_take(NT, E)
        best = plain_take(NT)
        earlier = plain_take(E)
        top = plain_take(2, NT, E)
        member = sb("member", [P, NT * E], BF16)
        totals = plain_take(E, NT)
        upto = plain_take(E, NT)
        steps = plain_take(max(NBLK, LANES))
        steps_i = sb("steps_i", [P, max(NBLK, LANES)], I32)
        used = plain_take(E, LANES)
        nblk = plain_take(E)
        first = plain_take(E)
        base = plain_take(E)
        position = plain_take(NT, E)
        pick = plain_take(NT, E)
        slot_f = plain_take(NT, 2)
        chosen = plain_take(NT, 2)
        own_cmp = plain_take(NBLK, E)
        own_f = plain_take(NBLK)
        zero_row = plain_take(TE)
        r_iota = sem("r_iota")
        r_dve = sem("r_dve_chain")
        r_member = sem("r_member")
        r_pre = sem("r_prefix")
        r_chosen = sem("r_chosen")
        r_final = sem("r_last_blocks_known")

        def r_sync(sp):
            sp.wait_ge(s_zero, N_ZERO)
            sp.wait_ge(r_final, 1)
            for e in range(E):
                zero_block(sp, sp.value_load(final[0:1, e:e + 1], min_val=0, max_val=NBLK - 1))

        def r_gpsimd(pool):
            pool.iota(steps_i[:, :], [[1, max(NBLK, LANES)]], base=0, channel_multiplier=0).then_inc(r_iota, 1)
            pool.memset(zero_row[:, :], 0.0).then_inc(r_iota, 1)

        def r_tensor(pe):
            pe.wait_ge(r_member, 1)
            pe.matmul(psum[:, 0, :], before[:, :], member[:, :], start=True, stop=True)
            pe.matmul(psum[:, 1, :], ones[:, :], member[:, :], start=True, stop=True).then_inc(r_pre, 1)

        def r_scalar(act):
            act.wait_ge(r_chosen, 1)
            act.activation(coef[:, :, :].rearrange("p t k -> p (t k)"),
                           chosen[:, :, :].rearrange("p t k -> p (t k)"), ACT.Sigmoid)

        def r_vector(dve):
            k = [0]

            def then(ins):
                k[0] += 1
                ins.then_inc(r_dve, 1)
                dve.wait_ge(r_dve, k[0])

            dve.wait_ge(r_iota, 2)
            then(dve.tensor_copy(steps[:, :], steps_i[:, :]))
            then(dve.tensor_scalar(earlier[:, :], steps[:, 0:E], -1.0, float(E), ALU.mult, ALU.add))
            then(dve.tensor_tensor(lb[:, :, :], logits[:, :, :],
                                   beta_sb[:, :].unsqueeze(1).to_broadcast([P, NT, E]), ALU.add))
            for n in range(2):
                then(dve.tensor_reduce(best[:, :], lb[:, :, :], AX.X, ALU.max))
                then(dve.tensor_tensor(pick[:, :, :], lb[:, :, :], best[:, :].unsqueeze(2).to_broadcast(
                    [P, NT, E]), ALU.is_equal))
                then(dve.tensor_tensor(pick[:, :, :], pick[:, :, :],
                                       earlier[:, :].unsqueeze(1).to_broadcast([P, NT, E]), ALU.mult))
                then(dve.tensor_reduce(best[:, :], pick[:, :, :], AX.X, ALU.max))
                then(dve.tensor_tensor(top[:, n, :, :], pick[:, :, :], best[:, :].unsqueeze(2).to_broadcast(
                    [P, NT, E]), ALU.is_equal))
                if n == 0:
                    then(dve.scalar_tensor_tensor(out=lb[:, :, :], in0=top[:, 0, :, :], scalar=-3e38,
                                                  in1=lb[:, :, :], op0=ALU.mult, op1=ALU.add))
            flat = lambda v: v.rearrange("p t e -> p (t e)")
            dve.tensor_tensor(member[:, :], flat(top[:, 0, :, :]), flat(top[:, 1, :, :]), ALU.add).then_inc(r_member, 1)
            for n in range(2):
                then(dve.tensor_tensor(pick[:, :, :], top[:, n, :, :], logits[:, :, :], ALU.mult))
                then(dve.tensor_reduce(chosen[:, :, n], pick[:, :, :], AX.X, ALU.add))
            dve.sem_inc(r_chosen, 1)
            dve.wait_ge(r_pre, 1)
            then(dve.tensor_copy(totals[:, :, :], psum[:, 1, :].rearrange("p (t e) -> p e t", e=E)))
            then(dve.tensor_tensor_scan(upto[:, :, :].rearrange("p e t -> p (e t)"),
                                        totals[:, :, :].rearrange("p e t -> p (e t)"),
                                        zero_row[:, :], 0.0, ALU.add, ALU.add))
            then(dve.tensor_tensor(totals[:, :, :], upto[:, :, :], totals[:, :, :], ALU.subtract))
            then(dve.tensor_tensor(nblk[:, :], upto[:, :, NT - 1], totals[:, :, 0], ALU.subtract))
            then(dve.tensor_scalar(own_f[:, 0:LANES], steps[:, 0:LANES], float(BLK), None, ALU.mult))
            then(dve.tensor_tensor(used[:, :, :], nblk[:, :].unsqueeze(2).to_broadcast([P, E, LANES]),
                                   own_f[:, 0:LANES].unsqueeze(1).to_broadcast([P, E, LANES]), ALU.is_gt))
            then(dve.tensor_reduce(nblk[:, :], used[:, :, :], AX.X, ALU.add))
            then(dve.tensor_tensor_scan(first[:, :], nblk[:, :], zero_row[:, 0:E], 0.0, ALU.add, ALU.add))
            then(dve.tensor_tensor(first[:, :], first[:, :], nblk[:, :], ALU.subtract))
            then(dve.tensor_tensor(own_f[:, 0:E], first[:, :], nblk[:, :], ALU.add))
            then(dve.tensor_scalar(final[:, :], own_f[:, 0:E], -1.0, 0.0, ALU.add, ALU.max))
            dve.sem_inc(r_final, 1)
            then(dve.scalar_tensor_tensor(out=base[:, :], in0=first[:, :], scalar=float(BLK),
                                          in1=totals[:, :, 0], op0=ALU.mult, op1=ALU.subtract))
            then(dve.tensor_tensor(position[:, :, :].rearrange("p t e -> p e t"), totals[:, :, :],
                                   base[:, :].unsqueeze(2).to_broadcast([P, E, NT]), ALU.add))
            then(dve.tensor_tensor(flat(position[:, :, :]), psum[:, 0, :], flat(position[:, :, :]), ALU.add))
            for n in range(2):
                then(dve.tensor_tensor(pick[:, :, :], top[:, n, :, :], position[:, :, :], ALU.mult))
                then(dve.tensor_reduce(slot_f[:, :, n], pick[:, :, :], AX.X, ALU.add))
            then(dve.tensor_copy(slot[:, :, :], slot_f[:, :, :]))
            then(dve.tensor_tensor(own_cmp[:, :, :], steps[:, 0:NBLK].unsqueeze(2).to_broadcast([P, NBLK, E]),
                                   first[:, :].unsqueeze(1).to_broadcast([P, NBLK, E]), ALU.is_ge))
            then(dve.tensor_reduce(own_f[:, :], own_cmp[:, :, :], AX.X, ALU.add))
            then(dve.tensor_scalar(owner[:, :], own_f[:, :], -1.0, None, ALU.add))


        split_take = layout(split_arena, SPLIT_WORDS)
        split_take(2, G, D)
        split_take(2, 3, KD, D)
        split_take(BLK * D // P)
        q_xt = split_take(2, 2, KD, S)
        q_qk = split_take(2, 2, 2, KD, S)
        q_v = split_take(2, T, H, 2, DH)
        plain_take = layout(plain_arena, PLAIN_WORDS)
        q_x = plain_take(ROW_SLOTS, T, D)
        q_vf = plain_take(T, D)
        q_pair = plain_take(2, D)
        q_vs = plain_take(H, 2, DH)
        q_idx = sb("q_idx", [P, ROW_SLOTS, T, 2], U32)
        q_ld = [sem(f"q_rows_loaded{u}") for u in range(ROW_SLOTS)]
        q_tr = sem("q_transposed")
        q_xhi = sem("q_xt_hi")
        q_xlo = sem("q_xt_lo")
        q_mm = sem("q_projected")
        q_hi = sem("q_proj_hi")
        q_lo = sem("q_proj_lo")
        q_vb = sem("q_v_biased")
        q_vhi = sem("q_v_hi")
        q_vlo = sem("q_v_lo")
        q_pairs = sem("q_v_pairs_summed")
        q_vsum = sem("q_v_summed")
        q_vt = sem("q_v_total")
        q_vtc = sem("q_v_total_copied")
        q_st = [sem(f"q_qk_stored{u}") for u in range(2)]
        q_vst = [sem(f"q_v_stored{u}") for u in range(2)]
        q_ix = sem("q_index_staged")
        q_free = sem("q_index_slot_free")
        q_sc = [sem(f"q_scattered{u}") for u in range(ROW_SLOTS)]

        def over_batches(eng, body):
            over_rows(eng, lambda b, u, n, more: body(b, u % 2, 2 * n + u // 2, more))

        def q_sync(sp):
            def rows(b, u):
                sp.dma_start(q_x[:, u, :, :],
                             xn_d[ds(b * S, S), :].rearrange("(a p) d -> p a d", p=P)).then_inc(q_ld[u], 16)

            def body(b, u):
                sp.wait_ge(q_lo, 4 * b + 4)
                for k, dram in enumerate((q_d, k_d)):
                    for part in range(2):
                        sp.dma_start(dram[ds(b, 1), part, :, :].rearrange("o (m p) s -> p (o m) s", p=P),
                                     q_qk[:, u, k, part, :, :].bitcast(F32)).then_inc(q_st[u], 16)
                sp.wait_ge(q_vlo, 2 * b + 2)
                sp.dma_start(v_d[ds(b, 1), :, :, :].rearrange("o p a c -> p (o a) c"),
                             q_v[:, u, :, :, :, :].rearrange("p a h s d -> p a (h s d)").bitcast(F32)
                             ).then_inc(q_vst[u], 16)
            for u in range(ROW_SLOTS):
                rows(u, u)
            for u in range(2):
                sp.sem_inc(q_st[u], 64)
                sp.sem_inc(q_vst[u], 16)
            sp.sem_inc(q_free, ROW_SLOTS)

            def step(b, u, n, more):
                body(b, u % 2)
                if not isinstance(b, int):
                    v, k = (u - 1) % ROW_SLOTS, (n if u > 0 else n - 1)
                    sp.wait_ge(q_tr, b)
                    sp.wait_ge(q_sc[v], 16 * 2 * T * k + 16 * 2 * T)
                    sp.sem_inc(q_free, 1)
                    rows(b + ROW_SLOTS - 1, v)
            over_rows(sp, step)
            for u in range(2):
                sp.wait_ge(q_st[u], 64 * (B // 2) + 64)
                sp.wait_ge(q_vst[u], 16 * (B // 2) + 16)

        def q_gpsimd(pool):
            pool.wait_ge(s_zero, N_ZERO + 16 * E)
            with pool.Fori(0, B // ROW_SLOTS) as i:
                for u in range(ROW_SLOTS):
                    pool.wait_ge(q_ld[u], 16 * i + 16)
                    hold(pool, q_ix, ROW_SLOTS * i + u + 1)
                    for a in range(T):
                        for n in range(2):
                            pool.indirect_dma_start(
                                sorted_d, bass.IndirectOffsetOnAxis(q_idx[:, u, a, n:n + 1], 0),
                                q_x[:, u, a, :], None).then_inc(q_sc[u], 16)
            for u in range(ROW_SLOTS):
                pool.wait_ge(q_sc[u], 16 * 2 * T * (B // ROW_SLOTS))

        def q_tensor(pe):
            def turn_rows(b, u, n):
                pe.wait_ge(q_ld[u], 16 * n + 16)
                after(pe, q_xlo, b)
                after(pe, q_vtc, b - 1)
                for c in range(KD):
                    for a in range(T):
                        last = pe.transpose(psum[:, c, a * P:(a + 1) * P],
                                            q_x[:, u, a, c * P:(c + 1) * P], ident[:, :])
                last.then_inc(q_tr, 1)

            def total(b, known_parts):
                pe.wait_ge(q_vsum, b + 1)
                pe.wait_ge(q_xlo, known_parts)
                for g in range(G):
                    last = pe.matmul(psum[:, 0, g:g + 1],
                                     q_vs[:, g * HG:(g + 1) * HG, :, :].rearrange("p h s d -> p (h s d)"),
                                     half_tiny[:, :], start=True, stop=True)
                last.then_inc(q_vt, 1)

            def body(b, row_slot, count, more):
                u = row_slot % 2
                pe.wait_ge(q_xlo, b + 1)
                for k in range(2):
                    for m in range(KD):
                        bank = 2 + 2 * k + m
                        after(pe, q_lo, 4 * b + 2 * k + m - 3)
                        split_products(pe, psum[:, bank, :], [
                            (lambda part, c=c: wqkv[:, part, k, c, m * P:(m + 1) * P],
                             lambda part, c=c: q_xt[:, u, part, c, :]) for c in range(KD)]
                        ).then_inc(q_mm, 1)
                    if k == 0 and not is_first(b):
                        total(b - 1, b + 1)
                if more:
                    turn_rows(b + 1, (row_slot + 1) % ROW_SLOTS, count + (row_slot + 1) // ROW_SLOTS)
                for h in range(2):
                    after(pe, q_vb, 2 * b + h - 1)
                    for a in (2 * h, 2 * h + 1):
                        last = split_products(pe, psum[:, 6 + h, (a % 2) * D:(a % 2 + 1) * D], [
                            (lambda part, c=c: q_xt[:, u, part, c, a * P:(a + 1) * P],
                             lambda part, c=c: wqkv[:, part, 2, c, :]) for c in range(KD)])
                    last.then_inc(q_mm, 1)
            turn_rows(0, 0, 0)
            over_rows(pe, body)
            total(B - 1, B)

        def q_scalar(act):
            def rows_hi(b, u):
                act.wait_ge(q_tr, b + 1)
                for c in range(KD):
                    act.copy(q_xt[:, u, 0, c, :], psum[:, c, :]).then_inc(q_xhi, 1)

            def body(b, u, n, more):
                act.wait_ge(q_st[u], 64 * n + 64)
                for k in range(2):
                    for m in range(KD):
                        act.wait_ge(q_mm, 6 * b + 2 * k + m + 1)
                        act.activation(q_qk[:, u, k, 0, m, :], psum[:, 2 + 2 * k + m, :], ACT.Identity,
                                       bias=bqk[:, k, m:m + 1]).then_inc(q_hi, 1)
                if more:
                    rows_hi(b + 1, 1 - u)
                act.wait_ge(q_vst[u], 16 * n + 16)
                for h in range(2):
                    act.wait_ge(q_vb, 2 * b + h + 1)
                    act.copy(q_v[:, u, 2 * h:2 * h + 2, :, 0, :],
                             q_vf[:, 2 * h:2 * h + 2, :].rearrange("p a (h d) -> p a h d", h=H)
                             ).then_inc(q_vhi, 1)
            rows_hi(0, 0)
            over_batches(act, body)

        def q_vector(dve):
            def rows_lo(b, u):
                for c in range(KD):
                    dve.wait_ge(q_xhi, 2 * b + c + 1)
                    last = dve.tensor_tensor(q_xt[:, u, 1, c, :], psum[:, c, :],
                                             q_xt[:, u, 0, c, :].bitcast(F32), ALU.subtract)
                last.then_inc(q_xlo, 1)

            def total_out(b):
                dve.wait_ge(q_vt, b + 1)
                dve.tensor_copy(vtot[:, ds(b, 1), :].rearrange("p o g -> p (o g)"),
                                psum[:, 0, 0:G]).then_inc(q_vtc, 1)

            def body(b, row_slot, count, more):
                u = row_slot % 2
                dve.wait_ge(q_free, b + 1)
                dve.tensor_copy(q_idx[:, row_slot, :, :], slot[:, ds(b * T, T), :]).then_inc(q_ix, 1)
                for k in range(2):
                    for m in range(KD):
                        dve.wait_ge(q_hi, 4 * b + 2 * k + m + 1)
                        dve.scalar_tensor_tensor(out=q_qk[:, u, k, 1, m, :], in0=psum[:, 2 + 2 * k + m, :],
                                                 scalar=bqk[:, k, m:m + 1],
                                                 in1=q_qk[:, u, k, 0, m, :].bitcast(F32),
                                                 op0=ALU.add, op1=ALU.subtract).then_inc(q_lo, 1)
                    if k == 0 and not is_first(b):
                        total_out(b - 1)
                if more:
                    rows_lo(b + 1, 1 - u)
                for h in range(2):
                    dve.wait_ge(q_mm, 6 * b + 4 + h + 1)
                    after(dve, q_vlo, 2 * b + h - 1)
                    if h == 0:
                        after(dve, q_pairs, b)
                    dve.tensor_tensor(q_vf[:, 2 * h:2 * h + 2, :],
                                      psum[:, 6 + h, :].rearrange("p (a d) -> p a d", a=2),
                                      bv_sb[:, :].unsqueeze(1).to_broadcast([P, 2, D]),
                                      ALU.add).then_inc(q_vb, 1)
                for h in range(2):
                    dve.wait_ge(q_vhi, 2 * b + h + 1)
                    dve.tensor_tensor(q_v[:, u, 2 * h:2 * h + 2, :, 1, :],
                                      q_vf[:, 2 * h:2 * h + 2, :].rearrange("p a (h d) -> p a h d", h=H),
                                      q_v[:, u, 2 * h:2 * h + 2, :, 0, :].bitcast(F32),
                                      ALU.subtract).then_inc(q_vlo, 1)
                after(dve, q_vsum, b)
                dve.tensor_tensor(q_pair[:, :, :], q_vf[:, 0:2, :], q_vf[:, 2:4, :], ALU.add).then_inc(q_pairs, 1)
                dve.wait_ge(q_pairs, b + 1)
                after(dve, q_vt, b)
                halves = [q_pair[:, k, :].rearrange("p (h d) -> p h d", h=H).unsqueeze(2).to_broadcast(
                    [P, H, 2, DH]) for k in range(2)]
                dve.tensor_tensor(q_vs[:, :, :, :], halves[0], halves[1], ALU.add).then_inc(q_vsum, 1)
            rows_lo(0, 0)
            over_rows(dve, body)
            total_out(B - 1)

        split_take = layout(split_arena, SPLIT_WORDS)
        split_take(2, G, D)
        c_w = split_take(2, 2, 3, 1024)
        c_xt = split_take(2, 2, KD, S)
        c_h = split_take(2, 2, MC, S)
        plain_take = layout(plain_arena, PLAIN_WORDS)
        c_x = plain_take(T, D)
        c_sg = plain_take(2, S)
        c_y = plain_take(2, T, D)
        c_hf = plain_take(2, S)
        plain_take(T, D)
        c_raw = plain_take(3, 1024)
        assert NBLK % 2 == 1
        b_raw = plain_take(3, 1024)
        b_w = c_w[:, 1, :, :, :]
        b_k = split_take(2, 2, 2, S)
        b_q = split_take(2, 2, S)
        b_ldw = sem("b_shared_loaded")
        b_whi = sem("b_shared_hi")
        b_wlo = sem("b_shared_lo")
        b_kz = sem("b_k_zeroed")
        c_ldw = [sem(f"c_raw_loaded{n}") for n in range(3)]
        c_ldx = sem("c_rows_loaded")
        c_tr = sem("c_transposed")
        c_xhi = sem("c_xt_hi")
        c_xlo = sem("c_xt_lo")
        c_whi = sem("c_w_hi")
        c_wlo = sem("c_w_lo")
        c_gu = sem("c_gate_up")
        c_silu = sem("c_silu")
        c_mul = sem("c_hidden")
        c_hhi = sem("c_hidden_hi")
        c_hlo = sem("c_hidden_lo")
        c_dn = sem("c_down")
        c_yc = sem("c_y_copied")
        c_st = [sem(f"c_y_stored{u}") for u in range(2)]

        def gate_up(pe, m, banks, w, xt):
            for n in range(2):
                last = split_products(pe, psum[:, banks[n], :], [
                    (lambda part, c=c: w(part, n, c * M + m * P, P), lambda part, c=c: xt(part, c))
                    for c in range(KD)])
            return last

        def down(pe, m, h, w, first):
            for a in range(T):
                for k, (p, q) in enumerate(PASSES):
                    last = pe.matmul(psum[:, 6 + a // 2, (a % 2) * D:(a % 2 + 1) * D],
                                     h(p, m, a), w(q, 2, m * D, D),
                                     start=(first and k == 0 and a % 2 == 0), stop=(m == MC - 1 and k == 2),
                                     skip_group_check=True)
            return last

        def over_blocks(eng, body):
            with eng.Fori(0, (NBLK - 1) // 2) as i:
                for u in range(2):
                    body(2 * i + u, u, i, True)
            if NBLK % 2 == 0:
                body(NBLK - 2, 0, NBLK // 2 - 1, True)
            body(NBLK - 1, (NBLK - 1) % 2, (NBLK - 1) // 2, False)

        def c_sync(sp):
            def rows(blk):
                sp.dma_start(c_x[:, :, :], sorted_d[ds(blk * BLK, BLK), :].rearrange("(a p) d -> p a d", p=P)
                             ).then_inc(c_ldx, 16)

            def weights(e, k):
                for n, w in enumerate((gate_w, up_w, down_w)):
                    if k is not None:
                        sp.wait_ge(c_wlo, k + n)
                    rowsz = w.shape[2]
                    sp.dma_start(c_raw[:, n, :].rearrange("p (k n) -> p k n", n=rowsz),
                                 w[ds(e, 1), :, :].rearrange("o (k p) n -> p (o k) n", p=P)).then_inc(c_ldw[n], 16)
            e0 = sp.value_load(owner[0:1, 0:1], min_val=0, max_val=E - 1)
            weights(e0, None)
            wall(sp, 3)
            rows(0)
            for n, w in enumerate((sh_gate, sh_up, sh_down)):
                sp.dma_start(b_raw[:, n, :].rearrange("p (k n) -> p k n", n=w.shape[2]),
                             w.rearrange("o (k p) n -> p (o k) n", p=P)).then_inc(b_ldw, 16)

            def body(blk, u, n, more):
                if not more:
                    return
                sp.wait_ge(c_tr, blk + 1)
                rows(blk + 1)
                e = sp.value_load(owner[0:1, ds(blk + 1, 1)], min_val=0, max_val=E - 1)
                weights(e, 3 * blk + 4)
            over_blocks(sp, body)

        def c_tensor(pe):
            def turn():
                for c in range(KD):
                    for a in range(T):
                        last = pe.transpose(psum[:, 4 + c, a * P:(a + 1) * P],
                                            c_x[:, a, c * P:(c + 1) * P], ident[:, :])
                last.then_inc(c_tr, 1)
            pe.wait_ge(c_ldx, 16)
            turn()

            def body(blk, u, n, more):
                w = lambda part, n, at, cols: c_w[:, u, part, n, at:at + cols]
                pe.wait_ge(c_xlo, blk + 1)
                pe.wait_ge(c_wlo, 3 * blk + 6)
                for m in range(MC):
                    pe.wait_ge(c_mul, 4 * blk + m + 1)
                    gate_up(pe, m, (2 * (m % 2), 2 * (m % 2) + 1), w,
                            lambda part, c: c_xt[:, u, part, c, :]).then_inc(c_gu, 1)
                if more:
                    pe.wait_ge(c_ldx, 16 * blk + 32)
                    turn()
                pe.wait_ge(c_yc, 2 * blk + 2)
                for m in range(MC):
                    pe.wait_ge(c_hlo, 4 * blk + m + 3)
                    last = down(pe, m, lambda part, m, a: c_h[:, u, part, m, a * P:(a + 1) * P], w, m == 0)
                last.then_inc(c_dn, 1)
            over_blocks(pe, body)

        def c_scalar(act):
            def w_hi(v, n, k):
                act.wait_ge(c_ldw[n], k)
                act.copy(c_w[:, v, 0, n, :], c_raw[:, n, :]).then_inc(c_whi, 1)

            def x_hi(v, k):
                act.wait_ge(c_tr, k)
                for c in range(KD):
                    act.copy(c_xt[:, v, 0, c, :], psum[:, 4 + c, :]).then_inc(c_xhi, 1)
            act.sem_inc(c_dn, 1)
            act.sem_inc(c_st[0], 16)
            act.sem_inc(c_st[1], 16)
            for n in range(3):
                w_hi(0, n, 16)
            x_hi(0, 1)

            def body(blk, u, n, more):
                def hid_hi(m):
                    act.wait_ge(c_mul, 4 * blk + m + 3)
                    act.copy(c_h[:, u, 0, m, :], c_hf[:, m % 2, :]).then_inc(c_hhi, 1)
                for m in range(MC):
                    act.wait_ge(c_gu, 4 * blk + m + 1)
                    act.activation(c_sg[:, m % 2, :], psum[:, 2 * (m % 2), :], ACT.Silu).then_inc(c_silu, 1)
                    if m == 0:
                        act.wait_ge(c_dn, blk + 1)
                    if m >= 1:
                        hid_hi(m - 1)
                    if more and m < 3:
                        w_hi(1 - u, m, 16 * blk + 32)
                hid_hi(MC - 1)
                if more:
                    x_hi(1 - u, blk + 2)
                else:
                    act.wait_ge(b_ldw, 48)
                    for k in range(3):
                        act.activation(b_w[:, 0, k, :], b_raw[:, k, :], ACT.Copy,
                                       scale=(0.5 if k == 2 else 1.0)).then_inc(b_whi, 1)
                act.wait_ge(c_yc, 2 * blk + 4)
                act.dma_start(y_d[ds(blk * BLK, BLK), :].rearrange("(a p) d -> p a d", p=P),
                              c_y[:, u, :, :]).then_inc(c_st[u], 16)
            over_blocks(act, body)
            for u in range(2):
                act.wait_ge(c_st[u], 16 * ((NBLK + 1 - u) // 2) + 16)

        def c_vector(dve):
            def w_lo(v, n, k):
                dve.wait_ge(c_whi, k)
                dve.tensor_tensor(c_w[:, v, 1, n, :], c_raw[:, n, :], c_w[:, v, 0, n, :].bitcast(F32),
                                  ALU.subtract).then_inc(c_wlo, 1)

            def x_lo(v, k):
                for c in range(KD):
                    dve.wait_ge(c_xhi, k + c)
                    last = dve.tensor_tensor(c_xt[:, v, 1, c, :], psum[:, 4 + c, :],
                                             c_xt[:, v, 0, c, :].bitcast(F32), ALU.subtract)
                last.then_inc(c_xlo, 1)
            dve.sem_inc(c_wlo, 3)
            dve.sem_inc(c_mul, 2)
            dve.sem_inc(c_hlo, 2)
            dve.sem_inc(c_yc, 2)
            for n in range(3):
                w_lo(0, n, n + 1)
            x_lo(0, 1)

            def body(blk, u, n, more):
                def hid_lo(m):
                    dve.wait_ge(c_hhi, 4 * blk + m + 1)
                    dve.tensor_tensor(c_h[:, u, 1, m, :], c_hf[:, m % 2, :],
                                      c_h[:, u, 0, m, :].bitcast(F32), ALU.subtract).then_inc(c_hlo, 1)
                for m in range(MC):
                    dve.wait_ge(c_silu, 4 * blk + m + 1)
                    dve.wait_ge(c_hlo, 4 * blk + m + 1)
                    dve.tensor_tensor(c_hf[:, m % 2, :], psum[:, 2 * (m % 2) + 1, :], c_sg[:, m % 2, :],
                                      ALU.mult).then_inc(c_mul, 1)
                    if m >= 1:
                        hid_lo(m - 1)
                    if more and m < 3:
                        w_lo(1 - u, m, 3 * blk + m + 4)
                hid_lo(MC - 1)
                if more:
                    x_lo(1 - u, 2 * blk + 3)
                else:
                    for k in range(3):
                        dve.wait_ge(b_whi, k + 1)
                        dve.scalar_tensor_tensor(out=b_w[:, 1, k, :], in0=b_raw[:, k, :],
                                                 scalar=(0.5 if k == 2 else 1.0),
                                                 in1=b_w[:, 0, k, :].bitcast(F32),
                                                 op0=ALU.mult, op1=ALU.subtract).then_inc(b_wlo, 1)
                dve.wait_ge(c_dn, blk + 2)
                dve.wait_ge(c_st[u], 16 * n + 16)
                for h in range(2):
                    dve.tensor_copy(c_y[:, u, 2 * h:2 * h + 2, :].rearrange("p a d -> p (a d)"),
                                    psum[:, 6 + h, :]).then_inc(c_yc, 1)
            over_blocks(dve, body)

        split_take = layout(split_arena, SPLIT_WORDS)
        split_take(2, G, D)
        b_xt = split_take(2, KD, S)
        b_h = split_take(2, MC, S)
        split_take(2 * 3 * 1024)
        b_v = split_take(2, T, HG, P)
        b_pt = split_take(2, 2, 8, P)
        b_cx = split_take(2, G, S)
        plain_take = layout(plain_arena, PLAIN_WORDS)
        b_x = plain_take(T, D)
        b_o = plain_take(T, D)
        b_y = plain_take(2, T, D)
        b_p = plain_take(4, T, 2 * P)
        b_sg = plain_take(2, S // 2)
        b_gg = plain_take(2, S // 2)
        b_hf = plain_take(2, S)
        b_nm = sb("b_nm", [P, 4, T], F32)
        b_zs = sb("b_zs", [P, 4, T], F32)
        b_rz = sb("b_rz", [P, 4, T], F32)
        b_vt = sb("b_vt", [P, G], F32)
        b_cf = sb("b_cf", [P, T, 2], F32)
        b_ix = sb("b_ix", [P, T, 2], U32)
        b_zeroed = sem("b_zeroed")
        b_ldx = sem("b_rows_loaded")
        b_ldo = sem("b_x_loaded")
        b_ldqk = [sem(f"b_qk_loaded{s}") for s in range(2)]
        b_ldv = [sem(f"b_v_loaded{s}") for s in range(2)]
        b_tr = sem("b_rows_transposed")
        b_xhi = sem("b_xt_hi")
        b_xlo = sem("b_xt_lo")
        b_gu = sem("b_gate_up")
        b_silu = sem("b_silu")
        b_gt = sem("b_gate_factor")
        b_mul = sem("b_hidden")
        b_hhi = sem("b_hidden_hi")
        b_hlo = sem("b_hidden_lo")
        b_s = sem("b_scores")
        b_mx = sem("b_masked_max")
        b_ex = sem("b_exp")
        b_rc = sem("b_reciprocal")
        b_nr = sem("b_normalised")
        b_pT = sem("b_probs_transposed")
        b_phi = sem("b_probs_hi")
        b_plo = sem("b_probs_lo")
        b_pv = sem("b_values_summed")
        b_chi = sem("b_context_hi")
        b_clo = sem("b_context_lo")
        b_cxr = sem("b_context_read")
        b_yy = sem("b_rows_projected")
        b_stg = sem("b_staged")
        b_ga = sem("b_gathered")
        b_xb = sem("b_x_biased")
        b_f = sem("b_routed_added")
        b_fin = sem("b_result_half_ready")
        b_st = sem("b_result_stored")
        BLOCKS = [(0, 0), (1, 0), (1, 1), (2, 1), (2, 2), (3, 2), (3, 3)]

        def turns(eng, turn):
            turn(0, True, False)
            with eng.Fori(1, B) as b:
                turn(b, True, True)
            turn(B, False, True)

        def lagging(h, lag, new, old):
            n = h - lag
            return n if (new if n >= 0 else old) else None

        PROJECTIONS = [(0, 0), (1, 0), (0, 1), (1, 1), (2, 0), (3, 0), (2, 1), (3, 1)]

        def halves_of(h, new, old):
            if h >= 14:
                return (h - 14,) if new else ()
            if h < 5 and old:
                return (6, 7) if h == 4 else (h + 2,)
            return ()

        def b_sync(sp):
            def load_qk(b, g):
                s = g % 2
                after(sp, b_s, 32 * b + 8 * g - 8)
                for c in range(4):
                    sp.dma_start(b_q[32 * c:32 * c + 32, s, :, :].bitcast(F32),
                                 q_d[ds(b, 1), c // 2, g * 64:(g + 1) * 64, :].rearrange(
                                     "o (h w) s -> w (o h) s", h=2)).then_inc(b_ldqk[s], 16)
                    for w in range(2):
                        sp.dma_start(b_k[32 * c + 16 * w:32 * c + 16 * w + 16, s, :, w, :].bitcast(F32),
                                     k_d[ds(b, 1), c % 2, g * 64:(g + 1) * 64, :].rearrange(
                                         "o (h w d) s -> w d (o h) s", h=2, w=2)[w]).then_inc(b_ldqk[s], 16)

            def load_v(b, g):
                s = g % 2
                if isinstance(b, int) and g == 0:
                    sp.wait_ge(b_zeroed, 1)
                after(sp, b_pv, 16 * b + 4 * g - 4)
                for c in range(4):
                    sp.dma_start(b_v[:, s, :, c, 32 * c:32 * c + 32].bitcast(F32),
                                 v_d[ds(b, 1), :, :, g * P + 32 * c:g * P + 32 * c + 32].rearrange(
                                     "o p a c -> p (o a) c")).then_inc(b_ldv[s], 16)

            def load_result(b):
                after(sp, b_st, 16 * b)
                sp.dma_start(b_o[:, :, :], xf[ds(b * S, S), :].rearrange("(a p) d -> p a d", p=P)
                             ).then_inc(b_ldo, 16)

            def turn(b, new, old):
                if new:
                    after(sp, b_tr, b)
                    sp.dma_start(b_x[:, :, :], xn_d[ds(b * S, S), :].rearrange("(a p) d -> p a d", p=P)
                                 ).then_inc(b_ldx, 16)
                for g in range(G if new else 0):
                    if g > 1 or not is_first(b):
                        load_qk(b, g)
                    load_v(b, g)
                    if old and g == 0:
                        load_result(b - 1)
                if not new:
                    load_result(b - 1)
            sp.wait_ge(b_kz, 1)
            load_qk(0, 0)
            load_qk(0, 1)
            wall(sp, 4)
            turns(sp, turn)

        def b_gpsimd(pool):
            pool.memset(b_v.bitcast(F32), 0.0).then_inc(b_zeroed, 1)
            pool.memset(b_pt[:, :, :, 0, :].bitcast(F32), 0.0).then_inc(b_zeroed, 1)
            def hidden_lo(b, m):
                pool.wait_ge(b_hhi, 4 * b + m + 1)
                pool.tensor_tensor(b_h[:, 1, m, :], b_hf[:, m % 2, :], b_h[:, 0, m, :].bitcast(F32),
                                   ALU.subtract).then_inc(b_hlo, 1)

            def turn(b, new, old):
                for h in range(H):
                    n = lagging(h, 2, new, old)
                    if n is not None:
                        hold(pool, b_rc, 16 * b + n + 1)
                        for i in range(T):
                            v = b_p[:, n % 4, i, 0:(P if i == 0 else 2 * P)]
                            last = pool.tensor_scalar(v, v, b_rz[:, n % 4, i:i + 1], 0.0, ALU.mult, ALU.add)
                        last.then_inc(b_nr, 1)
                    if old and h in (1, 3, 5, 6):
                        hidden_lo(b - 1, h // 2)
                    if old and h in (4, 7):
                        if h == 4:
                            pool.wait_ge(b_ldo, 16 * b)
                        for a in (range(0, 2) if h == 4 else range(2, T)):
                            pool.tensor_tensor(b_o[:, a, :], b_o[:, a, :], bo_sb[:, :], ALU.add).then_inc(b_xb, 1)
                    k = h - 10 if new and h >= 10 else 6 + h // 2 if old and h in (0, 2) else None
                    if k is not None:
                        if k == 0:
                            hold(pool, b_stg, b + 1)
                        pool.indirect_dma_start(b_y[:, k % 2, k // 2, :], None, y_d,
                                                bass.IndirectOffsetOnAxis(b_ix[:, k // 2, k % 2:k % 2 + 1], 0)
                                                ).then_inc(b_ga, 16)
            turns(pool, turn)

        def b_tensor(pe):
            def scores(b, h):
                g, r = h // HG, h % HG
                if r == 0:
                    pe.wait_ge(b_ldqk[g % 2], 192 * (2 * b + g // 2) + 192)
                for i in range(T):
                    if i % 2 == 0:
                        after(pe, b_mx, 32 * b + 2 * h + i // 2 - 1)
                    last = pe.matmul(psum[:, i // 2, (i % 2) * 2 * P:(i % 2 + 1) * 2 * P],
                                     b_q[:, g % 2, r // 2, i * P:(i + 1) * P],
                                     b_k[:, g % 2, r // 2, r % 2, max(i - 1, 0) * P:(max(i - 1, 0) + 2) * P],
                                     start=True, stop=True)
                    if i % 2 == 1:
                        last.then_inc(b_s, 1)

            def turn_probs(b, n):
                pe.wait_ge(b_nr, 16 * b + n + 1)
                for k, (i, j) in enumerate(BLOCKS):
                    if k % 4 == 0:
                        after(pe, b_plo, 32 * b + 2 * n - 1 + k // 4)
                    half = j if i == 0 else j - i + 1
                    last = pe.transpose(psum[:, 2 + k // 4, (k % 4) * P:(k % 4 + 1) * P],
                                        b_p[:, n % 4, i, half * P:(half + 1) * P], ident[:, :])
                    if k in (3, 6):
                        last.then_inc(b_pT, 1)

            def values(b, n):
                g, r = n % H // HG, n % HG
                if r == 0:
                    pe.wait_ge(b_ldv[g % 2], 64 * (2 * (b if n >= 0 else b - 1) + g // 2) + 64)
                    after(pe, b_clo, 4 * b + n // HG - 1)
                pe.wait_ge(b_plo, 32 * b + 2 * n + 2)
                for j in range(T):
                    at = j if j < T - 1 else T - 2
                    for part in range(2):
                        blocks = (b_pt[:, n % 2, part, 2 * j + 1:2 * j + 3, :] if j < T - 1
                                  else b_pt[:, n % 2, part, 0:8:7, :])
                        last = pe.matmul(psum[:, 4 + g % 2, at * P:(at + 2) * P],
                                         b_v[:, g % 2, j, r, :], blocks,
                                         start=(r == 0 and j == 0 and part == 0),
                                         stop=(r == HG - 1 and j == T - 1 and part == 1),
                                         skip_group_check=True)
                last.then_inc(b_pv, 1)

            def turn_rows(b):
                pe.wait_ge(b_ldx, 16 * b + 16)
                after(pe, b_fin, 2 * b)
                for c in range(KD):
                    for a in range(T):
                        last = pe.transpose(psum[:, 6 + c, a * P:(a + 1) * P],
                                            b_x[:, a, c * P:(c + 1) * P], ident[:, :])
                last.then_inc(b_tr, 1)

            def gate_up_half(b, k):
                m, half = k // 2, (k % 2) * (S // 2)
                if k < 2:
                    pe.wait_ge(b_xlo, 2 * b + 2)
                else:
                    pe.wait_ge(b_mul, 8 * b + k - 1)
                for n in range(2):
                    last = split_products(pe, psum[:, 6 + k % 2, n * (S // 2):(n + 1) * (S // 2)], [
                        (lambda part, c=c: b_w[:, part, n, c * M + m * P:c * M + (m + 1) * P],
                         lambda part, c=c: b_xt[:, part, c, half:half + S // 2]) for c in range(KD)])
                last.then_inc(b_gu, 1)

            def project_rows(b, a, which):
                out = psum[:, 7 - a // 2, (a % 2) * D:(a % 2 + 1) * D]
                if which == 0:
                    if a == 0:
                        pe.wait_ge(b_clo, 4 * b + 4)
                        pe.wait_ge(b_mul, 8 * b + 8)
                    last = split_products(pe, out, [
                        (lambda part, g=g: b_cx[:, part, g, a * P:(a + 1) * P],
                         lambda part, g=g: wo[:, part, g, :]) for g in range(G)],
                        begins=(a % 2 == 0), ends=False)
                    if a == 3:
                        last.then_inc(b_cxr, 1)
                else:
                    if a == 0:
                        pe.wait_ge(b_hlo, 4 * b + 4)
                    split_products(pe, out, [
                        (lambda part, m=m: b_h[:, part, m, a * P:(a + 1) * P],
                         lambda part, m=m: b_w[:, part, 2, m * D:(m + 1) * D]) for m in range(MC)],
                        begins=False, ends=True).then_inc(b_yy, 1)

            def turn(b, new, old):
                for h in range(H):
                    n = lagging(h, 3, new, old)
                    if n is not None:
                        turn_probs(b, n)
                    if new:
                        scores(b, h)
                    n = lagging(h, 4, new, old)
                    if n is not None:
                        values(b, n)
                    for k in halves_of(h, new, old):
                        gate_up_half(b if h >= 14 else b - 1, k)
                    if old and 5 <= h < 13:
                        project_rows(b - 1, *PROJECTIONS[h - 5])
                    if new and h == 13:
                        turn_rows(b)
            pe.wait_ge(b_zeroed, 2)
            turns(pe, turn)

        def b_scalar(act):
            def exponentials(b, n, tiles):
                act.wait_ge(b_mx, 32 * b + 2 * n + 1 + tiles[0] // 2)
                for i in tiles:
                    v = b_p[:, n % 4, i, 0:(P if i == 0 else 2 * P)]
                    last = act.activation(v, v, ACT.Exp, bias=b_nm[:, n % 4, i:i + 1], scale=-1.0,
                                          accum_out=b_zs[:, n % 4, i:i + 1])
                if tiles[-1] == T - 1:
                    last.then_inc(b_ex, 1)

            def probs_hi(b, n, part):
                act.wait_ge(b_pT, 32 * b + 2 * n + 1 + part)
                after(act, b_pv, 16 * b + n - 1)
                blocks = slice(1, 5) if part == 0 else slice(5, 8)
                cols = 4 * P if part == 0 else 3 * P
                act.copy(b_pt[:, n % 2, 0, blocks, :].rearrange("p a b -> p (a b)"),
                         psum[:, 2 + part, 0:cols]).then_inc(b_phi, 1)

            def silu(b, k):
                act.wait_ge(b_gu, 8 * b + k + 1)
                after(act, b_mul, 8 * b + k - 1)
                act.activation(b_sg[:, k % 2, :], psum[:, 6 + k % 2, 0:S // 2], ACT.Tanh, scale=0.5
                               ).then_inc(b_silu, 1)

            def hidden_hi(b, m):
                act.wait_ge(b_mul, 8 * b + 2 * m + 2)
                act.copy(b_h[:, 0, m, :], b_hf[:, m % 2, :]).then_inc(b_hhi, 1)

            def context_hi(b, g):
                act.wait_ge(b_pv, 16 * b + 4 * g + 4)
                if g == 0:
                    act.wait_ge(b_stg, b + 1)
                    after(act, b_cxr, b)
                act.activation(b_cx[:, 0, g, :], psum[:, 4 + g % 2, :], ACT.Identity,
                               bias=b_vt[:, g:g + 1]).then_inc(b_chi, 1)

            def turn(b, new, old):
                for h in range(H):
                    e, p = lagging(h, 1, new, old), lagging(h, 3, new, old)
                    for part in range(2):
                        if p is not None:
                            probs_hi(b, p, part)
                    for part in range(2):
                        if e is not None:
                            exponentials(b, e, (2 * part, 2 * part + 1))
                    if old and h in (0, 2, 4, 5):
                        hidden_hi(b - 1, (h + 1) // 2)
                    for k in halves_of(h, new, old):
                        silu(b if h >= 14 else b - 1, k)
                    if old and h in (0, 4):
                        context_hi(b - 1, 2 + h // 4)
                    if new and h in (11, 13):
                        context_hi(b, (h - 11) // 2)
                    if new and h == 13:
                        act.wait_ge(b_tr, b + 1)
                        for c in range(KD):
                            act.copy(b_xt[:, 0, c, :], psum[:, 6 + c, :]).then_inc(b_xhi, 1)
                    if old and h == 14:
                        act.wait_ge(b_fin, 2 * b)
                        act.dma_start(of[ds((b - 1) * S, S), :].rearrange("(a p) d -> p a d", p=P),
                                      b_o[:, :, :]).then_inc(b_st, 16)
            turns(act, turn)
            act.wait_ge(b_st, 16 * B)

        def b_vector(dve):
            def masked_max(b, h, part):
                hold(dve, b_s, 32 * b + 2 * h + 1 + part)
                for i in (2 * part, 2 * part + 1):
                    cols = P if i == 0 else 2 * P
                    at = (i % 2) * 2 * P
                    last = dve.tensor_tensor_reduce(
                        b_p[:, h % 4, i, 0:cols], psum[:, i // 2, at:at + cols],
                        mask[:, 2 * P - cols:2 * P], -SCALE, 3e38, ALU.add, ALU.min,
                        b_nm[:, h % 4, i:i + 1])
                last.then_inc(b_mx, 1)

            def probs_lo(b, n, part):
                dve.wait_ge(b_phi, 32 * b + 2 * n + 1 + part)
                blocks = slice(1, 5) if part == 0 else slice(5, 8)
                cols = 4 * P if part == 0 else 3 * P
                dve.tensor_tensor(b_pt[:, n % 2, 1, blocks, :].rearrange("p a b -> p (a b)"),
                                  psum[:, 2 + part, 0:cols],
                                  b_pt[:, n % 2, 0, blocks, :].rearrange("p a b -> p (a b)").bitcast(F32),
                                  ALU.subtract).then_inc(b_plo, 1)

            def hidden(b, k):
                m, half = k // 2, (k % 2) * (S // 2)
                dve.wait_ge(b_silu, 8 * b + k + 1)
                after(dve, b_hlo, 4 * b + m - 1)
                dve.scalar_tensor_tensor(out=b_gg[:, k % 2, :], in0=b_sg[:, k % 2, :], scalar=1.0,
                                         in1=psum[:, 6 + k % 2, 0:S // 2],
                                         op0=ALU.add, op1=ALU.mult).then_inc(b_gt, 1)
                dve.wait_ge(b_gt, 8 * b + k + 1)
                dve.tensor_tensor(b_hf[:, m % 2, half:half + S // 2], psum[:, 6 + k % 2, S // 2:S],
                                  b_gg[:, k % 2, :], ALU.mult).then_inc(b_mul, 1)

            def context_lo(b, g):
                dve.wait_ge(b_chi, 4 * b + g + 1)
                dve.scalar_tensor_tensor(out=b_cx[:, 1, g, :], in0=psum[:, 4 + g % 2, :],
                                         scalar=b_vt[:, g:g + 1], in1=b_cx[:, 0, g, :].bitcast(F32),
                                         op0=ALU.add, op1=ALU.subtract).then_inc(b_clo, 1)

            def add_routed(b, n):
                dve.wait_ge(b_ga, 16 * 2 * T * b + 16 * 2 * T)
                if n == 0:
                    dve.wait_ge(b_xb, T * b + T)
                else:
                    dve.wait_ge(b_f, 2 * T * b + T)
                for a in range(T):
                    dve.scalar_tensor_tensor(out=b_o[:, a, :], in0=b_y[:, n, a, :],
                                             scalar=b_cf[:, a, n:n + 1], in1=b_o[:, a, :],
                                             op0=ALU.mult, op1=ALU.add).then_inc(b_f, 1)

            def finish(b, half):
                dve.wait_ge(b_yy, 4 * b + 2 * half + 2)
                dve.wait_ge(b_f, 2 * T * b + 2 * T)
                v = b_o[:, 2 * half:2 * half + 2, :].rearrange("p a d -> p (a d)")
                dve.tensor_tensor(v, psum[:, 7 - half, :], v, ALU.add).then_inc(b_fin, 1)

            def turn(b, new, old):
                for h in range(H):
                    p, r = lagging(h, 3, new, old), lagging(h, 1, new, old)
                    if old and h in (10, 13):
                        finish(b - 1, (h - 10) // 3)
                    for part in range(2):
                        if p is not None:
                            probs_lo(b, p, part)
                        if new:
                            masked_max(b, h, part)
                    if r is not None:
                        dve.wait_ge(b_ex, 16 * b + r + 1)
                        dve.reciprocal(b_rz[:, r % 4, :], b_zs[:, r % 4, :]).then_inc(b_rc, 1)
                    for k in halves_of(h, new, old):
                        hidden(b if h >= 14 else b - 1, k)
                    if old and h in (0, 4):
                        context_lo(b - 1, 2 + h // 4)
                    if old and h in (8, 9):
                        add_routed(b - 1, h - 8)
                    if new and h == 9:
                        after(dve, b_f, 2 * T * b)
                        dve.tensor_copy(b_ix[:, :, :], slot[:, ds(b * T, T), :])
                        dve.tensor_copy(b_cf[:, :, :], coef[:, ds(b * T, T), :])
                        dve.tensor_copy(b_vt[:, :], vtot[:, ds(b, 1), :].rearrange("p o g -> p (o g)")
                                        ).then_inc(b_stg, 1)
                    if new and h in (11, 13):
                        context_lo(b, (h - 11) // 2)
                    if new and h == 13:
                        for c in range(KD):
                            dve.wait_ge(b_xhi, 2 * b + c + 1)
                            dve.tensor_tensor(b_xt[:, 1, c, :], psum[:, 6 + c, :],
                                              b_xt[:, 0, c, :].bitcast(F32), ALU.subtract).then_inc(b_xlo, 1)
            turns(dve, turn)

        @block.sync
        def _(sp):
            start_sync(sp)
            a_sync(sp)
            wall(sp, 1)
            r_sync(sp)
            wall(sp, 2)
            q_sync(sp)
            c_sync(sp)
            b_sync(sp)

        @block.gpsimd
        def _(pool):
            start_gpsimd(pool)
            constants_gpsimd(pool)
            wall(pool, 1)
            r_gpsimd(pool)
            wall(pool, 2)
            q_gpsimd(pool)
            wall(pool, 3)
            pool.memset(b_k.bitcast(F32), 0.0).then_inc(b_kz, 1)
            wall(pool, 4)
            b_gpsimd(pool)

        @block.scalar
        def _(act):
            a_scalar(act)
            split_weights_scalar(act)
            wall(act, 1)
            r_scalar(act)
            wall(act, 2)
            q_scalar(act)
            wall(act, 3)
            c_scalar(act)
            wall(act, 4)
            b_scalar(act)

        @block.vector
        def _(dve):
            a_vector(dve)
            split_weights_vector(dve)
            wall(dve, 1)
            r_vector(dve)
            wall(dve, 2)
            q_vector(dve)
            wall(dve, 3)
            c_vector(dve)
            wall(dve, 4)
            b_vector(dve)

        @block.tensor
        def _(pe):
            a_tensor(pe)
            wall(pe, 1)
            r_tensor(pe)
            wall(pe, 2)
            q_tensor(pe)
            wall(pe, 3)
            c_tensor(pe)
            wall(pe, 4)
            b_tensor(pe)


def kernel(**inputs):
    import numpy as _np
    import concourse.bacc as _bacc
    from concourse.bass_utils import run_bass_kernel_spmd as _run

    pre = {n: _np.asarray(a) for n, a in inputs.items()}
    laid = {
        "x": pre["L0_attn_x"],
        "wq_t": pre["L0_attn_Wq"].T, "wk_t": pre["L0_attn_Wk"].T,
        "wv_t": pre["L0_attn_Wv"].T, "wo_t": pre["L0_attn_Wo"].T,
        "bq": pre["L0_attn_bq"], "bk": pre["L0_attn_bk"], "bv": pre["L0_attn_bv"], "bo": pre["L0_attn_bo"],
        "gate_t": pre["L0_ffn_gate_w"].T, "beta": pre["L0_ffn_beta"],
        "gate_w": pre["L0_ffn_gate_proj_w"], "up_w": pre["L0_ffn_up_proj_w"],
        "down_w": pre["L0_ffn_down_proj_w"],
        "sh_gate": pre["L0_ffn_shared_gate_w"], "sh_up": pre["L0_ffn_shared_up_w"],
        "sh_down": pre["L0_ffn_shared_down_w"],
    }
    nc = _bacc.Bacc("TRN2", target_bir_lowering=False, num_devices=1)
    arrays, args = {}, []
    for name, a in laid.items():
        a = _np.ascontiguousarray(a)
        arrays[f"in_{name}"] = a
        args.append(nc.dram_tensor(f"in_{name}", a.shape, mybir.dt.from_np(a.dtype), kind="ExternalInput").ap())
    args.append(nc.dram_tensor("out_0", pre["L0_attn_x"].shape, F32, kind="ExternalOutput").ap())
    moe_attention_layer(nc, *args)
    r = _run(nc, [arrays], core_ids=[0])
    return r.results[0]["out_0"]
```
